# Optimizing a Trainium2 kernel written in Bass

```python
import numpy as np
import jax
import jax.numpy as jnp

def _softmax(x, axis=-1):
    return jax.nn.softmax(x, axis=axis)

def _gelu(x):
    return jax.nn.gelu(x, approximate=True)

def _silu(x):
    return jax.nn.silu(x)

def _sigmoid(x):
    return jax.nn.sigmoid(x)

def _layernorm(x, axis=-1, eps=1e-05):
    m = jnp.mean(x, axis=axis, keepdims=True)
    v = jnp.var(x, axis=axis, keepdims=True)
    return (x - m) / jnp.sqrt(v + eps)

def _scatter_add(tgt, idx, src, axis=0):
    return tgt.at[idx].add(src)

def _segment_sum(src, seg, n):
    return jax.ops.segment_sum(src, seg, n)
kernel_name = 'mk_adj_resnorm_d4_adj_r2_0992ef'

def setup_inputs(seed: int=0):
    np.random.seed(seed)
    _w = jnp.asarray

    def _rec_inputs():
        import jax
        import jax.numpy as jnp
        _gk = jax.random.key(seed)
        x = -0.0005207 + 1.001 * jax.random.normal(jax.random.fold_in(_gk, 1), (4096, 128), jnp.float32)
        _w = (1.0 + jnp.arange(4096, dtype=jnp.float32)) ** (-0.5)
        _w = _w / _w.mean()
        _pij = jnp.clip(0.00195312 * _w[:, None] * _w[None, :], 0.0, 1.0)
        _a = jax.random.uniform(jax.random.fold_in(_gk, 2), (4096, 4096)) < _pij
        _a = jnp.logical_or(_a, jnp.eye(4096, dtype=bool))
        _af = _a.astype(jnp.float32)
        adj = _af
        return (x, adj)
    x, adj = _rec_inputs()

    def _L0_gnn_setup():
        import jax, jax.numpy as jnp
        import numpy as np
        N = 4096
        F = 128
        NEG_INF = -9000000000000000.0
        ALPHA = 0.2
        THRESH = 1e-06
        key = jax.random.key(seed)
        k1, k2, k3, k4 = jax.random.split(key, 4)
        x = jax.random.normal(k1, (N, F), jnp.float32)
        h0 = jax.random.normal(k2, (N, F), jnp.float32)
        limit = float(np.sqrt(6.0 / (2 * F + 1)) * 1.414)
        a = jax.random.uniform(k3, (2 * F, 1), jnp.float32, -limit, limit)
        temp = jnp.zeros((5,), jnp.float32)
        adj = jax.random.bernoulli(k4, 0.005, (N, N)).astype(jnp.float32)
        adj = jnp.maximum(adj, jnp.eye(N, dtype=jnp.float32))
        return {'x': x, 'h0': h0, 'a': a, 'temp': temp, 'adj': adj, 'l': 1}
    _L0_gnn_all = _L0_gnn_setup()
    _L0_gnn_in = {k: v for k, v in _L0_gnn_all.items() if k in ('h0', 'a', 'temp')}
    del _L0_gnn_all

    def _L1_gnn_setup():
        import jax, jax.numpy as jnp
        import numpy as np
        N = 4096
        F_IN = 128
        F_OUT = 128
        key = jax.random.key(seed)
        k1, k2, k3, k4 = jax.random.split(key, 4)
        return {'input': jax.random.normal(k1, (N, F_IN), dtype=jnp.float32), 'adj': jax.random.uniform(k2, (N, N), dtype=jnp.float32), 'weight': jax.random.normal(k3, (F_IN, F_OUT), dtype=jnp.float32) * (1.0 / np.sqrt(F_OUT)), 'bias': jax.random.normal(k4, (F_OUT,), dtype=jnp.float32) * (1.0 / np.sqrt(F_OUT))}
    _L1_gnn_all = _L1_gnn_setup()
    _L1_gnn_in = {k: v for k, v in _L1_gnn_all.items() if k in ('weight', 'bias')}
    del _L1_gnn_all

    def _L2_gnn_setup():
        import jax, jax.numpy as jnp
        import numpy as np
        from jax import lax
        D_MODEL = 128
        D_STATE = 16
        D_CONV = 4
        EXPAND = 2
        D_INNER = EXPAND * D_MODEL
        DT_RANK = (D_MODEL + 15) // 16
        N = 2048
        EPS = 1e-05

        def _mamba(h, w_in, conv_w, conv_b, w_xp, w_dt, b_dt, A_log, D_skip, w_out):
            L = h.shape[0]
            xz = h @ w_in
            xc, z = (xz[:, :D_INNER], xz[:, D_INNER:])
            xpad = jnp.pad(xc, ((D_CONV - 1, 0), (0, 0)))
            xconv = sum((xpad[k:k + L] * conv_w[:, k] for k in range(D_CONV))) + conv_b
            u = jax.nn.silu(xconv)
            dbc = u @ w_xp
            dt = jax.nn.softplus(dbc[:, :DT_RANK] @ w_dt + b_dt)
            B = dbc[:, DT_RANK:DT_RANK + D_STATE]
            C = dbc[:, DT_RANK + D_STATE:]
            A = -jnp.exp(A_log)
            dA = jnp.exp(dt[:, :, None] * A[None])
            dBu = dt[:, :, None] * B[:, None, :] * u[:, :, None]

            def step(hst, inp):
                dAt, dBut, Ct = inp
                hst = dAt * hst + dBut
                return (hst, hst @ Ct)
            _, ys = lax.scan(step, jnp.zeros((D_INNER, D_STATE), h.dtype), (dA, dBu, C))
            y = ys + u * D_skip
            y = y * jax.nn.silu(z)
            return y @ w_out
        key = jax.random.key(seed)
        ks = jax.random.split(key, 16)
        x = jax.random.normal(ks[0], (N, D_MODEL), dtype=jnp.float32)
        a = jax.random.uniform(ks[1], (N, N), dtype=jnp.float32)
        adj = a / a.sum(axis=1, keepdims=True)
        s = lambda fi, fo: 1.0 / np.sqrt(fi)
        gcn_w = jax.random.uniform(ks[2], (D_MODEL, D_MODEL), jnp.float32, -s(D_MODEL, 0), s(D_MODEL, 0))
        gcn_b = jnp.zeros((D_MODEL,), jnp.float32)
        ln_g = jnp.ones((D_MODEL,), jnp.float32)
        ln_b = jnp.zeros((D_MODEL,), jnp.float32)
        w_in = jax.random.normal(ks[3], (D_MODEL, 2 * D_INNER), jnp.float32) * s(D_MODEL, 0)
        conv_w = jax.random.normal(ks[4], (D_INNER, D_CONV), jnp.float32) * s(D_CONV, 0)
        conv_b = jnp.zeros((D_INNER,), jnp.float32)
        w_xp = jax.random.normal(ks[5], (D_INNER, DT_RANK + 2 * D_STATE), jnp.float32) * s(D_INNER, 0)
        w_dt = jax.random.normal(ks[6], (DT_RANK, D_INNER), jnp.float32) * s(DT_RANK, 0)
        b_dt = jnp.log(jnp.expm1(jnp.exp(jax.random.uniform(ks[7], (D_INNER,), jnp.float32, np.log(0.001), np.log(0.1)))))
        A_log = jnp.log(jnp.broadcast_to(jnp.arange(1, D_STATE + 1, dtype=jnp.float32), (D_INNER, D_STATE)))
        D_skip = jnp.ones((D_INNER,), jnp.float32)
        w_out = jax.random.normal(ks[8], (D_INNER, D_MODEL), jnp.float32) * s(D_INNER, 0)
        return dict(x=x, adj=adj, gcn_w=gcn_w, gcn_b=gcn_b, ln_g=ln_g, ln_b=ln_b, w_in=w_in, conv_w=conv_w, conv_b=conv_b, w_xp=w_xp, w_dt=w_dt, b_dt=b_dt, A_log=A_log, D_skip=D_skip, w_out=w_out)
    _L2_gnn_all = _L2_gnn_setup()
    _L2_gnn_in = {k: v for k, v in _L2_gnn_all.items() if k in ('gcn_w', 'gcn_b', 'ln_g', 'ln_b', 'w_in', 'conv_w', 'conv_b', 'w_xp', 'w_dt', 'b_dt', 'A_log', 'D_skip', 'w_out')}
    del _L2_gnn_all

    def _L3_gnn_setup():
        import jax, jax.numpy as jnp
        import numpy as np
        N = 4096
        D = 128
        CUTOFF = 1.0
        MU = 1.0
        SIGMA = 0.5

        def sensitivity(r, mu, sigma):
            return jnp.exp(-(1.0 / r - 1.0 / mu) ** 2 / (2.0 * sigma * sigma))
        key = jax.random.key(seed)
        k_z, k_d, k_w = jax.random.split(key, 3)
        z = jax.random.normal(k_z, (N, D), dtype=jnp.float32)
        dist_matrix = jax.random.uniform(k_d, (N, N), dtype=jnp.float32) * 2.0 + 0.05
        W = jax.random.normal(k_w, (D, D), dtype=jnp.float32)
        B = jnp.zeros((D,), dtype=jnp.float32)
        return {'z': z, 'dist_matrix': dist_matrix, 'W': W, 'B': B}
    _L3_gnn_all = _L3_gnn_setup()
    _L3_gnn_in = {k: v for k, v in _L3_gnn_all.items() if k in ('W', 'B')}
    del _L3_gnn_all
    return {'x': x, 'adj': adj, 'L0_gnn_h0': _L0_gnn_in['h0'], 'L0_gnn_a': _L0_gnn_in['a'], 'L0_gnn_temp': _L0_gnn_in['temp'], 'L1_gnn_weight': _L1_gnn_in['weight'], 'L1_gnn_bias': _L1_gnn_in['bias'], 'L2_gnn_gcn_w': _L2_gnn_in['gcn_w'], 'L2_gnn_gcn_b': _L2_gnn_in['gcn_b'], 'L2_gnn_ln_g': _L2_gnn_in['ln_g'], 'L2_gnn_ln_b': _L2_gnn_in['ln_b'], 'L2_gnn_w_in': _L2_gnn_in['w_in'], 'L2_gnn_conv_w': _L2_gnn_in['conv_w'], 'L2_gnn_conv_b': _L2_gnn_in['conv_b'], 'L2_gnn_w_xp': _L2_gnn_in['w_xp'], 'L2_gnn_w_dt': _L2_gnn_in['w_dt'], 'L2_gnn_b_dt': _L2_gnn_in['b_dt'], 'L2_gnn_A_log': _L2_gnn_in['A_log'], 'L2_gnn_D_skip': _L2_gnn_in['D_skip'], 'L2_gnn_w_out': _L2_gnn_in['w_out'], 'L3_gnn_W': _L3_gnn_in['W'], 'L3_gnn_B': _L3_gnn_in['B']}

def reference(x, adj, L0_gnn_h0, L0_gnn_a, L0_gnn_temp, L1_gnn_weight, L1_gnn_bias, L2_gnn_gcn_w, L2_gnn_gcn_b, L2_gnn_ln_g, L2_gnn_ln_b, L2_gnn_w_in, L2_gnn_conv_w, L2_gnn_conv_b, L2_gnn_w_xp, L2_gnn_w_dt, L2_gnn_b_dt, L2_gnn_A_log, L2_gnn_D_skip, L2_gnn_w_out, L3_gnn_W, L3_gnn_B):
    import jax
    import jax.numpy as jnp

    def _L0_gnn_ref(x, h0, a, temp, adj, l):
        import jax, jax.numpy as jnp
        import numpy as np
        N = 4096
        F = 128
        NEG_INF = -9000000000000000.0
        ALPHA = 0.2
        THRESH = 1e-06
        Fdim = x.shape[1]
        feat_1 = x @ a[:Fdim]
        feat_2 = x @ a[Fdim:]
        e = jax.nn.leaky_relu(feat_1 + feat_2.T, ALPHA)
        att = jnp.where(adj > 0, e, NEG_INF)
        U = jax.nn.softmax(att, axis=1)
        P = 0.5 * U
        prop_u = U @ x
        rowsum = jnp.sum(U * P, axis=1)
        coe = jax.nn.sigmoid(temp)
        xi = x * rowsum[:, None]
        feat_odd = prop_u - xi
        feat_even = x + prop_u - xi
        feat = coe[2] * feat_odd + (1.0 - coe[2]) * feat_even
        sgn = jnp.sign(feat)
        mod = jnp.abs(feat)
        mod = jnp.where(mod > THRESH, mod - THRESH, 0.0)
        feat = mod * sgn
        pu = U @ feat
        feat_odd2 = feat - coe[3] * pu
        feat_even2 = pu + feat_odd2 * rowsum[:, None]
        feat_odd2 = coe[0] * feat_odd2 + (1.0 - coe[0]) * h0
        out = coe[1] * feat_even2 + (1.0 - coe[1]) * feat_odd2
        return out

    def _L1_gnn_ref(input, adj, weight, bias):
        import jax, jax.numpy as jnp
        import numpy as np
        N = 4096
        F_IN = 128
        F_OUT = 128
        n = input.shape[0]
        a = adj + jnp.eye(n, dtype=adj.dtype)
        d = jax.lax.rsqrt(jnp.sum(a, axis=1))
        adj_norm = d[:, None] * a * d[None, :]
        support = input @ weight
        out = adj_norm @ support + bias
        return out

    def _L2_gnn_ref(x, adj, gcn_w, gcn_b, ln_g, ln_b, w_in, conv_w, conv_b, w_xp, w_dt, b_dt, A_log, D_skip, w_out):
        import jax, jax.numpy as jnp
        import numpy as np
        from jax import lax
        D_MODEL = 128
        D_STATE = 16
        D_CONV = 4
        EXPAND = 2
        D_INNER = EXPAND * D_MODEL
        DT_RANK = (D_MODEL + 15) // 16
        N = 2048
        EPS = 1e-05

        def _mamba(h, w_in, conv_w, conv_b, w_xp, w_dt, b_dt, A_log, D_skip, w_out):
            L = h.shape[0]
            xz = h @ w_in
            xc, z = (xz[:, :D_INNER], xz[:, D_INNER:])
            xpad = jnp.pad(xc, ((D_CONV - 1, 0), (0, 0)))
            xconv = sum((xpad[k:k + L] * conv_w[:, k] for k in range(D_CONV))) + conv_b
            u = jax.nn.silu(xconv)
            dbc = u @ w_xp
            dt = jax.nn.softplus(dbc[:, :DT_RANK] @ w_dt + b_dt)
            B = dbc[:, DT_RANK:DT_RANK + D_STATE]
            C = dbc[:, DT_RANK + D_STATE:]
            A = -jnp.exp(A_log)
            dA = jnp.exp(dt[:, :, None] * A[None])
            dBu = dt[:, :, None] * B[:, None, :] * u[:, :, None]

            def step(hst, inp):
                dAt, dBut, Ct = inp
                hst = dAt * hst + dBut
                return (hst, hst @ Ct)
            _, ys = lax.scan(step, jnp.zeros((D_INNER, D_STATE), h.dtype), (dA, dBu, C))
            y = ys + u * D_skip
            y = y * jax.nn.silu(z)
            return y @ w_out
        h = jax.nn.relu(adj @ x @ gcn_w + gcn_b)
        mu = h.mean(-1, keepdims=True)
        var = h.var(-1, keepdims=True)
        h = (h - mu) * lax.rsqrt(var + EPS) * ln_g + ln_b
        return _mamba(h, w_in, conv_w, conv_b, w_xp, w_dt, b_dt, A_log, D_skip, w_out)

    def _L3_gnn_ref(z, dist_matrix, W, B):
        import jax, jax.numpy as jnp
        import numpy as np
        N = 4096
        D = 128
        CUTOFF = 1.0
        MU = 1.0
        SIGMA = 0.5

        def sensitivity(r, mu, sigma):
            return jnp.exp(-(1.0 / r - 1.0 / mu) ** 2 / (2.0 * sigma * sigma))
        msg = z @ W + B
        sens = sensitivity(dist_matrix, MU, SIGMA)
        weights = jnp.where(dist_matrix < CUTOFF, sens, 0.0)
        return weights @ msg
    x = _layernorm(x + _L0_gnn_ref(x, L0_gnn_h0, L0_gnn_a, L0_gnn_temp, adj, 1), axis=-1)
    x = _layernorm(x + _L1_gnn_ref(x, adj, L1_gnn_weight, L1_gnn_bias), axis=-1)
    x = _layernorm(x + _L2_gnn_ref(x, adj, L2_gnn_gcn_w, L2_gnn_gcn_b, L2_gnn_ln_g, L2_gnn_ln_b, L2_gnn_w_in, L2_gnn_conv_w, L2_gnn_conv_b, L2_gnn_w_xp, L2_gnn_w_dt, L2_gnn_b_dt, L2_gnn_A_log, L2_gnn_D_skip, L2_gnn_w_out), axis=-1)
    x = _layernorm(x + _L3_gnn_ref(x, adj, L3_gnn_W, L3_gnn_B), axis=-1)
    return x

_drawn_inputs = setup_inputs


def setup_inputs(seed=0):
    import zlib

    import numpy as np

    out = dict(_drawn_inputs(seed))
    spreads = {'L0_gnn_temp': (0.0, 0.8),
     'L2_gnn_gcn_b': (0.0, 0.1),
     'L2_gnn_ln_g': (1.0, 0.2),
     'L2_gnn_ln_b': (0.0, 0.1),
     'L2_gnn_conv_b': (0.0, 0.1),
     'L2_gnn_D_skip': (1.0, 0.2),
     'L3_gnn_B': (0.0, 0.1)}
    factors = {}
    for name, (base, spread) in spreads.items():
        noise = np.random.default_rng([zlib.crc32(name.encode()), seed]).standard_normal(out[name].shape)
        drawn = base * np.exp(spread * noise) if base else spread * noise
        out[name] = jnp.asarray(drawn.astype(out[name].dtype))
    for name, factor in factors.items():
        out[name] = (out[name] * factor).astype(out[name].dtype)
    return out
```

```python
from contextlib import ExitStack

import concourse.bass as bass
from concourse import mybir

ALU = mybir.AluOpType
ACT = mybir.ActivationFunctionType
AX_X = mybir.AxisListType.X
F32, BF16, F16 = mybir.dt.float32, mybir.dt.bfloat16, mybir.dt.float16
F8, U8, I32 = mybir.dt.float8e4, mybir.dt.uint8, mybir.dt.int32
RMAX = bass.bass_isa.ReduceOp.max

P = 128
N = 4096
D = 128
NT = N // P
BANK = 512
COLS = D + 3
ALPHA = 0.2
THRESH = 1e-6
EPS = 1e-5
SUMSCALE = 16384.0
HALFMAX = 30000.0
ROWNORM = 11.32
SPREAD = 14.0
DI = 256
NH = DI // P
DS = 16
DTR = 8
KC = 4
T = 1024
NCH = N // T
TB = T // BANK
TPC = T // P


class Chain:

    def __init__(self, eng, sem):
        self.eng, self.sem, self.start, self.per = eng, sem, 0, None

    def begin(self, idx=0, per=None):
        self.idx, self.k = idx, 0
        self.per = self.per if per is None else per

    def __call__(self, ins):
        self.k += 1
        ins.then_inc(self.sem, 1)
        at = self.start + self.k
        if self.per is not None:
            at = at + self.idx * self.per
        self.eng.wait_ge(self.sem, at)

    def end(self):
        if self.per is None:
            self.per = self.k
        assert self.per == self.k

    def close(self, n=1):
        self.start += n * self.per
        self.per = None


def build(nc, A, out):
    ctx = ExitStack()
    with ctx:
        ctx.enter_context(nc.allow_non_contiguous_dma(reason="a few small vectors go to one element a partition"))
        sb = lambda n, s, d: ctx.enter_context(nc.sbuf_tensor(n, s, d))
        sem = lambda n: ctx.enter_context(nc.semaphore(n))

        xs = sb("xs", [P, NT, D], F32)
        feat = sb("feat", [P, NT, D], F32)
        y1 = sb("y1", [P, NT, 2 * COLS], F16)
        y2 = sb("y2", [P, NT, 2 * COLS], F16)
        y1b = sb("y1b", [P, NT, 2 * D], F16)
        y2b = sb("y2b", [P, NT, 2 * D], F16)
        f2row = sb("f2row", [P, N + 4], F32)
        adjt = sb("adjt", [P, 2, N], F32)
        s1r = sb("s1r", [P, 2, N], BF16)
        s1T = sb("s1T", [P, 2, N], F8)
        s2T = sb("s2T", [P, 2, N], F8)
        mT = sb("mT", [P, 2, N], F8)
        idf = sb("idf", [P, P], F32)
        idb = sb("idb", [P, P], BF16)
        ones = sb("ones", [P, P], F32)
        acol = sb("acol", [P, 2], F32)
        a2rep = sb("a2rep", [P, P], F32)
        coe = sb("coe", [P, 5], F32)
        W1 = sb("W1", [P, D], F32)
        Wg = sb("Wg", [P, D], F32)
        b1row = sb("b1row", [P, D], F32)
        bgrow = sb("bgrow", [P, D], F32)
        lng = sb("lng", [P, 1], F32)
        lnb = sb("lnb", [P, 1], F32)
        win = sb("win", [P, 2 * DI], F32)
        wtap = sb("wtap", [P, KC, DI], F32)
        convb = sb("convb", [P, NH], F32)
        wxp = sb("wxp", [P, NH, DTR + 2 * DS], F32)
        wdt = sb("wdt", [DTR, DI], F32)
        bdt = sb("bdt", [P, NH], F32)
        Aneg = sb("Aneg", [P, NH, DS], F32)
        dskip = sb("dskip", [P, NH], F32)
        wout = sb("wout", [P, NH, D], F32)
        f12 = sb("f12", [P, NT, 2], F32)
        nf1 = sb("nf1", [P, NT], F32)
        Ea = sb("Ea", [P, NT], F32)
        Eb = sb("Eb", [P, NT], F32)
        Ea2 = sb("Ea2", [P, NT], F32)
        Eb2 = sb("Eb2", [P, NT], F32)
        EE = sb("EE", [P, 2, NT], F32)
        EE2 = sb("EE2", [P, 2, NT], F32)
        Es = sb("Es", [P, 2, NT], F32)
        Es2 = sb("Es2", [P, 2, NT], F32)
        cnt = sb("cnt", [P, NT], F32)
        deg = sb("deg", [P, NT], F32)
        dinv = sb("dinv", [P, NT], F32)
        dsc = sb("dsc", [P, NT], F32)
        rden = sb("rden", [P, NT], F32)
        rsum = sb("rsum", [P, NT], F32)
        k2 = sb("k2", [P, NT], F32)
        g1 = sb("g1", [P, NT], F32)
        g2 = sb("g2", [P, NT], F32)
        sc = sb("sc", [P, 48], F32)
        stat = sb("stat", [P, 4], F32)
        red = sb("red", [P, 4], F32)
        ta = sb("ta", [P, 2, 2 * COLS], F32)
        tb = sb("tb", [P, 2 * COLS], F32)
        tc = sb("tc", [P, COLS + 9], F32)
        h0t = sb("h0t", [P, 2, D], F32)
        bn6 = sb("bn6", [P, 6], F32)
        mv = sb("mv", [P, 2], F32)
        rstd = sb("rstd", [P, 2], F32)
        xTt = sb("xTt", [P, 2, P], F32)
        state = sb("state", [P, NH * DS], F32)
        xn = sb("xn", [P, 2, D], F32)
        x3t = sb("x3t", [P, D], F32)
        flag = sb("flag", [P, 1], I32)
        W3, b3row = ones, a2rep
        outt = xn

        cwrow = s1r[:, 0, 0:2 * DI * KC].bitcast(F32)
        dbcs = mT[0:DTR + 2 * DS, 0, :].bitcast(F32)

        PS = ctx.enter_context(nc.psum_tensor("PS", [P, 8, BANK], F32))

        stS = nc.dram_tensor("scratch_s1T", [NT, P, N], U8).ap()
        stM = nc.dram_tensor("scratch_mT", [NT, P, N], U8).ap()
        f2d = nc.dram_tensor("scratch_f2", [1, N], F32).ap()
        bcd = nc.dram_tensor("scratch_bc", [2 * DS, N], F32).ap()

        h2T = f2row
        xT = feat[:, :, :].rearrange("p t d -> p (t d)")
        adj_rows = A["adj"].rearrange("(t p) n -> t p n", p=P)
        h0_rows = A["L0_gnn_h0"].rearrange("(t p) d -> t p d", p=P)
        out_rows = out.rearrange("(t p) d -> t p d", p=P)

        S = {n: sem(n) for n in (
            "pad", "s_f2d", "s_flag", "s_x", "s_w", "s_id", "s_tr0", "s_xT", "s_f", "s_fc", "s_col", "s_red", "s_ex", "s_exd", "s_y0", "s_y0a", "s_init",
            "v_chain", "a_chain", "g_chain", "p_w",
            "adj0", "adj1", "a_s1", "a_adjT", "a_adjE", "a_s1Tp", "a_s1E", "a_s2", "a_prod", "a_ta", "a_tail", "a_feat", "a_low", "a_spl", "a_stS0", "a_stS1", "a_stM0", "a_stM1",
            "b_ldS0", "b_ldS1", "b_ldM0", "b_ldM1", "b_h0", "b_h1", "b_s2", "b_prod", "b_ta", "b_var", "b_std", "b_x1", "b_xTp", "b_xTe", "b_y", "b_hi", "b_tail", "b_low", "b_cp",
            "c_ldM0", "c_ldM1", "c_prod", "c_ta", "c_var", "c_std", "c_x", "c_xTp", "c_xTe", "c_y", "c_hi", "c_low", "c_cp", 
            "d_ldM0", "d_ldM1", "d_prod", "d_ta", "d_var", "d_std", "d_x", "d_xTp", "d_xTe", 
            "m_x", "m_u", "m_z", "m_sz", "m_dbc", "m_dbcE", "m_dt", "m_sp", "m_dtu", "m_bcS", "m_B0", "m_B1", "m_C0", "m_C1",
            "m_dA", "m_dBu", "m_h", "m_st", "m_hC", "m_y", "m_yg", "m_yo", "m_o", "m_var", "m_std", "m_x3", "m_out0", "m_out1", "m_s0")}

        S.update({"g_" + n: sem("g_" + n) for n in ("bar", "in", "adj", "ask", "did", "rows", "tr", "trE", "prod", "end",
                                                    "hx", "hT", "hE", "px", "pT", "pE", "py", "pd", "fin", "var", "std", "out")})

        def passed(eng):
            eng.sem_inc(S["pad"], 1)


        work = adjt[:, :, :].rearrange("p a n -> p (a n)").rearrange("p (k t) -> p k t", t=T)
        u, dt, dtu, sz = work[:, 0:2, :], work[:, 2:4, :], work[:, 4:6, :], work[:, 6:8, :]
        ring = s1r[:, :, :].rearrange("p a n -> p (a n)").bitcast(F32).rearrange("p (k t) -> p k t", t=T)
        Br, Cr = ring[:, 0:2, :], ring[:, 2:4, :]
        wa = y1b[:, :, :].rearrange("p t d -> p (t d)").bitcast(F32).rearrange("p (k t) -> p k t", t=T)
        wb = y2b[:, :, :].rearrange("p t d -> p (t d)").bitcast(F32).rearrange("p (k t) -> p k t", t=T)
        dA, hh, dBu, hC = wa[:, 0:2, :], wa[:, 2:4, :], wb[:, 0:2, :], wb[:, 2:4, :]
        sp = s1T[:, :, :].rearrange("p a n -> p (a n)").bitcast(F32).rearrange("p (k t) -> p k t", t=T)
        sp2 = s2T[:, :, :].rearrange("p a n -> p (a n)").bitcast(F32).rearrange("p (k t) -> p k t", t=T)
        PER = NH * DS

        def chunks(eng, chunk, c0):
            chunk(c0, 0)
            with eng.Fori(1, NCH) as a:
                chunk(a + c0 if c0 else a, a)

        def bank2(b):
            return PS[:, b:b + TB, :].rearrange("p b n -> p (b n)")

        def mamba_sync(q, c0):
            def chunk(c, a):
                q.wait_ge(S["m_dbcE"], c + 1)
                passed(q)
                q.dma_start(bcd[:, bass.ds(a * T, T)], dbcs[DTR:DTR + 2 * DS, :]).then_inc(S["m_bcS"], 16)
                q.wait_ge(S["m_bcS"], c * 16 + 16)
                passed(q)
                for n in range(DS):
                    if n < 2:
                        q.wait_ge(S["m_hC"], c * PER)
                        passed(q)
                        q.wait_ge(S["m_dBu"], c * PER)
                    else:
                        q.wait_ge(S["m_dBu"], c * PER + NH * (n - 1))
                        passed(q)
                        q.wait_ge(S["m_hC"], c * PER + NH * (n - 1))
                    k = n % 2
                    passed(q)
                    q.dma_start(Br[:, k, :], bcd[n, bass.ds(a * T, T)].partition_broadcast(P)).then_inc(S[f"m_B{k}"], 16)
                    q.dma_start(Cr[:, k, :], bcd[DS + n, bass.ds(a * T, T)].partition_broadcast(P)).then_inc(S[f"m_C{k}"], 16)
                for t in range(TPC):
                    q.wait_ge(S["m_x3"], c * TPC + t + 1)
                    passed(q)
                    q.dma_start(out_rows[bass.ds(a * TPC + t, 1)].rearrange("o p d -> (o p) d"), outt[:, t % 2, :]).then_inc(S[f"m_out{t % 2}"], 16)
            chunks(q, chunk, c0)

        def mamba_pe(p, c0):
            p.wait_ge(S["m_s0"], 4 if c0 else 2)
            def chunk(c, a):
                p.wait_ge(S["m_o"], c * TPC)
                for h in range(NH):
                    for b in range(TB):
                        for k in range(KC):
                            ins = p.matmul(PS[:, TB * h + b, :], wtap[:, k, h * P:(h + 1) * P], h2T[:, bass.ds(a * T + (b * BANK + k), BANK)], start=(k == 0), stop=(k == KC - 1))
                    ins.then_inc(S["m_x"], 1)
                for h in range(NH):
                    for b in range(TB):
                        ins = p.matmul(PS[:, 4 + TB * h + b, :], win[:, DI + h * P:DI + (h + 1) * P], h2T[:, bass.ds(a * T + (b * BANK + KC - 1), BANK)], start=True, stop=True)
                    ins.then_inc(S["m_z"], 1)
                p.wait_ge(S["m_u"], c * NH + NH)
                for b in range(TB):
                    for h in range(NH):
                        ins = p.matmul(PS[0:DTR + 2 * DS, b, :], wxp[:, h, :], u[:, h, b * BANK:(b + 1) * BANK], start=(h == 0), stop=(h == NH - 1))
                ins.then_inc(S["m_dbc"], 1)
                p.wait_ge(S["m_dbcE"], c + 1)
                p.wait_ge(S["m_sz"], c * NH + NH)
                for h in range(NH):
                    for b in range(TB):
                        ins = p.matmul(PS[:, 4 + TB * h + b, :], wdt[:, h * P:(h + 1) * P], dbcs[0:DTR, b * BANK:(b + 1) * BANK], start=True, stop=True)
                    ins.then_inc(S["m_dt"], 1)
                for i in range(PER):
                    h = i % NH
                    p.wait_ge(S["m_hC"], c * PER + i + 1)
                    for b in range(TB):
                        ins = p.matmul(PS[:, TB * h + b, :], idf[:], hC[:, i % 2, b * BANK:(b + 1) * BANK], start=(i < NH), stop=(i >= PER - NH))
                    ins.then_inc(S["m_y"], 1)
                p.wait_ge(S["m_yg"], c * NH + NH)
                p.wait_ge(S["m_sp"], c * NH + NH)
                for t in range(TPC):
                    bank = 4 + t % 4
                    if t >= 4:
                        p.wait_ge(S["m_o"], c * TPC + t - 3)
                    for h in range(NH):
                        ins = p.matmul(PS[:, bank, 0:D], dtu[:, h, t * P:(t + 1) * P], wout[:, h, :], start=(h == 0), stop=(h == NH - 1))
                    ins.then_inc(S["m_yo"], 1)
            chunks(p, chunk, c0)

        def mamba_scalar(s, ch, c0):
            def chunk(c, a):
                ch.begin(a, 4 * NH)
                s.wait_ge(S["m_yo"], c * TPC)
                for h in range(NH):
                    s.wait_ge(S["m_x"], c * NH + h + 1)
                    s.activation(u[:, h, :], bank2(TB * h), ACT.Silu, bias=convb[:, h:h + 1]).then_inc(S["m_u"], 1)
                for h in range(NH):
                    s.wait_ge(S["m_z"], c * NH + h + 1)
                    s.activation(sz[:, h, :], bank2(4 + TB * h), ACT.Silu).then_inc(S["m_sz"], 1)
                s.wait_ge(S["m_dbc"], c + 1)
                s.wait_ge(S["m_bcS"], c * 16)
                s.activation(dbcs, PS[0:DTR + 2 * DS, 0:TB, :].rearrange("p b n -> p (b n)"), ACT.Copy).then_inc(S["m_dbcE"], 1)
                for h in range(NH):
                    v_ = bank2(4 + TB * h)
                    s.wait_ge(S["m_dt"], c * NH + h + 1)
                    if h:
                        s.wait_ge(S["m_dtu"], c * NH + h)
                    ch(s.activation(sp2[:, 0, :], v_, ACT.Abs, bias=bdt[:, h:h + 1]))
                    ch(s.activation(sp2[:, 0, :], sp2[:, 0, :], ACT.Exp, scale=-1.0))
                    ch(s.activation(sp2[:, 1, :], v_, ACT.Relu, bias=bdt[:, h:h + 1]))
                    ch(s.activation(sp[:, 0, :], sp2[:, 0, :], ACT.Identity, bias=1.0))
                    s.activation(sp[:, 1, :], sp[:, 0, :], ACT.Ln).then_inc(S["m_sp"], 1)
                for i in range(PER):
                    n, h = i // NH, i % NH
                    if i == 0:
                        s.wait_ge(S["m_dtu"], c * NH + NH)
                    if i < 2:
                        s.wait_ge(S["m_h"], c * PER)
                    else:
                        s.wait_ge(S["m_h"], c * PER + i - 1)
                    s.activation(dA[:, i % 2, :], dt[:, h, :], ACT.Exp, scale=Aneg[:, h, n:n + 1]).then_inc(S["m_dA"], 1)
                for t in range(TPC):
                    s.wait_ge(S["m_var"], c * 2 * TPC + 2 * t + 1)
                    s.activation(rstd[:, 0:1], mv[:, 1:2], ACT.Sqrt, bias=sc[:, 12:13]).then_inc(S["m_std"], 1)
                    s.wait_ge(S["m_var"], c * 2 * TPC + 2 * t + 2)
                    s.activation(rstd[:, 1:2], mv[:, 1:2], ACT.Sqrt, bias=sc[:, 12:13]).then_inc(S["m_std"], 1)
                ch.end()
            chunks(s, chunk, c0)
            ch.close(NCH)

        def mamba_gpsimd(g, c0):
            def chunk(c, a):
                g.wait_ge(S["m_dtu"], c * NH + NH)
                for i in range(PER):
                    n, h = i // NH, i % NH
                    if h == 0:
                        g.wait_ge(S[f"m_B{n % 2}"], c * (8 * DS) + 16 * (n // 2 + 1))
                    if i < 2:
                        g.wait_ge(S["m_h"], c * PER)
                    else:
                        g.wait_ge(S["m_h"], c * PER + i - 1)
                    g.tensor_tensor(dBu[:, i % 2, :], dtu[:, h, :], Br[:, n % 2, :], ALU.mult).then_inc(S["m_dBu"], 1)
            chunks(g, chunk, c0)

        def mamba_vector(v, ct, norm, c0):
            def chunk(c, a):
                ct.begin(a, 4 * NH + (7 if c0 else 6) * TPC)
                for h in range(NH):
                    v.wait_ge(S["m_sp"], c * NH + h + 1)
                    ct(v.scalar_tensor_tensor(out=dt[:, h, :], in0=sp[:, 0, :], scalar=1.0, in1=sp2[:, 0, :], op0=ALU.subtract, op1=ALU.subtract))
                    ct(v.tensor_tensor(dt[:, h, :], sp[:, 1, :], dt[:, h, :], ALU.subtract))
                    ct(v.tensor_tensor(dt[:, h, :], dt[:, h, :], sp2[:, 1, :], ALU.add))
                    v.tensor_tensor(dtu[:, h, :], dt[:, h, :], u[:, h, :], ALU.mult).then_inc(S["m_dtu"], 1)
                def readout(i):
                    n, h = i // NH, i % NH
                    if h == 0:
                        v.wait_ge(S[f"m_C{n % 2}"], c * (8 * DS) + 16 * (n // 2 + 1))
                    if i < 2:
                        v.wait_ge(S["m_y"], c * PER)
                    else:
                        v.wait_ge(S["m_y"], c * PER + i - 1)
                    v.wait_ge(S["m_h"], c * PER + i + 1)
                    v.tensor_tensor(hC[:, i % 2, :], hh[:, i % 2, :], Cr[:, n % 2, :], ALU.mult).then_inc(S["m_hC"], 1)
                    v.tensor_copy(state[:, i:i + 1], hh[:, i % 2, T - 1:T]).then_inc(S["m_st"], 1)
                for i in range(PER):
                    v.wait_ge(S["m_dA"], c * PER + i + 1)
                    v.wait_ge(S["m_dBu"], c * PER + i + 1)
                    v.wait_ge(S["m_st"], c * PER + (i - 1 if i >= 2 else 0))
                    v.tensor_tensor_scan(hh[:, i % 2, :], dA[:, i % 2, :], dBu[:, i % 2, :], state[:, i:i + 1], ALU.mult, ALU.add).then_inc(S["m_h"], 1)
                    if i:
                        readout(i - 1)
                readout(PER - 1)
                v.wait_ge(S["m_y"], c * PER + PER)
                v.wait_ge(S["m_st"], c * PER + PER)
                for h in range(NH):
                    ct(v.scalar_tensor_tensor(out=u[:, h, :], in0=u[:, h, :], scalar=dskip[:, h:h + 1], in1=bank2(TB * h), op0=ALU.mult, op1=ALU.add))
                    v.tensor_tensor(dtu[:, h, :], u[:, h, :], sz[:, h, :], ALU.mult).then_inc(S["m_yg"], 1)
                for t in range(TPC):
                    r = xs[:, bass.ds(a * TPC + t, 1), :].rearrange("p o d -> p (o d)")
                    v.wait_ge(S["m_yo"], c * TPC + t + 1)
                    ct(v.tensor_tensor(tb[:, 0:D], PS[:, 4 + t % 4, 0:D], r, ALU.add))
                    v.sem_inc(S["m_o"], 1)
                    ct(norm("m", tb[:, 0:D], x3t[:], 0, c * 2 * TPC + 2 * t + 1))
                    if c0:
                        passed(v)
                        ct(v.tensor_copy(r, x3t[:]))
                    if t >= 2:
                        v.wait_ge(S[f"m_out{t % 2}"], c * 64 + 16 * (t // 2))
                    else:
                        v.wait_ge(S[f"m_out{t % 2}"], c * 64)
                    norm("m", x3t[:], outt[:, t % 2, :], 1, c * 2 * TPC + 2 * t + 2).then_inc(S["m_x3"], 1)
                    v.wait_ge(S["m_x3"], c * TPC + t + 1)
                ct.end()
            chunks(v, chunk, c0)
            ct.close(NCH)


        A0, A1 = adjt[:, 0, :], adjt[:, 1, :]
        GT = s1r[:, :, :].rearrange("p a n -> p (a n)").bitcast(F32)
        KEYS1, KEYS2, CONV, GCN, DIST = range(5)
        ASKS = [2, 2, 1, 1, 3]
        RHS = [xs, feat, feat, feat, feat]
        STEPS = [17, 14, 7, 6, 9]
        NEG = -9000000000000000.0

        def if_general(eng, body):
            eng.wait_ge(S["s_flag"], 1)
            r = eng.value_load(flag[0:1, 0:1])
            with eng.If(r > 0):
                eng.drain().then_inc(S["g_bar"], 1)
                eng.wait_ge(S["g_bar"], 5)
                body(eng)

        def general_sync(q):
            q.dma_start(xs[:, :, :], A["x"].rearrange("(t p) d -> p t d", p=P)).then_inc(S["g_in"], 16)
            q.dma_start(f2row[:, 0:N], f2d[0].partition_broadcast(P)).then_inc(S["g_in"], 16)
            q.dma_start(W3[:], A["L3_gnn_W"]).then_inc(S["g_in"], 16)
            q.dma_start(b3row[:], A["L3_gnn_B"].partition_broadcast(P)).then_inc(S["g_in"], 16)
            for m in range(5):
                if m == DIST:
                    mamba_sync(q, NCH)
                    for par in range(2):
                        q.wait_ge(S[f"m_out{par}"], 16 * NT)
                with q.Fori(0, NT) as it:
                    q.wait_ge(S["g_end"], it + (1 + m * NT))
                    passed(q)
                    if m == KEYS2:
                        q.dma_start(h0t[:, 0, :], h0_rows[bass.ds(it, 1)].rearrange("o p d -> (o p) d")).then_inc(S["g_adj"], 16)
                    q.dma_start(A0, adj_rows[bass.ds(it, 1)].rearrange("o p n -> (o p) n")).then_inc(S["g_adj"], 16)
                    if m == DIST:
                        q.wait_ge(S["g_fin"], it + 2)
                        passed(q)
                        q.dma_start(out_rows[bass.ds(it, 1)].rearrange("o p d -> (o p) d"), outt[:, 0, :]).then_inc(S["g_out"], 16)
            q.wait_ge(S["g_out"], 16 * NT)

        def general_pe(p):
            def product(m):
                with p.Fori(0, NT) as it:
                    p.wait_ge(S["g_rows"], it + (1 + m * NT))
                    for g in range(8):
                        if g >= 2:
                            p.wait_ge(S["g_trE"], it * 8 + (8 * m * NT + g - 1))
                        for k in range(4):
                            j = 4 * g + k
                            src = A0 if m in (CONV, GCN) else A1
                            ins = p.transpose(PS[:, 4 + g % 2, k * P:(k + 1) * P], src[:, j * P:(j + 1) * P], idf[:])
                        ins.then_inc(S["g_tr"], 1)
                    p.wait_ge(S["g_trE"], it * 8 + (8 * m * NT + 8))
                    for j in range(NT):
                        ins = p.matmul(PS[:, 0, 0:D], GT[:, j * P:(j + 1) * P], RHS[m][:, j, :], start=(j == 0), stop=(j == NT - 1))
                    ins.then_inc(S["g_prod"], 1)
                    if m == GCN:
                        p.wait_ge(S["g_hx"], it + 1)
                        p.transpose(PS[:, 6, 0:P], xn[:, 0, :], idf[:]).then_inc(S["g_hT"], 1)

            def project(k, W):
                with p.Fori(0, NT) as t:
                    p.wait_ge(S["g_px"], t + (1 + k * NT))
                    p.transpose(PS[:, 4, 0:P], xn[:, 0, :], idf[:]).then_inc(S["g_pT"], 1)
                    p.wait_ge(S["g_pE"], t + (1 + k * NT))
                    p.matmul(PS[:, 5, 0:D], xTt[:, 0, :], W[:], start=True, stop=True).then_inc(S["g_py"], 1)
            product(KEYS1)
            product(KEYS2)
            project(0, W1)
            product(CONV)
            project(1, Wg)
            product(GCN)
            p.wait_ge(S["g_hE"], NT)
            mamba_pe(p, NCH)
            project(2, W3)
            product(DIST)

        def general_scalar(s, ch):
            def product(m):
                with s.Fori(0, NT) as it:
                    asks = [sum(ASKS[:m]) * NT]
                    def asked():
                        asks[0] += 1
                        s.wait_ge(S["g_ask"], it * ASKS[m] + asks[0])
                    if m in (KEYS1, KEYS2):
                        asked()
                        s.activation(A1, A1, ACT.Exp, bias=tc[:, 1:2], accum_out=tc[:, 2:3]).then_inc(S["g_did"], 1)
                    if m == KEYS1:
                        asked()
                        s.activation(A0, A1, ACT.Square, accum_out=tc[:, 3:4]).then_inc(S["g_did"], 1)
                    if m == DIST:
                        asked()
                        s.activation(A1, A1, ACT.Square, bias=tc[:, 1:2]).then_inc(S["g_did"], 1)
                        asked()
                        s.activation(A1, A1, ACT.Exp, scale=-2.0).then_inc(S["g_did"], 1)
                    for g in range(8):
                        s.wait_ge(S["g_tr"], it * 8 + (8 * m * NT + g + 1))
                        s.activation(GT[:, g * BANK:(g + 1) * BANK], PS[:, 4 + g % 2, :], ACT.Copy).then_inc(S["g_trE"], 1)
                    if m != KEYS1:
                        asked()
                        s.activation(rstd[:, 0:1], mv[:, 1:2], ACT.Sqrt, bias=sc[:, 12:13]).then_inc(S["g_did"], 1)
                    if m == GCN:
                        s.wait_ge(S["g_hT"], it + 1)
                        s.activation(h2T[:, bass.ds(it * P + 3, P)], PS[:, 6, 0:P], ACT.Identity, scale=lng[:, 0:1], bias=lnb[:, 0:1]).then_inc(S["g_hE"], 1)

            def project(k):
                with s.Fori(0, NT) as t:
                    s.wait_ge(S["g_pT"], t + (1 + k * NT))
                    s.activation(xTt[:, 0, :], PS[:, 4, 0:P], ACT.Copy).then_inc(S["g_pE"], 1)
            product(KEYS1)
            product(KEYS2)
            s.wait_ge(S["g_fin"], 1)
            s.activation(dsc[:], dinv[:], ACT.Sqrt).then_inc(S["g_std"], 1)
            project(0)
            product(CONV)
            project(1)
            product(GCN)
            mamba_scalar(s, ch, NCH)
            project(2)
            product(DIST)

        def general_gpsimd(g):
            mamba_gpsimd(g, NCH)

        def general_vector(v, ct, norm):
            row = lambda ap, t: ap[:, bass.ds(t, 1), :].rearrange("p o d -> p (o d)")
            z = tb[:, 0:D]

            def product(m):
                asks = [0]
                with v.Fori(0, NT) as it:
                    one = lambda ap: ap[:, bass.ds(it, 1)]
                    base = sum(ASKS[:m]) * NT
                    ct.begin(it, STEPS[m])

                    def ask(ins):
                        asks[0] += 1
                        ins.then_inc(S["g_ask"], 1)
                        v.wait_ge(S["g_did"], it * ASKS[m] + (base + asks[0]))
                    loads = 2 if m == KEYS2 else 1
                    v.wait_ge(S["g_adj"], it * (16 * loads) + 16 * (loads + (m + (m > KEYS2)) * NT))
                    if m in (KEYS1, KEYS2):
                        if m == KEYS1:
                            ct(v.tensor_reduce(tc[:, 4:5], A0, AX_X, ALU.add))
                            passed(v)
                            ct(v.tensor_copy(one(deg), tc[:, 4:5]))
                        ct(v.tensor_scalar(A1, f2row[:, 0:N], f12[:, bass.ds(it, 1), 0], None, ALU.add))
                        ct(v.scalar_tensor_tensor(out=A1, in0=A1, scalar=ALPHA, in1=A1, op0=ALU.mult, op1=ALU.max))
                        ct(v.tensor_scalar(A0, A0, 0.0, NEG, ALU.is_le, ALU.mult))
                        ct(v.tensor_tensor(A1, A1, A0, ALU.add))
                        ct(v.tensor_reduce(tc[:, 0:1], A1, AX_X, ALU.max))
                        ask(v.tensor_scalar(tc[:, 1:2], tc[:, 0:1], -1.0, None, ALU.mult))
                        if m == KEYS1:
                            ask(v.tensor_copy(tc[:, 0:1], tc[:, 2:3]))
                        v.sem_inc(S["g_rows"], 1)
                    elif m == DIST:
                        ct(v.memset(tc[:, 1:2], -1.0))
                        ct(v.tensor_scalar(A1, A0, 0.0, 0.001, ALU.is_equal, ALU.mult))
                        ct(v.tensor_tensor(A1, A1, A0, ALU.add))
                        ct(v.reciprocal(A1, A1))
                        ask(v.tensor_scalar(A1, A1, -10000.0, 10000.0, ALU.max, ALU.min))
                        ask(v.tensor_copy(tc[:, 0:1], tc[:, 1:2]))
                        ct(v.scalar_tensor_tensor(out=A1, in0=A0, scalar=1.0, in1=A1, op0=ALU.is_lt, op1=ALU.mult))
                        v.sem_inc(S["g_rows"], 1)
                    else:
                        ct(v.memset(tc[:, 1:2], -1.0))
                        v.sem_inc(S["g_rows"], 1)
                    v.wait_ge(S["g_prod"], it + (1 + m * NT))
                    num = PS[:, 0, 0:D]
                    if m == KEYS1:
                        ct(v.reciprocal(tc[:, 4:5], tc[:, 2:3]))
                        passed(v)
                        ct(v.tensor_copy(one(rden), tc[:, 4:5]))
                        ct(v.tensor_scalar(tc[:, 5:6], tc[:, 3:4], tc[:, 4:5], 0.5, ALU.mult, ALU.mult))
                        ct(v.tensor_scalar(tc[:, 5:6], tc[:, 5:6], tc[:, 4:5], None, ALU.mult))
                        passed(v)
                        ct(v.tensor_copy(one(rsum), tc[:, 5:6]))
                        ct(v.tensor_tensor(tc[:, 6:7], sc[:, 22:23], tc[:, 5:6], ALU.subtract))
                        ct(v.tensor_scalar(z, row(xs, it), tc[:, 6:7], None, ALU.mult))
                        ct(v.scalar_tensor_tensor(out=z, in0=num, scalar=tc[:, 4:5], in1=z, op0=ALU.mult, op1=ALU.add))
                        ct(v.tensor_scalar(tb[:, D:2 * D], z, -THRESH, THRESH, ALU.max, ALU.min))
                        ct(v.tensor_tensor(row(feat, it), z, tb[:, D:2 * D], ALU.subtract))
                    elif m == KEYS2:
                        ct(v.reciprocal(tc[:, 4:5], tc[:, 2:3]))
                        ct(v.tensor_scalar(z, num, tc[:, 4:5], None, ALU.mult))
                        ct(v.scalar_tensor_tensor(out=tb[:, D:2 * D], in0=z, scalar=sc[:, 27:28], in1=row(feat, it), op0=ALU.mult, op1=ALU.add))
                        ct(v.scalar_tensor_tensor(out=z, in0=z, scalar=coe[:, 1:2], in1=row(xs, it), op0=ALU.mult, op1=ALU.add))
                        ct(v.scalar_tensor_tensor(out=z, in0=tb[:, D:2 * D], scalar=one(k2), in1=z, op0=ALU.mult, op1=ALU.add))
                        ct(v.scalar_tensor_tensor(out=z, in0=h0t[:, 0, :], scalar=sc[:, 26:27], in1=z, op0=ALU.mult, op1=ALU.add))
                    elif m == CONV:
                        ct(v.tensor_tensor(z, num, row(feat, it), ALU.add))
                        ct(v.scalar_tensor_tensor(out=z, in0=z, scalar=one(dinv), in1=row(xs, it), op0=ALU.mult, op1=ALU.add))
                        ct(v.tensor_tensor(z, z, b1row[:], ALU.add))
                    elif m == GCN:
                        ct(v.tensor_tensor(z, num, bgrow[:], ALU.add))
                        ct(v.tensor_scalar(z, z, 0.0, None, ALU.max))
                    else:
                        ct(v.tensor_tensor(z, num, row(xs, it), ALU.add))
                    if m != KEYS1:
                        ct(v.bn_stats(bn6[:], z))
                        passed(v)
                        ask(v.bn_aggr(mv[:], bn6[:]))
                        ct(v.reciprocal(rstd[:, 0:1], rstd[:, 0:1]))
                        dst = xn[:, 0, :] if m in (GCN, DIST) else row(xs, it)
                        ct(v.tensor_scalar(dst, z, mv[:, 0:1], rstd[:, 0:1], ALU.subtract, ALU.mult))
                    if m == GCN:
                        v.sem_inc(S["g_hx"], 1)
                        v.wait_ge(S["g_hE"], it + 1)
                    if m == DIST:
                        v.sem_inc(S["g_fin"], 1)
                        v.wait_ge(S["g_out"], it * 16 + 16)
                    passed(v)
                    v.sem_inc(S["g_end"], 1)
                    ct.end()
                ct.close(NT)

            def project(k, scale, bias):
                with v.Fori(0, NT) as t:
                    ct.begin(t, 2)
                    passed(v)
                    ct(v.tensor_copy(xn[:, 0, :], row(xs, t)))
                    v.sem_inc(S["g_px"], 1)
                    v.wait_ge(S["g_py"], t + (1 + k * NT))
                    if scale is not None:
                        ct(v.tensor_scalar(row(feat, t), PS[:, 5, 0:D], scale[:, bass.ds(t, 1)], None, ALU.mult))
                    elif bias is not None:
                        ct(v.tensor_tensor(row(feat, t), PS[:, 5, 0:D], bias, ALU.add))
                    else:
                        passed(v)
                        ct(v.tensor_copy(row(feat, t), PS[:, 5, 0:D]))
                    ct.end()
                ct.close(NT)
            v.wait_ge(S["g_in"], 64)
            v.sem_inc(S["g_end"], 1)
            product(KEYS1)
            ct.begin()
            ct(v.tensor_scalar(k2[:], rsum[:], coe[:, 1:2], sc[:, 25:26], ALU.mult, ALU.add))
            ct.end(); ct.close()
            product(KEYS2)
            ct.begin()
            v.tensor_scalar(dinv[:], deg[:], 1.0, None, ALU.add).then_inc(S["g_fin"], 1)
            v.wait_ge(S["g_std"], 1)
            ct(v.reciprocal(dinv[:], dsc[:]))
            ct.end(); ct.close()
            project(0, dinv, None)
            product(CONV)
            project(1, None, None)
            v.memset(h2T[:, 0:3], 0.0).then_inc(S["m_s0"], 1)
            v.memset(state[:], 0.0).then_inc(S["m_s0"], 1)
            product(GCN)
            mamba_vector(v, ct, norm, NCH)
            for par in range(2):
                v.wait_ge(S[f"m_out{par}"], 16 * NT)
            project(2, None, b3row[:])
            product(DIST)

        block = ctx.enter_context(nc.Block())

        def tiles(eng, step, n=NT, lag=0):
            head = 4 if lag else 2
            for it in range(head):
                step(it, it % 2, it)
            with eng.Fori(head // 2, n // 2) as i:
                step(i * 2, 0, None)
                step(i * 2 + 1, 1, None)
            for it in range(n, n + lag):
                step(it, it % 2, it)

        @block.sync
        def _(q):
            q.dma_start(xs[:, :, :], A["x"].rearrange("(t p) d -> p t d", p=P)).then_inc(S["s_x"], 16)
            q.dma_start(acol[:], A["L0_gnn_a"].rearrange("(k d) o -> d (k o)", k=2)).then_inc(S["s_x"], 16)
            q.dma_start(adjt[:, 0, :], adj_rows[0]).then_inc(S["adj0"], 16)
            q.dma_start(adjt[:, 1, :], adj_rows[1]).then_inc(S["adj1"], 16)
            n_w = 0
            for dst, src in (
                (coe[:], A["L0_gnn_temp"].partition_broadcast(P)),
                (W1[:], A["L1_gnn_weight"]), (Wg[:], A["L2_gnn_gcn_w"]),
                (b1row[:], A["L1_gnn_bias"].partition_broadcast(P)),
                (bgrow[:], A["L2_gnn_gcn_b"].partition_broadcast(P)),
                (lng[:], A["L2_gnn_ln_g"].rearrange("(p o) -> p o", o=1)),
                (lnb[:], A["L2_gnn_ln_b"].rearrange("(p o) -> p o", o=1)),
                (win[:], A["L2_gnn_w_in"]),
                (cwrow, A["L2_gnn_conv_w"].rearrange("e k -> (e k)").partition_broadcast(P)),
                (convb[:], A["L2_gnn_conv_b"].rearrange("(h p) -> p h", p=P)),
                (wxp[:], A["L2_gnn_w_xp"].rearrange("(h p) n -> p h n", p=P)),
                (wdt[:], A["L2_gnn_w_dt"]),
                (bdt[:], A["L2_gnn_b_dt"].rearrange("(h p) -> p h", p=P)),
                (Aneg[:], A["L2_gnn_A_log"].rearrange("(h p) n -> p h n", p=P)),
                (dskip[:], A["L2_gnn_D_skip"].rearrange("(h p) -> p h", p=P)),
                (wout[:], A["L2_gnn_w_out"].rearrange("(h p) n -> p h n", p=P)),
            ):
                q.dma_start(dst, src).then_inc(S["s_w"], 16)
                n_w += 1

            q.wait_ge(S["s_fc"], 8)
            q.dma_start(f2d, f2row[0:1, 0:N]).then_inc(S["s_f2d"], 16)
            def step(it, par, static):
                q.wait_ge(S["a_s1E"], 4 * (it + 1))
                passed(q)
                q.dma_start(stS[bass.ds(it, 1)].rearrange("o p n -> (o p) n"), s1T[:, par, :].bitcast(U8)).then_inc(S[f"a_stS{par}"], 16)
                q.dma_start(stM[bass.ds(it, 1)].rearrange("o p n -> (o p) n"), mT[:, par, :].bitcast(U8)).then_inc(S[f"a_stM{par}"], 16)
                if static is None or static < NT - 2:
                    q.wait_ge(S["a_s1"], it + 1)
                    passed(q)
                    q.dma_start(adjt[:, par, :], adj_rows[bass.ds(it + 2, 1)].rearrange("o p n -> (o p) n")).then_inc(S[f"adj{par}"], 16)
            step(0, 0, 0)
            step(1, 1, 1)
            with q.Fori(1, NT // 2 - 1) as i:
                step(i * 2, 0, None)
                step(i * 2 + 1, 1, None)
            step(NT - 2, 0, NT - 2)
            step(NT - 1, 1, NT - 1)
            for par in range(2):
                q.wait_ge(S[f"a_stS{par}"], 16 * NT // 2)
                q.wait_ge(S[f"a_stM{par}"], 16 * NT // 2)

            def step(it, par, static):
                if static == 0:
                    q.wait_ge(S["a_prod"], NT)
                    q.wait_ge(S["a_s2"], NT)
                elif static == 1:
                    pass
                else:
                    q.wait_ge(S["b_prod"], it - 1)
                passed(q)
                q.dma_start(s1T[:, par, :].bitcast(U8), stS[bass.ds(it, 1)].rearrange("o p n -> (o p) n")).then_inc(S[f"b_ldS{par}"], 16)
                q.dma_start(mT[:, par, :].bitcast(U8), stM[bass.ds(it, 1)].rearrange("o p n -> (o p) n")).then_inc(S[f"b_ldM{par}"], 16)
                if static is None or static >= 2:
                    q.wait_ge(S["b_x1"], it - 1)
                passed(q)
                q.dma_start(h0t[:, par, :], h0_rows[bass.ds(it, 1)].rearrange("o p d -> (o p) d")).then_inc(S[f"b_h{par}"], 16)
            tiles(q, step)

            for st, prev in (("c", "b"), ("d", "c")):
                def step(it, par, static):
                    if static == 0:
                        q.wait_ge(S[prev + "_prod"], NT)
                    elif static != 1:
                        q.wait_ge(S[st + "_prod"], it - 1)
                    passed(q)
                    q.dma_start(mT[:, par, :].bitcast(U8), stM[bass.ds(it, 1)].rearrange("o p n -> (o p) n")).then_inc(S[f"{st}_ldM{par}"], 16)
                tiles(q, step)

            mamba_sync(q, 0)
            for par in range(2):
                q.wait_ge(S[f"m_out{par}"], 16 * NT // 2)
            q.wait_ge(S["s_f2d"], 16)
            if_general(q, general_sync)

        @block.tensor
        def _(p):
            p.wait_ge(S["s_id"], 4)
            p.wait_ge(S["s_x"], 32)
            for t in range(NT):
                g = t // 4
                if t % 4 == 0 and g >= 2:
                    p.wait_ge(S["s_xT"], g - 1)
                ins = p.transpose(PS[:, g % 2, (t % 4) * P:(t % 4 + 1) * P], xs[:, t, :], idf[:])
                if t % 4 == 3:
                    ins.then_inc(S["s_tr0"], 1)
            p.wait_ge(S["s_xT"], NT // 4)
            p.wait_ge(S["s_col"], 1)
            for b in range(8):
                ins = p.matmul(PS[:, b, :], a2rep[:], xT[:, b * BANK:(b + 1) * BANK], start=True, stop=True)
                ins.then_inc(S["s_f"], 1)
            p.wait_ge(S["s_fc"], 8)
            for t in range(NT):
                ins = p.matmul(PS[:, 0, 2 * t:2 * t + 2], xT[:, t * P:(t + 1) * P], acol[:], start=True, stop=True)
            ins.then_inc(S["s_f"], 1)
            p.wait_ge(S["p_w"], 1)
            p.matmul(PS[:, 1, 0:2 * D], ones[:], tb[:, 0:2 * D], start=True, stop=True).then_inc(S["s_f"], 1)

            p.wait_ge(S["s_y0"], 1)
            def step(it, par, static):
                if static is None or static < NT:
                    p.wait_ge(S[f"adj{par}"], 16 * (it // 2 + 1) if static is not None else 16 * (it - par) // 2 + 16)
                    for g in range(8):
                        if static != 0 or g >= 2:
                            p.wait_ge(S["a_adjE"], 8 * it + g - 1)
                        for k in range(4):
                            j = 4 * g + k
                            ins = p.transpose(PS[:, 4 + g % 2, k * P:(k + 1) * P], adjt[:, par, j * P:(j + 1) * P], idf[:])
                        ins.then_inc(S["a_adjT"], 1)
                    p.wait_ge(S["a_s1"], it + 1)
                    for g in range(4):
                        if static != 0 or g >= 2:
                            p.wait_ge(S["a_s1E"], 4 * it + g - 1)
                        bank = PS[:, 6 + g % 2, :].bitcast(BF16)
                        for k in range(8):
                            j = 8 * g + k
                            ins = p.transpose(bank[:, k * P:(k + 1) * P], s1r[:, par, j * P:(j + 1) * P], idb[:])
                        ins.then_inc(S["a_s1Tp"], 1)
                if static is None or static >= 1:
                    op = 1 - par
                    p.wait_ge(S["a_s1E"], 4 * it)
                    if static is None or static >= 3:
                        p.wait_ge(S["a_tail"], it - 2)
                    passed(p)
                    for j in range(NT):
                        p.matmul(PS[:, 2 * op, 0:2 * COLS], s1T[:, op, j * P:(j + 1) * P], y1[:, j, :], start=(j == 0), stop=(j == NT - 1))
                    p.wait_ge(S["a_s2"], it)
                    passed(p)
                    for j in range(NT):
                        ins = p.matmul(PS[:, 2 * op + 1, 0:2 * COLS], s2T[:, op, j * P:(j + 1) * P], y2[:, j, :], start=(j == 0), stop=(j == NT - 1))
                    ins.then_inc(S["a_prod"], 1)
            tiles(p, step, lag=1)

            def step(it, par, static):
                if static == 0:
                    p.wait_ge(S["a_spl"], NT)
                    p.wait_ge(S["a_low"], NT)
                if static is None or static < NT:
                    p.wait_ge(S[f"b_ldS{par}"], (it - par) * 8 + 16)
                    if static is None or static >= 2:
                        p.wait_ge(S["b_tail"], it - 1)
                    passed(p)
                    for j in range(NT):
                        p.matmul(PS[:, 2 * par, 0:2 * D], s1T[:, par, j * P:(j + 1) * P], y1b[:, j, :], start=(j == 0), stop=(j == NT - 1))
                    p.wait_ge(S["b_s2"], it + 1)
                    passed(p)
                    for j in range(NT):
                        ins = p.matmul(PS[:, 2 * par + 1, 0:2 * D], s2T[:, par, j * P:(j + 1) * P], y2b[:, j, :], start=(j == 0), stop=(j == NT - 1))
                    ins.then_inc(S["b_prod"], 1)
                if static is None or static >= 2:
                    project("b", W1, it - 2, par)
            def project(st, W, t, par):
                p.wait_ge(S[st + "_x1" if st == "b" else st + "_x"], t + 1)
                if st == "d" and t is not None:
                    p.wait_ge(S["d_xTe"], t)
                p.transpose(PS[:, 4, 0:P], xn[:, par, :], idf[:]).then_inc(S[st + "_xTp"], 1)
                if W is not None:
                    p.wait_ge(S[st + "_xTe"], t + 1)
                    p.wait_ge(S[st + "_low"], t)
                    p.matmul(PS[:, 5, 0:D], xTt[:, par, :], W[:], start=True, stop=True).then_inc(S[st + "_y"], 1)
            tiles(p, step, lag=2)

            for st, W, y, prev in (("c", Wg, y1, "b"), ("d", None, y2, "c")):
                def step(it, par, static):
                    if static == 0:
                        p.wait_ge(S[prev + "_hi"], NT)
                        p.wait_ge(S[prev + "_low"], NT)
                    if static is None or static < NT:
                        p.wait_ge(S[f"{st}_ldM{par}"], (it - par) * 8 + 16)
                        if static is None or static >= 2:
                            p.wait_ge(S[st + "_x"], it - 1)
                        passed(p)
                        for j in range(NT):
                            ins = p.matmul(PS[:, par, 0:2 * D], mT[:, par, j * P:(j + 1) * P], y[:, j, 0:2 * D], start=(j == 0), stop=(j == NT - 1))
                        ins.then_inc(S[st + "_prod"], 1)
                    if static is None or static >= 2:
                        project(st, W, it - 2, par)
                tiles(p, step, lag=2)
            p.wait_ge(S["d_xTe"], NT)
            mamba_pe(p, 0)
            if_general(p, general_pe)

        @block.gpsimd
        def _(g):
            g.memset(idf[:], 0.0).then_inc(S["s_id"], 1)
            g.memset(idb[:], 0.0).then_inc(S["s_id"], 1)
            g.wait_ge(S["s_id"], 2)
            for m in (idf, idb):
                g.affine_select(out=m[:], in_=m[:], compare_op=ALU.not_equal, fill=1.0, base=0, pattern=[[-1, P]], channel_multiplier=1).then_inc(S["s_id"], 1)
            g.wait_ge(S["s_red"], 1)
            g.partition_all_reduce(stat[:], red[:], P, RMAX).then_inc(S["s_red"], 1)
            def step(it, par, static):
                g.wait_ge(S["a_s1E"], 4 * it + 4)
                if static is None or static >= 2:
                    g.wait_ge(S["a_prod"], it - 1)
                passed(g)
                g.tensor_tensor(s2T[:, par, :], mT[:, par, :], s1T[:, par, :], ALU.subtract, saturate=False).then_inc(S["a_s2"], 1)
            tiles(g, step)
            g.wait_ge(S["s_red"], 3)
            g.partition_all_reduce(stat[:], red[:], P, RMAX).then_inc(S["s_red"], 1)
            for st, x in (("b", "b_x1"), ("c", "c_x")):
                def step(it, par, static):
                    g.wait_ge(S[x], it + 1)
                    g.tensor_copy(xs[:, bass.ds(it, 1), :].rearrange("p o d -> p (o d)"), xn[:, par, :]).then_inc(S[st + "_cp"], 1)
                tiles(g, step)
            mamba_gpsimd(g, 0)
            if_general(g, general_gpsimd)

        @block.scalar
        def _(s):
            ch = Chain(s, S["a_chain"])
            for g in range(8):
                s.wait_ge(S["s_tr0"], g + 1)
                s.activation(xT[:, g * BANK:(g + 1) * BANK], PS[:, g % 2, :], ACT.Copy).then_inc(S["s_xT"], 1)
            for b in range(8):
                s.wait_ge(S["s_f"], b + 1)
                s.activation(f2row[:, b * BANK:(b + 1) * BANK], PS[:, b, :], ACT.Copy).then_inc(S["s_fc"], 1)
            s.wait_ge(S["s_w"], 16 * 16)
            ch.begin()
            ch(s.activation(coe[:], coe[:], ACT.Sigmoid))
            ch(s.activation(Aneg[:], Aneg[:], ACT.Exp))
            ch(s.activation(Aneg[:], Aneg[:], ACT.Copy, scale=-1.0))
            s.wait_ge(S["s_ex"], 1)
            s.activation(EE[:, 0, :], f12[:, :, 1], ACT.Exp, bias=sc[:, 0:1])
            s.activation(EE[:, 1, :], f12[:, :, 1], ACT.Exp, bias=sc[:, 1:2], scale=ALPHA)
            s.activation(Ea[:], Ea2[:], ACT.Exp)
            s.activation(Eb[:], Eb2[:], ACT.Exp)
            ch(s.activation(sc[:, 8:10], sc[:, 6:8], ACT.Sqrt))
            s.sem_inc(S["s_exd"], 1)
            s.wait_ge(S["s_y0a"], 1)
            for t in range(NT):
                s.activation(y1[:, t, 0:D], xs[:, t, :], ACT.Copy, scale=Es[:, 0, t:t + 1])
                ins = s.activation(y2[:, t, 0:D], xs[:, t, :], ACT.Copy, scale=Es[:, 1, t:t + 1])
                ins.then_inc(S["s_init"], 1)
            ch.end(); ch.close()

            def step(it, par, static):
                if static is None or static < NT:
                    for g in range(8):
                        s.wait_ge(S["a_adjT"], 8 * it + g + 1)
                        if g == 0 and (static is None or static >= 2):
                            s.wait_ge(S[f"a_stM{par}"], (it - par) * 8)
                            s.wait_ge(S["a_s2"], it - 1)
                        passed(s)
                        s.activation(mT[:, par, g * BANK:(g + 1) * BANK], PS[:, 4 + g % 2, :], ACT.Copy, saturate=False).then_inc(S["a_adjE"], 1)
                    for g in range(4):
                        s.wait_ge(S["a_s1Tp"], 4 * it + g + 1)
                        if g == 0 and (static is None or static >= 2):
                            s.wait_ge(S[f"a_stS{par}"], (it - par) * 8)
                            s.wait_ge(S["a_prod"], it - 1)
                        passed(s)
                        s.activation(s1T[:, par, g * 1024:(g + 1) * 1024], PS[:, 6 + g % 2, :].bitcast(BF16), ACT.Copy, saturate=False).then_inc(S["a_s1E"], 1)
                if static is None or static >= 2:
                    t = it - 2
                    s.wait_ge(S["a_prod"], it - 1)
                    if static is None or static >= 4:
                        s.wait_ge(S["a_tail"], it - 3)
                    s.activation(ta[:, par, :], PS[:, 2 * par, 0:2 * COLS], ACT.Copy, scale=Ea[:, bass.ds(t, 1)]).then_inc(S["a_ta"], 1)
                    s.wait_ge(S["a_feat"], it - 1)
                    f = feat[:, bass.ds(t, 1), :].rearrange("p o d -> p (o d)")
                    s.activation(y1b[:, bass.ds(t, 1), 0:D].rearrange("p o d -> p (o d)"), f, ACT.Copy, scale=Es2[:, 0, bass.ds(t, 1)])
                    s.activation(y2b[:, bass.ds(t, 1), 0:D].rearrange("p o d -> p (o d)"), f, ACT.Copy, scale=Es2[:, 1, bass.ds(t, 1)]).then_inc(S["a_spl"], 1)
            tiles(s, step, lag=2)

            s.wait_ge(S["s_ex"], 2)
            s.activation(dsc[:], dinv[:], ACT.Sqrt).then_inc(S["s_exd"], 1)

            def rstd_step(st, t, par):
                s.wait_ge(S[st + "_var"], t + 1)
                s.activation(rstd[:, par:par + 1], mv[:, 1:2], ACT.Sqrt, bias=sc[:, 12:13]).then_inc(S[st + "_std"], 1)

            def evac_xT(st, t, par, scale):
                s.wait_ge(S[st + "_xTp"], t + 1)
                s.activation(xTt[:, par, :], PS[:, 4, 0:P], ACT.Copy).then_inc(S[st + "_xTe"], 1)
                s.wait_ge(S[st + "_y"], t + 1)

            def step(it, par, static):
                if static is None or static < NT:
                    s.wait_ge(S["b_prod"], it + 1)
                    if static is None or static >= 2:
                        s.wait_ge(S["b_tail"], it - 1)
                    s.activation(ta[:, par, 0:2 * D], PS[:, 2 * par, 0:2 * D], ACT.Copy, scale=g1[:, bass.ds(it, 1)]).then_inc(S["b_ta"], 1)
                    rstd_step("b", it, par)
                if static is None or static >= 2:
                    t, op = it - 2, par
                    evac_xT("b", t, op, None)
                    s.activation(y1[:, bass.ds(t, 1), 0:D].rearrange("p o d -> p (o d)"), PS[:, 5, 0:D], ACT.Copy, scale=dsc[:, bass.ds(t, 1)]).then_inc(S["b_hi"], 1)
            tiles(s, step, lag=2)

            def step(it, par, static):
                if static is None or static < NT:
                    s.wait_ge(S["c_prod"], it + 1)
                    if static is None or static >= 2:
                        s.wait_ge(S["c_x"], it - 1)
                    s.activation(ta[:, par, 0:D], PS[:, par, D:2 * D], ACT.Copy).then_inc(S["c_ta"], 1)
                    rstd_step("c", it, par)
                if static is None or static >= 2:
                    t, op = it - 2, par
                    evac_xT("c", t, op, None)
                    s.activation(y2[:, bass.ds(t, 1), 0:D].rearrange("p o d -> p (o d)"), PS[:, 5, 0:D], ACT.Copy, scale=sc[:, 11:12]).then_inc(S["c_hi"], 1)
            tiles(s, step, lag=2)

            def step(it, par, static):
                if static is None or static < NT:
                    s.wait_ge(S["d_prod"], it + 1)
                    if static is None or static >= 2:
                        s.wait_ge(S["d_x"], it - 1)
                    s.activation(ta[:, par, 0:D], PS[:, par, D:2 * D], ACT.Copy, scale=sc[:, 13:14]).then_inc(S["d_ta"], 1)
                    rstd_step("d", it, par)
                if static is None or static >= 2:
                    t = it - 2
                    s.wait_ge(S["d_xTp"], t + 1)
                    s.activation(h2T[:, bass.ds(t * P + 3, P)], PS[:, 4, 0:P], ACT.Identity, scale=lng[:, 0:1], bias=lnb[:, 0:1]).then_inc(S["d_xTe"], 1)
            tiles(s, step, lag=2)
            mamba_scalar(s, ch, 0)
            if_general(s, lambda q: general_scalar(q, ch))

        @block.vector
        def _(v):
            ch = Chain(v, S["v_chain"])
            ch.begin()
            ch(v.memset(ones[:], 1.0))
            v.wait_ge(S["s_x"], 32)
            v.tensor_scalar(a2rep[:], ones[:], acol[:, 1:2], None, ALU.mult).then_inc(S["s_col"], 1)
            ch(v.tensor_reduce(red[:, 2:3], xs[:, :, :].rearrange("p t d -> p (t d)"), AX_X, ALU.max))
            ch(v.tensor_reduce(red[:, 3:4], xs[:, :, :].rearrange("p t d -> p (t d)"), AX_X, ALU.min))
            ch(v.tensor_scalar(red[:, 3:4], red[:, 3:4], -1.0, None, ALU.mult))
            ch(v.tensor_tensor(red[:, 2:3], red[:, 2:3], red[:, 3:4], ALU.max))
            v.wait_ge(S["s_w"], 16 * 16)
            ch(v.tensor_tensor(wtap[:, :, :], cwrow.rearrange("p (e k) -> p k e", k=KC),
                               win[:, 0:DI].unsqueeze(1).broadcast_to([P, KC, DI]), ALU.mult))
            ch(v.tensor_tensor(tb[:, 0:D], W1[:], W1[:], ALU.mult))
            v.tensor_tensor(tb[:, D:2 * D], Wg[:], Wg[:], ALU.mult).then_inc(S["p_w"], 1)
            v.wait_ge(S["s_f"], 9)
            ch(v.tensor_copy(f12[:, :, :].rearrange("p t k -> p (t k)"), PS[:, 0, 0:2 * NT]))
            v.wait_ge(S["s_f"], 10)
            ch(v.tensor_reduce(sc[:, 6:8], PS[:, 1, 0:2 * D].rearrange("p (k d) -> p k d", k=2), AX_X, ALU.max))
            ch(v.tensor_scalar(nf1[:], f12[:, :, 0], -1.0, None, ALU.mult))
            ch(v.tensor_reduce(red[:, 0:1], f12[:, :, 1], AX_X, ALU.max))
            ch(v.tensor_reduce(red[:, 1:2], f12[:, :, 1], AX_X, ALU.min))
            v.tensor_scalar(red[:, 1:2], red[:, 1:2], -1.0, None, ALU.mult).then_inc(S["s_red"], 1)
            v.wait_ge(S["s_red"], 2)
            ch(v.tensor_scalar(sc[:, 0:1], stat[:, 0:1], -1.0, None, ALU.mult))
            ch(v.tensor_scalar(sc[:, 1:2], stat[:, 0:1], -ALPHA, None, ALU.mult))
            ch(v.tensor_tensor(sc[:, 14:15], stat[:, 0:1], stat[:, 1:2], ALU.add))
            ch(v.tensor_scalar(sc[:, 2:3], stat[:, 2:3], 1e-30, 1.0 / HALFMAX, ALU.max, ALU.mult))
            ch(v.reciprocal(sc[:, 3:4], sc[:, 2:3]))
            ch(v.tensor_scalar(sc[:, 4:5], sc[:, 2:3], SUMSCALE, None, ALU.mult))
            ch(v.tensor_scalar(sc[:, 5:6], sc[:, 2:3], SUMSCALE * 2.0, None, ALU.mult))
            ch(v.tensor_scalar(Ea[:], f12[:, :, 0], stat[:, 0:1], None, ALU.add))
            ch(v.tensor_scalar(Ea2[:], Ea[:], 1.0 - ALPHA, 0.0, ALU.mult, ALU.min))
            ch(v.tensor_scalar(Eb2[:], Ea[:], ALPHA - 1.0, 0.0, ALU.mult, ALU.min))
            v.memset(sc[:, 12:13], EPS).then_inc(S["s_ex"], 1)
            v.wait_ge(S["s_exd"], 1)
            ch(v.tensor_scalar(Es[:], EE[:], sc[:, 3:4], None, ALU.mult))
            v.tensor_scalar(Es2[:], EE[:], sc[:, 3:4], 0.5, ALU.mult, ALU.mult).then_inc(S["s_y0a"], 1)
            ch(v.tensor_tensor(Ea2[:], Ea[:], Ea[:], ALU.mult))
            ch(v.tensor_tensor(Eb2[:], Eb[:], Eb[:], ALU.mult))
            ch(v.tensor_tensor(EE2[:], EE[:], EE[:], ALU.mult))
            ch(v.tensor_scalar(sc[:, 8:10], sc[:, 8:10], 1e-30, ROWNORM / HALFMAX, ALU.max, ALU.mult))
            ch(v.reciprocal(sc[:, 10:12], sc[:, 8:10]))
            ch(v.tensor_copy(sc[:, 13:14], sc[:, 9:10]))
            ch(v.tensor_scalar(sc[:, 20:25], coe[:, 0:5], -1.0, 1.0, ALU.mult, ALU.add))
            ch(v.tensor_tensor(sc[:, 25:26], sc[:, 21:22], coe[:, 0:1], ALU.mult))
            ch(v.tensor_tensor(sc[:, 26:27], sc[:, 21:22], sc[:, 20:21], ALU.mult))
            ch(v.tensor_scalar(sc[:, 27:28], coe[:, 3:4], -1.0, None, ALU.mult))
            for y, k in ((y1, 0), (y2, 1)):
                for c, E in ((D, EE), (D + 1, EE2)):
                    ch(v.tensor_scalar(y[:, :, c], E[:, k, :], SUMSCALE, None, ALU.mult))
                    ch(v.scalar_tensor_tensor(out=y[:, :, COLS + c], in0=E[:, k, :], scalar=SUMSCALE, in1=y[:, :, c], op0=ALU.mult, op1=ALU.subtract))
                ch(v.memset(y[:, :, D + 2], 1.0))
                ch(v.memset(y[:, :, COLS + D + 2], 0.0))
            for t in range(NT):
                v.wait_ge(S["s_init"], t + 1)
                v.scalar_tensor_tensor(out=y1[:, t, COLS:COLS + D], in0=xs[:, t, :], scalar=Es[:, 0, t:t + 1], in1=y1[:, t, 0:D], op0=ALU.mult, op1=ALU.subtract)
                ins = v.scalar_tensor_tensor(out=y2[:, t, COLS:COLS + D], in0=xs[:, t, :], scalar=Es[:, 1, t:t + 1], in1=y2[:, t, 0:D], op0=ALU.mult, op1=ALU.subtract)
            ins.then_inc(S["s_y0"], 1)
            ch.end(); ch.close()

            ct = Chain(v, S["g_chain"])
            def row(ap, t):
                return ap[:, bass.ds(t, 1), :].rearrange("p o d -> p (o d)")
            def step(it, par, static):
                if static is None or static < NT:
                    ch.begin(it)
                    v.wait_ge(S[f"adj{par}"], (it - par) * 8 + 16)
                    if static is None or static >= 2:
                        v.wait_ge(S["a_s1Tp"], 4 * (it - 1))
                    ch(v.scalar_tensor_tensor(out=s1r[:, par, :], in0=adjt[:, par, :], scalar=0.0, in1=adjt[:, par, :],
                                              op0=ALU.is_gt, op1=ALU.not_equal, accum_out=cnt[:, bass.ds(it, 1)]))
                    v.scalar_tensor_tensor(out=s1r[:, par, :], in0=f2row[:, 0:N], scalar=nf1[:, bass.ds(it, 1)], in1=adjt[:, par, :],
                                           op0=ALU.is_gt, op1=ALU.mult).then_inc(S["a_s1"], 1)
                    ch.end()
                if static is None or static >= 2:
                    t = it - 2
                    one = lambda ap: ap[:, bass.ds(t, 1)]
                    ct.begin(t)
                    Bq = PS[:, 2 * par + 1, 0:2 * COLS]
                    v.wait_ge(S["a_ta"], it - 1)
                    taq = ta[:, par, :]
                    sq = slice(D + 1, D + 2 + COLS, COLS)
                    ct(v.scalar_tensor_tensor(out=tb[:], in0=Bq, scalar=one(Eb), in1=taq, op0=ALU.mult, op1=ALU.add))
                    ct(v.tensor_scalar(tc[:, 0:2], taq[:, sq], one(Ea), None, ALU.mult))
                    ct(v.scalar_tensor_tensor(out=tc[:, 2:4], in0=Bq[:, sq], scalar=one(Eb2), in1=tc[:, 0:2], op0=ALU.mult, op1=ALU.add))
                    ct(v.tensor_copy(tc[:, 6:7], Bq[:, D + 2:D + 3]))
                    ct(v.tensor_tensor(one(deg), PS[:, 2 * par, D + 2:D + 3], tc[:, 6:7], ALU.add))
                    ct(v.tensor_tensor(tc[:, 4:5], tc[:, 2:3], tc[:, 3:4], ALU.add))
                    v.sem_inc(S["a_tail"], 1)
                    ct(v.tensor_tensor(tc[:, 8:8 + D + 1], tb[:, 0:D + 1], tb[:, COLS:COLS + D + 1], ALU.add))
                    ct(v.reciprocal(one(rden), tc[:, 8 + D:9 + D]))
                    ct(v.tensor_scalar(tc[:, 5:6], tc[:, 4:5], one(rden), 0.5 * SUMSCALE, ALU.mult, ALU.mult))
                    ct(v.tensor_scalar(one(rsum), tc[:, 5:6], one(rden), None, ALU.mult))
                    ct(v.tensor_tensor(tc[:, 4:5], sc[:, 22:23], one(rsum), ALU.subtract))
                    ct(v.tensor_tensor(tc[:, 5:6], sc[:, 4:5], one(rden), ALU.mult))
                    ct(v.tensor_scalar(tb[:, 0:D], row(xs, t), tc[:, 4:5], None, ALU.mult))
                    ct(v.scalar_tensor_tensor(out=tb[:, 0:D], in0=tc[:, 8:8 + D], scalar=tc[:, 5:6], in1=tb[:, 0:D], op0=ALU.mult, op1=ALU.add))
                    ct(v.tensor_scalar(tb[:, D:2 * D], tb[:, 0:D], -THRESH, THRESH, ALU.max, ALU.min))
                    v.tensor_tensor(row(feat, t), tb[:, 0:D], tb[:, D:2 * D], ALU.subtract).then_inc(S["a_feat"], 1)
                    v.wait_ge(S["a_spl"], it - 1)
                    for k, y in ((0, y1b), (1, y2b)):
                        ct(v.scalar_tensor_tensor(out=y[:, bass.ds(t, 1), D:2 * D].rearrange("p o d -> p (o d)"), in0=row(feat, t), scalar=Es2[:, k, bass.ds(t, 1)],
                                                  in1=y[:, bass.ds(t, 1), 0:D].rearrange("p o d -> p (o d)"), op0=ALU.mult, op1=ALU.subtract))
                    v.sem_inc(S["a_low"], 1)
                    ct.end()
            tiles(v, step, lag=2)
            ch.close(NT); ct.close(NT)

            ct.begin()
            ct(v.tensor_reduce(red[:, 0:1], cnt[:], AX_X, ALU.add))
            ct(v.tensor_reduce(red[:, 1:2], deg[:], AX_X, ALU.min))
            ct(v.tensor_scalar(red[:, 1:2], red[:, 1:2], 0.5, None, ALU.is_lt))
            ct(v.tensor_scalar(red[:, 2:3], sc[:, 14:15], SPREAD, None, ALU.is_gt))
            v.tensor_tensor(red[:, 3:4], red[:, 1:2], red[:, 2:3], ALU.max).then_inc(S["s_red"], 1)
            v.wait_ge(S["s_red"], 4)
            ct(v.tensor_tensor(stat[:, 0:1], stat[:, 0:1], stat[:, 3:4], ALU.max))
            v.tensor_scalar(flag[:], stat[:, 0:1], 0.5, None, ALU.is_gt).then_inc(S["s_flag"], 1)
            ct(v.tensor_scalar(g1[:], rden[:], sc[:, 5:6], None, ALU.mult))
            ct(v.tensor_tensor(g2[:], g1[:], Eb[:], ALU.mult))
            ct(v.tensor_tensor(g1[:], g1[:], Ea[:], ALU.mult))
            ct(v.tensor_scalar(k2[:], rsum[:], coe[:, 1:2], sc[:, 25:26], ALU.mult, ALU.add))
            ct(v.tensor_scalar(dinv[:], deg[:], 1.0, None, ALU.add))
            v.sem_inc(S["s_ex"], 1)
            v.wait_ge(S["s_exd"], 2)
            ct(v.reciprocal(dinv[:], dsc[:]))
            ct(v.tensor_scalar(dsc[:], dinv[:], sc[:, 10:11], None, ALU.mult))
            ct(v.tensor_scalar(deg[:], dinv[:], sc[:, 8:9], None, ALU.mult))
            v.sem_inc(S["s_ex"], 1)
            ct.end(); ct.close()

            def norm(st, z, dst, par, inc):
                ct(v.bn_stats(bn6[:], z))
                passed(v)
                v.bn_aggr(mv[:], bn6[:]).then_inc(S[st + "_var"], 1)
                v.wait_ge(S[st + "_std"], inc)
                ct(v.reciprocal(rstd[:, par:par + 1], rstd[:, par:par + 1]))
                return v.tensor_scalar(dst, z, mv[:, 0:1], rstd[:, par:par + 1], ALU.subtract, ALU.mult)

            def stepB(it, par, static):
                one = lambda ap: ap[:, bass.ds(it, 1)]
                if static is None or static < NT:
                    masks(it, par, static)
                    ct.begin(it)
                    v.wait_ge(S["b_ta"], it + 1)
                    ct(v.scalar_tensor_tensor(out=tb[:, 0:2 * D], in0=PS[:, 2 * par + 1, 0:2 * D], scalar=one(g2), in1=ta[:, par, 0:2 * D], op0=ALU.mult, op1=ALU.add))
                    v.sem_inc(S["b_tail"], 1)
                    ct(v.tensor_tensor(tb[:, 0:D], tb[:, 0:D], tb[:, D:2 * D], ALU.add))
                    ct(v.scalar_tensor_tensor(out=tb[:, D:2 * D], in0=tb[:, 0:D], scalar=sc[:, 27:28], in1=row(feat, it), op0=ALU.mult, op1=ALU.add))
                    ct(v.scalar_tensor_tensor(out=tb[:, 0:D], in0=tb[:, 0:D], scalar=coe[:, 1:2], in1=row(xs, it), op0=ALU.mult, op1=ALU.add))
                    ct(v.scalar_tensor_tensor(out=tb[:, 0:D], in0=tb[:, D:2 * D], scalar=one(k2), in1=tb[:, 0:D], op0=ALU.mult, op1=ALU.add))
                    v.wait_ge(S[f"b_h{par}"], (it - par) * 8 + 16)
                    ct(v.scalar_tensor_tensor(out=tb[:, 0:D], in0=h0t[:, par, :], scalar=sc[:, 26:27], in1=tb[:, 0:D], op0=ALU.mult, op1=ALU.add))
                    if static is None or static >= 2:
                        v.wait_ge(S["b_xTp"], it - 1)
                        v.wait_ge(S["b_cp"], it - 1)
                    norm("b", tb[:, 0:D], xn[:, par, :], par, it + 1).then_inc(S["b_x1"], 1)
                    v.wait_ge(S["b_x1"], it + 1)
                    ct.end()
                if static is None or static >= 2:
                    lowpart("b", y1, feat, dsc, it - 2)
            def masks(it, par, static):
                v.wait_ge(S[f"b_ldS{par}"], (it - par) * 8 + 16)
                v.wait_ge(S[f"b_ldM{par}"], (it - par) * 8 + 16)
                if static is None or static >= 2:
                    v.wait_ge(S["b_prod"], it - 1)
                passed(v)
                v.tensor_tensor(s2T[:, par, :], mT[:, par, :], s1T[:, par, :], ALU.subtract, saturate=False).then_inc(S["b_s2"], 1)

            def lowpart(st, y, keep, scale, t):
                v.wait_ge(S[st + "_hi"], t + 1)
                sca = scale[:, bass.ds(t, 1)] if keep is not None else scale
                hi = y[:, bass.ds(t, 1), 0:D].rearrange("p o d -> p (o d)")
                low = y[:, bass.ds(t, 1), D:2 * D].rearrange("p o d -> p (o d)")
                if keep is not None:
                    v.tensor_scalar(row(keep, t), PS[:, 5, 0:D], sca, None, ALU.mult)
                v.scalar_tensor_tensor(out=low, in0=PS[:, 5, 0:D], scalar=sca, in1=hi, op0=ALU.mult, op1=ALU.subtract).then_inc(S[st + "_low"], 1)
            tiles(v, stepB, lag=2)
            ct.close(NT)

            def stepC(it, par, static):
                if static is None or static < NT:
                    ct.begin(it)
                    if static == 0:
                        v.wait_ge(S["b_cp"], NT)
                    v.wait_ge(S["c_ta"], it + 1)
                    ct(v.tensor_tensor(tb[:, 0:D], ta[:, par, 0:D], row(feat, it), ALU.add))
                    ct(v.tensor_tensor(tb[:, 0:D], PS[:, par, 0:D], tb[:, 0:D], ALU.add))
                    ct(v.scalar_tensor_tensor(out=tb[:, 0:D], in0=tb[:, 0:D], scalar=deg[:, bass.ds(it, 1)], in1=row(xs, it), op0=ALU.mult, op1=ALU.add))
                    ct(v.tensor_tensor(tb[:, 0:D], tb[:, 0:D], b1row[:], ALU.add))
                    if static is None or static >= 2:
                        v.wait_ge(S["c_xTp"], it - 1)
                        v.wait_ge(S["c_cp"], it - 1)
                    norm("c", tb[:, 0:D], xn[:, par, :], par, it + 1).then_inc(S["c_x"], 1)
                    v.wait_ge(S["c_x"], it + 1)
                    ct.end()
                if static is None or static >= 2:
                    lowpart("c", y2, None, sc[:, 11:12], it - 2)
            tiles(v, stepC, lag=2)
            ct.close(NT)

            def stepD(it, par, static):
                ct.begin(it)
                v.wait_ge(S["d_ta"], it + 1)
                ct(v.scalar_tensor_tensor(out=tb[:, 0:D], in0=PS[:, par, 0:D], scalar=sc[:, 13:14], in1=ta[:, par, 0:D], op0=ALU.mult, op1=ALU.add))
                ct(v.tensor_tensor(tb[:, 0:D], tb[:, 0:D], bgrow[:], ALU.add))
                ct(v.tensor_scalar(tb[:, 0:D], tb[:, 0:D], 0.0, None, ALU.max))
                if static is None or static >= 2:
                    v.wait_ge(S["d_xTp"], it - 1)
                norm("d", tb[:, 0:D], xn[:, par, :], par, it + 1).then_inc(S["d_x"], 1)
                v.wait_ge(S["d_x"], it + 1)
                ct.end()
            v.wait_ge(S["c_cp"], NT)
            v.memset(h2T[:, 0:3], 0.0).then_inc(S["m_s0"], 1)
            v.memset(state[:], 0.0).then_inc(S["m_s0"], 1)
            tiles(v, stepD)
            ct.close(NT)
            mamba_vector(v, ct, norm, 0)
            if_general(v, lambda q: general_vector(q, ct, norm))

    return nc


_INS = ['x', 'adj', 'L0_gnn_h0', 'L0_gnn_a', 'L0_gnn_temp', 'L1_gnn_weight', 'L1_gnn_bias', 'L2_gnn_gcn_w', 'L2_gnn_gcn_b', 'L2_gnn_ln_g', 'L2_gnn_ln_b', 'L2_gnn_w_in', 'L2_gnn_conv_w', 'L2_gnn_conv_b', 'L2_gnn_w_xp', 'L2_gnn_w_dt', 'L2_gnn_b_dt', 'L2_gnn_A_log', 'L2_gnn_D_skip', 'L2_gnn_w_out', 'L3_gnn_W', 'L3_gnn_B']
_OUTS = [((4096, 128), 'float32')]


def kernel(**inputs):
    import numpy as _np
    import concourse.bacc as _bacc
    from concourse import mybir as _mybir
    from concourse.bass_utils import run_bass_kernel_spmd as _run

    nc = _bacc.Bacc("TRN2", target_bir_lowering=False, num_devices=1)
    arrays, args = {}, {}
    for name in _INS:
        a = _np.ascontiguousarray(inputs[name])
        arrays[f"in_{name}_dram"] = a
        args[name] = nc.dram_tensor(f"in_{name}_dram", a.shape, _mybir.dt.from_np(a.dtype), kind="ExternalInput").ap()
    shape, dtype = _OUTS[0]
    out = nc.dram_tensor("out_0_dram", shape, _mybir.dt.from_np(_np.dtype(dtype)), kind="ExternalOutput").ap()
    build(nc, args, out)
    r = _run(nc, [arrays], core_ids=[0])
    return r.results[0]["out_0_dram"]
```

```python
from contextlib import ExitStack

import concourse.bass as bass
from concourse import mybir

ALU = mybir.AluOpType
ACT = mybir.ActivationFunctionType
AX_X = mybir.AxisListType.X
F32, BF16, F16 = mybir.dt.float32, mybir.dt.bfloat16, mybir.dt.float16
F8, U8, I32 = mybir.dt.float8e4, mybir.dt.uint8, mybir.dt.int32
RMAX = bass.bass_isa.ReduceOp.max

P = 128
N = 4096
D = 128
NT = N // P
BANK = 512
COLS = D + 3
ALPHA = 0.2
THRESH = 1e-6
EPS = 1e-5
SUMSCALE = 16384.0
HALFMAX = 30000.0
ROWNORM = 11.32
SPREAD = 14.0
DI = 256
NH = DI // P
DS = 16
DTR = 8
KC = 4
T = 1024
NCH = N // T
TB = T // BANK
TPC = T // P


class Chain:

    def __init__(self, eng, sem):
        self.eng, self.sem, self.start, self.per = eng, sem, 0, None

    def begin(self, idx=0, per=None):
        self.idx, self.k = idx, 0
        self.per = self.per if per is None else per

    def __call__(self, ins):
        self.k += 1
        ins.then_inc(self.sem, 1)
        at = self.start + self.k
        if self.per is not None:
            at = at + self.idx * self.per
        self.eng.wait_ge(self.sem, at)

    def end(self):
        if self.per is None:
            self.per = self.k
        assert self.per == self.k

    def close(self, n=1):
        self.start += n * self.per
        self.per = None


def build(nc, A, out):
    ctx = ExitStack()
    with ctx:
        ctx.enter_context(nc.allow_non_contiguous_dma(reason="a few small vectors go to one element a partition"))
        sb = lambda n, s, d: ctx.enter_context(nc.sbuf_tensor(n, s, d))
        sem = lambda n: ctx.enter_context(nc.semaphore(n))

        xs = sb("xs", [P, NT, D], F32)
        feat = sb("feat", [P, NT, D], F32)
        y1 = sb("y1", [P, NT, 2 * COLS], F16)
        y2 = sb("y2", [P, NT, 2 * COLS], F16)
        y1b = sb("y1b", [P, NT, 2 * D], F16)
        y2b = sb("y2b", [P, NT, 2 * D], F16)
        f2row = sb("f2row", [P, N + 4], F32)
        adjt = sb("adjt", [P, 2, N], F32)
        s1r = sb("s1r", [P, 2, N], BF16)
        s1T = sb("s1T", [P, 2, N], F8)
        s2T = sb("s2T", [P, 2, N], F8)
        mT = sb("mT", [P, 2, N], F8)
        idf = sb("idf", [P, P], F32)
        idb = sb("idb", [P, P], BF16)
        ones = sb("ones", [P, P], F32)
        acol = sb("acol", [P, 2], F32)
        a2rep = sb("a2rep", [P, P], F32)
        coe = sb("coe", [P, 5], F32)
        W1 = sb("W1", [P, D], F32)
        Wg = sb("Wg", [P, D], F32)
        b1row = sb("b1row", [P, D], F32)
        bgrow = sb("bgrow", [P, D], F32)
        lng = sb("lng", [P, 1], F32)
        lnb = sb("lnb", [P, 1], F32)
        win = sb("win", [P, 2 * DI], F32)
        wtap = sb("wtap", [P, KC, DI], F32)
        convb = sb("convb", [P, NH], F32)
        wxp = sb("wxp", [P, NH, DTR + 2 * DS], F32)
        wdt = sb("wdt", [DTR, DI], F32)
        bdt = sb("bdt", [P, NH], F32)
        Aneg = sb("Aneg", [P, NH, DS], F32)
        dskip = sb("dskip", [P, NH], F32)
        wout = sb("wout", [P, NH, D], F32)
        f12 = sb("f12", [P, NT, 2], F32)
        nf1 = sb("nf1", [P, NT], F32)
        Ea = sb("Ea", [P, NT], F32)
        Eb = sb("Eb", [P, NT], F32)
        Ea2 = sb("Ea2", [P, NT], F32)
        Eb2 = sb("Eb2", [P, NT], F32)
        EE = sb("EE", [P, 2, NT], F32)
        EE2 = sb("EE2", [P, 2, NT], F32)
        Es = sb("Es", [P, 2, NT], F32)
        Es2 = sb("Es2", [P, 2, NT], F32)
        cnt = sb("cnt", [P, NT], F32)
        deg = sb("deg", [P, NT], F32)
        dinv = sb("dinv", [P, NT], F32)
        dsc = sb("dsc", [P, NT], F32)
        rden = sb("rden", [P, NT], F32)
        rsum = sb("rsum", [P, NT], F32)
        k2 = sb("k2", [P, NT], F32)
        g1 = sb("g1", [P, NT], F32)
        g2 = sb("g2", [P, NT], F32)
        sc = sb("sc", [P, 48], F32)
        stat = sb("stat", [P, 4], F32)
        red = sb("red", [P, 4], F32)
        ta = sb("ta", [P, 2, 2 * COLS], F32)
        tb = sb("tb", [P, 2 * COLS], F32)
        tc = sb("tc", [P, COLS + 9], F32)
        h0t = sb("h0t", [P, 2, D], F32)
        bn6 = sb("bn6", [P, 6], F32)
        mv = sb("mv", [P, 2], F32)
        bn8 = sb("bn8", [P, TPC, 6], F32)
        mv8 = sb("mv8", [P, TPC, 2], F32)
        rstd8 = sb("rstd8", [P, TPC], F32)
        rstd = sb("rstd", [P, 2], F32)
        xTt = sb("xTt", [P, 2, P], F32)
        state = sb("state", [P, NH * DS], F32)
        xn = sb("xn", [P, 2, D], F32)
        flag = sb("flag", [P, 1], I32)
        W3, b3row = ones, a2rep
        outt = xn

        cwrow = s1r[:, 0, 0:2 * DI * KC].bitcast(F32)

        PS = ctx.enter_context(nc.psum_tensor("PS", [P, 8, BANK], F32))

        stS = nc.dram_tensor("scratch_s1T", [NT, P, N], U8).ap()
        stM = nc.dram_tensor("scratch_mT", [NT, P, N], U8).ap()
        f2d = nc.dram_tensor("scratch_f2", [1, N], F32).ap()
        bcd = nc.dram_tensor("scratch_bc", [2 * DS, N], F32).ap()

        h2T = f2row
        xT = feat[:, :, :].rearrange("p t d -> p (t d)")
        adj_rows = A["adj"].rearrange("(t p) n -> t p n", p=P)
        h0_rows = A["L0_gnn_h0"].rearrange("(t p) d -> t p d", p=P)
        out_rows = out.rearrange("(t p) d -> t p d", p=P)

        S = {n: sem(n) for n in (
            "pad", "s_f2d", "s_flag", "s_x", "s_w", "s_id", "s_tr0", "s_xT", "s_f", "s_fc", "s_col", "s_red", "s_ex", "s_exd", "s_y0", "s_y0a", "s_init",
            "v_chain", "a_chain", "g_chain", "p_w",
            "adj0", "adj1", "a_s1", "a_adjT", "a_adjE", "a_s1Tp", "a_s1E", "a_s2", "a_prod", "a_ta", "a_tail", "a_feat", "a_low", "a_spl", "a_stS0", "a_stS1", "a_stM0", "a_stM1",
            "b_ldS0", "b_ldS1", "b_ldM0", "b_ldM1", "b_h0", "b_h1", "b_s2", "b_prod", "b_ta", "b_var", "b_std", "b_x1", "b_xTp", "b_xTe", "b_y", "b_hi", "b_tail", "b_low", "b_cp",
            "c_ldM0", "c_ldM1", "c_prod", "c_ta", "c_var", "c_std", "c_x", "c_xTp", "c_xTe", "c_y", "c_hi", "c_low", "c_cp", 
            "d_ldM0", "d_ldM1", "d_prod", "d_ta", "d_var", "d_std", "d_x", "d_xTp", "d_xTe", 
            "m_x", "m_u", "m_z", "m_sz", "m_dbc", "m_dbcE", "m_dt", "m_sp", "m_dtu", "m_lp", "m_bcS", "m_BC0", "m_BC1", "m_BC2", "m_BC3",
            "m_dA", "m_dBu", "m_h", "m_st", "m_hC", "m_y", "m_yg", "m_yo", "m_o", "m_var", "m_std", "m_x3", "m_out", "m_s0")}

        S.update({"g_" + n: sem("g_" + n) for n in ("bar", "in", "adj", "ask", "did", "rows", "tr", "trE", "prod", "end",
                                                    "hx", "hT", "hE", "px", "pT", "pE", "py", "pd", "fin", "var", "std", "out")})

        def passed(eng):
            eng.sem_inc(S["pad"], 1)


        def rows(ap):
            return ap.rearrange("p a n -> p (a n)").bitcast(F32)[:, 0:4 * T].rearrange("p (k t) -> p k t", t=T)
        u4, dt4 = rows(y1b[:, :, :]), rows(y2b[:, :, :])
        dtu4 = feat[:, :, :].rearrange("p t d -> p (t d)").rearrange("p (k t) -> p k t", t=T)
        sz4 = y1[:, :, :].rearrange("p t d -> p (t d)")[:, 0:8 * T].bitcast(F32).rearrange("p (k t) -> p k t", t=T)
        tmp = y2[:, :, :].rearrange("p t d -> p (t d)")[:, 0:8 * T].bitcast(F32).rearrange("p (k t) -> p k t", t=T)
        lnw, ex = tmp[:, 0:2, :], tmp[:, 2:4, :]
        yg = lnw
        dbcs = tmp[0:DTR + 2 * DS, 0, :]
        zt = ex[:, 0, :].rearrange("p (t d) -> p t d", d=D)
        zo = ex[:, 1, :].rearrange("p (t d) -> p t d", d=D)
        BC = adjt[:, :, :].rearrange("p a n -> p (a n)").rearrange("p (s k t) -> p s k t", k=2, t=T)
        NB = 4
        hh = s1r[:, :, :].rearrange("p a n -> p (a n)").bitcast(F32).rearrange("p (k t) -> p k t", t=T)
        dA = s1T[:, :, :].rearrange("p a n -> p (a n)").bitcast(F32).rearrange("p (k t) -> p k t", t=T)
        dBu = s2T[:, :, :].rearrange("p a n -> p (a n)").bitcast(F32).rearrange("p (k t) -> p k t", t=T)
        hC = mT[:, :, :].rearrange("p a n -> p (a n)").bitcast(F32).rearrange("p (k t) -> p k t", t=T)
        PER = NH * DS
        CR = {"m_h": 2, "m_dBu": NH * NB, "m_hC": NH * NB, "m_st": 4, "m_y": 2, "m_yg": 2 * NH, "m_o": 2, "m_yo": 2, "m_x3": 2,
              "m_bcS": 16, "m_out": 32}
        PE_AHEAD = {4: range(16), 8: [16], 9: [17], 10: [18], 11: [19], 14: [20], 15: [21], 18: [22], 19: [23]}
        ACT_AHEAD = {7: [0, 1], 12: [2, 3], 17: [4], **{20 + k // 2: [5 + k - 1, 5 + k] for k in range(1, 10, 2)}}
        DVE_AHEAD = {27 + k: [k] for k in range(4)}
        SYNC_AHEAD = 12

        EARLY = 4
        assert min(*PE_AHEAD, *ACT_AHEAD, *DVE_AHEAD) >= EARLY

        def halves(ap, a):
            if isinstance(a, int):
                return ap[:, NH * (a % 2):NH * (a % 2) + NH, :]
            return ap[:, bass.ds((a & 1) * NH, NH), :]

        def half(ap, a, h):
            if isinstance(a, int):
                return ap[:, NH * (a % 2) + h, :]
            return ap[:, bass.ds((a & 1) * NH + h, 1), :].rearrange("p o t -> p (o t)")

        def chunks(eng, ahead, parts, steps, tail, c0):
            for k in range(parts):
                ahead(k, c0, 0)
            steps(c0, 0, 0, EARLY, True)
            def chunk(c, a, more):
                steps(c, a, EARLY, PER, more)
                tail(c, a, more, lambda: steps(c + 1, a + 1, 0, EARLY, True) if more else None)
            with eng.Fori(0, NCH - 1) as a:
                chunk(a + c0 if c0 else a, a, True)
            chunk(c0 + NCH - 1, NCH - 1, False)

        def bank2(b):
            return PS[:, b:b + TB, :].rearrange("p b n -> p (b n)")

        def mamba_sync(q, c0):
            def ahead(k, c, a):
                q.wait_ge(S["m_dbcE"], c + 1)
                passed(q)
                q.dma_start(bcd[:, bass.ds(a * T, T)], dbcs[DTR:DTR + 2 * DS, :]).then_inc(S["m_bcS"], 16)
            def steps(c, a, lo, hi, more):
                if lo == 0:
                    q.wait_ge(S["m_bcS"], c * 16 + (CR["m_bcS"] + 16))
                for n in range(NB if lo else 0, DS if lo else NB):
                    q.wait_ge(S["m_dBu"], c * PER + NH * (n + 1))
                    q.wait_ge(S["m_hC"], c * PER + NH * (n + 1))
                    passed(q)
                    q.dma_start(BC[:, n % NB, :, :], bcd.rearrange("(k n) t -> n k t", k=2)[n, :, bass.ds(a * T, T)].partition_broadcast(P)).then_inc(S[f"m_BC{n % NB}"], 16)
                    if more and n == SYNC_AHEAD:
                        ahead(0, c + 1, a + 1)
            def tail(c, a, more, early):
                early()
                if not c0:
                    q.wait_ge(S["m_x3"], c + (CR["m_x3"] + 1))
                    passed(q)
                    q.dma_start(out.rearrange("(t p) d -> p t d", p=P)[:, bass.ds(a * TPC, TPC), :], zo).then_inc(S["m_out"], 16)
            chunks(q, ahead, 1, steps, tail, c0)

        def mamba_pe(p, c0):
            p.wait_ge(S["m_s0"], 4 if c0 else 2)
            def ahead(k, c, a):
                u_, b = halves(u4, a), k % TB
                if k < 16:
                    h, b, tap = k // 8, k // KC % TB, k % KC
                    if k == 0:
                        p.wait_ge(S["m_o"], c + (CR["m_o"] - 1))
                        p.wait_ge(S["m_sp"], c * NH)
                    ins = p.matmul(PS[:, 4 + TB * h + b, :], wtap[:, tap, h * P:(h + 1) * P], h2T[:, bass.ds(a * T + (b * BANK + tap), BANK)], start=(tap == 0), stop=(tap == KC - 1))
                    if k % 8 == 7:
                        ins.then_inc(S["m_x"], 1)
                elif k < 20:
                    h = k // TB % NH
                    if b == 0:
                        p.wait_ge(S["m_u"], c * NH + h + 1)
                    ins = p.matmul(PS[:, 4 + TB * h + b, :], win[:, DI + h * P:DI + (h + 1) * P], h2T[:, bass.ds(a * T + (b * BANK + KC - 1), BANK)], start=True, stop=True)
                    if b == TB - 1:
                        ins.then_inc(S["m_z"], 1)
                elif k < 22:
                    p.wait_ge(S["m_sz"], c * NH + 1)
                    for h in range(NH):
                        ins = p.matmul(PS[0:DTR + 2 * DS, 4 + b, :], wxp[:, h, :], half(u4, a, h)[:, b * BANK:(b + 1) * BANK], start=(h == 0), stop=(h == NH - 1))
                    if b == TB - 1:
                        ins.then_inc(S["m_dbc"], 1)
                else:
                    h = k - 22
                    p.wait_ge(S["m_dbcE"], c + 1)
                    p.wait_ge(S["m_sz"], c * NH + NH)
                    for b in range(TB):
                        ins = p.matmul(PS[:, 4 + TB * h + b, :], wdt[:, h * P:(h + 1) * P], dbcs[0:DTR, b * BANK:(b + 1) * BANK], start=True, stop=True)
                    ins.then_inc(S["m_dt"], 1)
            def steps(c, a, lo, hi, more):
                for i in range(lo, hi):
                    if more:
                        for k in PE_AHEAD.get(i, ()):
                            ahead(k, c + 1, a + 1)
                    h = i % NH
                    if i == 0:
                        p.wait_ge(S["m_yg"], c * NH + CR["m_yg"])
                    p.wait_ge(S["m_hC"], c * PER + (CR["m_hC"] + i + 1))
                    for b in range(TB):
                        ins = p.matmul(PS[:, TB * h + b, :], idf[:], hC[:, i % 2, b * BANK:(b + 1) * BANK], start=(i < NH), stop=(i >= PER - NH))
                    ins.then_inc(S["m_y"], 1)
            def tail(c, a, more, early):
                p.wait_ge(S["m_sp"], c * NH + (2 * NH if more else NH))
                p.wait_ge(S["m_yg"], c * NH + (CR["m_yg"] + NH))
                for t in range(TPC):
                    for h in range(NH):
                        ins = p.matmul(PS[:, 6 + t // 4, t % 4 * D:t % 4 * D + D], yg[:, h, t * P:(t + 1) * P], wout[:, h, :], start=(h == 0), stop=(h == NH - 1))
                ins.then_inc(S["m_yo"], 1)
                early()
            chunks(p, ahead, 24, steps, tail, c0)

        def mamba_scalar(s, ch, c0):
            def ahead(k, c, a):
                if k < 2:
                    if k == 0:
                        s.wait_ge(S["m_yg"], c * NH + (CR["m_yg"] - NH))
                    s.wait_ge(S["m_x"], c * NH + k + 1)
                    passed(s)
                    s.activation(half(u4, a, k), bank2(4 + TB * k), ACT.Silu, bias=convb[:, k:k + 1]).then_inc(S["m_u"], 1)
                elif k < 4:
                    h = k - 2
                    s.wait_ge(S["m_z"], c * NH + h + 1)
                    passed(s)
                    s.activation(half(sz4, a, h), bank2(4 + TB * h), ACT.Silu).then_inc(S["m_sz"], 1)
                elif k == 4:
                    s.wait_ge(S["m_dbc"], c + 1)
                    s.wait_ge(S["m_yo"], c + (CR["m_yo"] - 1))
                    s.wait_ge(S["m_bcS"], c * 16 + CR["m_bcS"])
                    s.activation(dbcs, PS[0:DTR + 2 * DS, 4:4 + TB, :].rearrange("p b n -> p (b n)"), ACT.Copy).then_inc(S["m_dbcE"], 1)
                else:
                    h, j = (k - 5) // 5, (k - 5) % 5
                    v_, w = bank2(4 + TB * h), half(dtu4, a, h)
                    if j == 0:
                        if h == 0:
                            ch.begin(a, 4 * NH)
                            s.wait_ge(S["m_x3"], c + (CR["m_x3"] - 1))
                            if not c0:
                                s.wait_ge(S["m_out"], c * 16 + (CR["m_out"] - 16))
                        s.wait_ge(S["m_dt"], c * NH + h + 1)
                        ch(s.activation(ex[:, h, :], v_, ACT.Abs, bias=bdt[:, h:h + 1]))
                    elif j == 1:
                        ch(s.activation(ex[:, h, :], ex[:, h, :], ACT.Exp, scale=-1.0))
                    elif j == 2:
                        passed(s)
                        ch(s.activation(half(dt4, a, h), v_, ACT.Relu, bias=bdt[:, h:h + 1]))
                    elif j == 3:
                        passed(s)
                        ch(s.activation(w, ex[:, h, :], ACT.Identity, bias=1.0))
                    else:
                        if h == 0:
                            s.wait_ge(S["m_dt"], c * NH + NH)
                            s.wait_ge(S["m_bcS"], c * 16 + (CR["m_bcS"] + 16))
                        passed(s)
                        s.activation(lnw[:, h, :], w, ACT.Ln).then_inc(S["m_sp"], 1)
                        if h == NH - 1:
                            ch.end()
            def steps(c, a, lo, hi, more):
                for i in range(lo, hi):
                    n, h = i // NH, i % NH
                    if i == 0:
                        s.wait_ge(S["m_dtu"], c + 1)
                    s.wait_ge(S["m_h"], c * PER + (i + 1))
                    passed(s)
                    s.activation(dA[:, i % 2, :], half(dt4, a, h), ACT.Exp, scale=Aneg[:, h, n:n + 1]).then_inc(S["m_dA"], 1)
                    if more:
                        for k in ACT_AHEAD.get(i, ()):
                            ahead(k, c + 1, a + 1)
            def tail(c, a, more, early):
                early()
                for r in range(1 if c0 else 2):
                    s.wait_ge(S["m_var"], (c - c0 if c0 else c) * (1 if c0 else 2) + (2 * NCH if c0 else 0) + r + 1)
                    s.activation(rstd8[:], mv8[:, :, 1], ACT.Sqrt, bias=sc[:, 12:13]).then_inc(S["m_std"], 1)
            chunks(s, ahead, 15, steps, tail, c0)
            ch.close(NCH)

        def mamba_gpsimd(g, c0):
            def steps(c, a, lo, hi, more):
                g.wait_ge(S["m_dtu"], c + 1)
                for i in range(lo, hi):
                    n, h = i // NH, i % NH
                    if h == 0:
                        g.wait_ge(S[f"m_BC{n % NB}"], c * (16 * DS // NB) + 16 * (n // NB + 1))
                    g.wait_ge(S["m_h"], c * PER + (i + 1))
                    passed(g)
                    g.tensor_tensor(dBu[:, i % 2, :], half(dtu4, a, h), BC[:, n % NB, 0, :], ALU.mult).then_inc(S["m_dBu"], 1)
            chunks(g, None, 0, steps, lambda c, a, more, early: early(), c0)

        def mamba_vector(v, ct, c0):
            def ahead(k, c, a):
                if k == 0:
                    v.wait_ge(S["m_sp"], c * NH + NH)
                    ins = v.scalar_tensor_tensor(out=ex, in0=halves(dtu4, a), scalar=1.0, in1=ex, op0=ALU.subtract, op1=ALU.subtract)
                else:
                    v.wait_ge(S["m_lp"], c * 3 + k)
                    if k == 1:
                        ins = v.tensor_tensor(ex, lnw, ex, ALU.subtract)
                    elif k == 2:
                        ins = v.tensor_tensor(halves(dt4, a), halves(dt4, a), ex, ALU.add)
                    else:
                        v.tensor_tensor(halves(dtu4, a), halves(dt4, a), halves(u4, a), ALU.mult).then_inc(S["m_dtu"], 1)
                        return
                ins.then_inc(S["m_lp"], 1)
            def steps(c, a, lo, hi, more):
                def readout(i):
                    n, h = i // NH, i % NH
                    v.wait_ge(S["m_h"], c * PER + (CR["m_h"] + i + 1))
                    v.tensor_copy(state[:, i:i + 1], hh[:, i % 4, T - 1:T]).then_inc(S["m_st"], 1)
                    if h == 0:
                        v.wait_ge(S[f"m_BC{n % NB}"], c * (16 * DS // NB) + 16 * (n // NB + 1))
                    v.wait_ge(S["m_y"], c * PER + (i + 1))
                    v.tensor_tensor(hC[:, i % 2, :], hh[:, i % 4, :], BC[:, n % NB, 1, :], ALU.mult).then_inc(S["m_hC"], 1)
                for i in range(lo, hi):
                    v.wait_ge(S["m_dA"], c * PER + i + 1)
                    v.wait_ge(S["m_dBu"], c * PER + (CR["m_dBu"] + i + 1))
                    v.wait_ge(S["m_st"], c * PER + (i + 1))
                    v.wait_ge(S["m_hC"], c * PER + (CR["m_hC"] + i - 3))
                    v.tensor_tensor_scan(hh[:, i % 4, :], dA[:, i % 2, :], dBu[:, i % 2, :], state[:, i:i + 1], ALU.mult, ALU.add).then_inc(S["m_h"], 1)
                    if more:
                        for k in DVE_AHEAD.get(i, ()):
                            ahead(k, c + 1, a + 1)
                    if i > lo:
                        readout(i - 1)
                readout(hi - 1)
            def tail(c, a, more, early):
                ct.begin(a, 1 + NH + 3 * (1 if c0 else 2))
                v.wait_ge(S["m_y"], c * PER + (CR["m_y"] + PER))
                for h in range(NH):
                    u_ = half(u4, a, h)
                    ct(v.scalar_tensor_tensor(out=u_, in0=u_, scalar=dskip[:, h:h + 1], in1=bank2(TB * h), op0=ALU.mult, op1=ALU.add))
                    v.tensor_tensor(yg[:, h, :], u_, half(sz4, a, h), ALU.mult).then_inc(S["m_yg"], 1)
                early()
                r = xs[:, bass.ds(a * TPC, TPC), :]
                v.wait_ge(S["m_yo"], c + (CR["m_yo"] + 1))
                ct(v.tensor_tensor(zt, PS[:, 6:8, :].rearrange("p b (t d) -> p (b t) d", d=D), r, ALU.add))
                v.sem_inc(S["m_o"], 1)
                for k in range(1 if c0 else 2):
                    for t in range(TPC):
                        ins = v.bn_stats(bn8[:, t, :], zt[:, t, :])
                    ct(ins)
                    passed(v)
                    for t in range(TPC):
                        ins = v.bn_aggr(mv8[:, t, :], bn8[:, t, :])
                    ins.then_inc(S["m_var"], 1)
                    v.wait_ge(S["m_std"], (c - c0 if c0 else c) * (1 if c0 else 2) + (2 * NCH if c0 else 0) + k + 1)
                    ct(v.reciprocal(rstd8[:], rstd8[:]))
                    for t in range(TPC):
                        if c0:
                            dst = xs[:, bass.ds(a * TPC + t, 1), :].rearrange("p o d -> p (o d)")
                        else:
                            dst = zo[:, t, :] if k else zt[:, t, :]
                        ins = v.tensor_scalar(dst, zt[:, t, :], mv8[:, t, 0:1], rstd8[:, t:t + 1], ALU.subtract, ALU.mult)
                    ct(ins)
                v.sem_inc(S["m_x3"], 1)
                ct.end()
            chunks(v, ahead, 4, steps, tail, c0)
            ct.close(NCH)


        A0, A1 = adjt[:, 0, :], adjt[:, 1, :]
        GT = s1r[:, :, :].rearrange("p a n -> p (a n)").bitcast(F32)
        KEYS1, KEYS2, CONV, GCN, DIST = range(5)
        ASKS = [2, 2, 1, 1, 3]
        RHS = [xs, feat, feat, feat, feat]
        STEPS = [17, 14, 7, 6, 9]
        NEG = -9000000000000000.0

        def if_general(eng, body):
            eng.wait_ge(S["s_flag"], 1)
            r = eng.value_load(flag[0:1, 0:1])
            with eng.If(r > 0):
                eng.drain().then_inc(S["g_bar"], 1)
                eng.wait_ge(S["g_bar"], 5)
                body(eng)

        def general_sync(q):
            q.dma_start(xs[:, :, :], A["x"].rearrange("(t p) d -> p t d", p=P)).then_inc(S["g_in"], 16)
            q.dma_start(f2row[:, 0:N], f2d[0].partition_broadcast(P)).then_inc(S["g_in"], 16)
            q.dma_start(W3[:], A["L3_gnn_W"]).then_inc(S["g_in"], 16)
            q.dma_start(b3row[:], A["L3_gnn_B"].partition_broadcast(P)).then_inc(S["g_in"], 16)
            for m in range(5):
                if m == DIST:
                    mamba_sync(q, NCH)
                with q.Fori(0, NT) as it:
                    q.wait_ge(S["g_end"], it + (1 + m * NT))
                    passed(q)
                    if m == KEYS2:
                        q.dma_start(h0t[:, 0, :], h0_rows[bass.ds(it, 1)].rearrange("o p d -> (o p) d")).then_inc(S["g_adj"], 16)
                    q.dma_start(A0, adj_rows[bass.ds(it, 1)].rearrange("o p n -> (o p) n")).then_inc(S["g_adj"], 16)
                    if m == DIST:
                        q.wait_ge(S["g_fin"], it + 2)
                        passed(q)
                        q.dma_start(out_rows[bass.ds(it, 1)].rearrange("o p d -> (o p) d"), outt[:, 0, :]).then_inc(S["g_out"], 16)
            q.wait_ge(S["g_out"], 16 * NT)

        def general_pe(p):
            def product(m):
                with p.Fori(0, NT) as it:
                    p.wait_ge(S["g_rows"], it + (1 + m * NT))
                    for g in range(8):
                        if g >= 2:
                            p.wait_ge(S["g_trE"], it * 8 + (8 * m * NT + g - 1))
                        for k in range(4):
                            j = 4 * g + k
                            src = A0 if m in (CONV, GCN) else A1
                            ins = p.transpose(PS[:, 4 + g % 2, k * P:(k + 1) * P], src[:, j * P:(j + 1) * P], idf[:])
                        ins.then_inc(S["g_tr"], 1)
                    p.wait_ge(S["g_trE"], it * 8 + (8 * m * NT + 8))
                    for j in range(NT):
                        ins = p.matmul(PS[:, 0, 0:D], GT[:, j * P:(j + 1) * P], RHS[m][:, j, :], start=(j == 0), stop=(j == NT - 1))
                    ins.then_inc(S["g_prod"], 1)
                    if m == GCN:
                        p.wait_ge(S["g_hx"], it + 1)
                        p.transpose(PS[:, 6, 0:P], xn[:, 0, :], idf[:]).then_inc(S["g_hT"], 1)

            def project(k, W):
                with p.Fori(0, NT) as t:
                    p.wait_ge(S["g_px"], t + (1 + k * NT))
                    p.transpose(PS[:, 4, 0:P], xn[:, 0, :], idf[:]).then_inc(S["g_pT"], 1)
                    p.wait_ge(S["g_pE"], t + (1 + k * NT))
                    p.matmul(PS[:, 5, 0:D], xTt[:, 0, :], W[:], start=True, stop=True).then_inc(S["g_py"], 1)
            product(KEYS1)
            product(KEYS2)
            project(0, W1)
            product(CONV)
            project(1, Wg)
            product(GCN)
            p.wait_ge(S["g_hE"], NT)
            mamba_pe(p, NCH)
            project(2, W3)
            product(DIST)

        def general_scalar(s, ch):
            def product(m):
                with s.Fori(0, NT) as it:
                    asks = [sum(ASKS[:m]) * NT]
                    def asked():
                        asks[0] += 1
                        s.wait_ge(S["g_ask"], it * ASKS[m] + asks[0])
                    if m in (KEYS1, KEYS2):
                        asked()
                        s.activation(A1, A1, ACT.Exp, bias=tc[:, 1:2], accum_out=tc[:, 2:3]).then_inc(S["g_did"], 1)
                    if m == KEYS1:
                        asked()
                        s.activation(A0, A1, ACT.Square, accum_out=tc[:, 3:4]).then_inc(S["g_did"], 1)
                    if m == DIST:
                        asked()
                        s.activation(A1, A1, ACT.Square, bias=tc[:, 1:2]).then_inc(S["g_did"], 1)
                        asked()
                        s.activation(A1, A1, ACT.Exp, scale=-2.0).then_inc(S["g_did"], 1)
                    for g in range(8):
                        s.wait_ge(S["g_tr"], it * 8 + (8 * m * NT + g + 1))
                        s.activation(GT[:, g * BANK:(g + 1) * BANK], PS[:, 4 + g % 2, :], ACT.Copy).then_inc(S["g_trE"], 1)
                    if m != KEYS1:
                        asked()
                        s.activation(rstd[:, 0:1], mv[:, 1:2], ACT.Sqrt, bias=sc[:, 12:13]).then_inc(S["g_did"], 1)
                    if m == GCN:
                        s.wait_ge(S["g_hT"], it + 1)
                        s.activation(h2T[:, bass.ds(it * P + 3, P)], PS[:, 6, 0:P], ACT.Identity, scale=lng[:, 0:1], bias=lnb[:, 0:1]).then_inc(S["g_hE"], 1)

            def project(k):
                with s.Fori(0, NT) as t:
                    s.wait_ge(S["g_pT"], t + (1 + k * NT))
                    s.activation(xTt[:, 0, :], PS[:, 4, 0:P], ACT.Copy).then_inc(S["g_pE"], 1)
            product(KEYS1)
            product(KEYS2)
            s.wait_ge(S["g_fin"], 1)
            s.activation(dsc[:], dinv[:], ACT.Sqrt).then_inc(S["g_std"], 1)
            project(0)
            product(CONV)
            project(1)
            product(GCN)
            mamba_scalar(s, ch, NCH)
            project(2)
            product(DIST)

        def general_gpsimd(g):
            mamba_gpsimd(g, NCH)

        def general_vector(v, ct, norm):
            row = lambda ap, t: ap[:, bass.ds(t, 1), :].rearrange("p o d -> p (o d)")
            z = tb[:, 0:D]

            def product(m):
                asks = [0]
                with v.Fori(0, NT) as it:
                    one = lambda ap: ap[:, bass.ds(it, 1)]
                    base = sum(ASKS[:m]) * NT
                    ct.begin(it, STEPS[m])

                    def ask(ins):
                        asks[0] += 1
                        ins.then_inc(S["g_ask"], 1)
                        v.wait_ge(S["g_did"], it * ASKS[m] + (base + asks[0]))
                    loads = 2 if m == KEYS2 else 1
                    v.wait_ge(S["g_adj"], it * (16 * loads) + 16 * (loads + (m + (m > KEYS2)) * NT))
                    if m in (KEYS1, KEYS2):
                        if m == KEYS1:
                            ct(v.tensor_reduce(tc[:, 4:5], A0, AX_X, ALU.add))
                            passed(v)
                            ct(v.tensor_copy(one(deg), tc[:, 4:5]))
                        ct(v.tensor_scalar(A1, f2row[:, 0:N], f12[:, bass.ds(it, 1), 0], None, ALU.add))
                        ct(v.scalar_tensor_tensor(out=A1, in0=A1, scalar=ALPHA, in1=A1, op0=ALU.mult, op1=ALU.max))
                        ct(v.tensor_scalar(A0, A0, 0.0, NEG, ALU.is_le, ALU.mult))
                        ct(v.tensor_tensor(A1, A1, A0, ALU.add))
                        ct(v.tensor_reduce(tc[:, 0:1], A1, AX_X, ALU.max))
                        ask(v.tensor_scalar(tc[:, 1:2], tc[:, 0:1], -1.0, None, ALU.mult))
                        if m == KEYS1:
                            ask(v.tensor_copy(tc[:, 0:1], tc[:, 2:3]))
                        v.sem_inc(S["g_rows"], 1)
                    elif m == DIST:
                        ct(v.memset(tc[:, 1:2], -1.0))
                        ct(v.tensor_scalar(A1, A0, 0.0, 0.001, ALU.is_equal, ALU.mult))
                        ct(v.tensor_tensor(A1, A1, A0, ALU.add))
                        ct(v.reciprocal(A1, A1))
                        ask(v.tensor_scalar(A1, A1, -10000.0, 10000.0, ALU.max, ALU.min))
                        ask(v.tensor_copy(tc[:, 0:1], tc[:, 1:2]))
                        ct(v.scalar_tensor_tensor(out=A1, in0=A0, scalar=1.0, in1=A1, op0=ALU.is_lt, op1=ALU.mult))
                        v.sem_inc(S["g_rows"], 1)
                    else:
                        ct(v.memset(tc[:, 1:2], -1.0))
                        v.sem_inc(S["g_rows"], 1)
                    v.wait_ge(S["g_prod"], it + (1 + m * NT))
                    num = PS[:, 0, 0:D]
                    if m == KEYS1:
                        ct(v.reciprocal(tc[:, 4:5], tc[:, 2:3]))
                        passed(v)
                        ct(v.tensor_copy(one(rden), tc[:, 4:5]))
                        ct(v.tensor_scalar(tc[:, 5:6], tc[:, 3:4], tc[:, 4:5], 0.5, ALU.mult, ALU.mult))
                        ct(v.tensor_scalar(tc[:, 5:6], tc[:, 5:6], tc[:, 4:5], None, ALU.mult))
                        passed(v)
                        ct(v.tensor_copy(one(rsum), tc[:, 5:6]))
                        ct(v.tensor_tensor(tc[:, 6:7], sc[:, 22:23], tc[:, 5:6], ALU.subtract))
                        ct(v.tensor_scalar(z, row(xs, it), tc[:, 6:7], None, ALU.mult))
                        ct(v.scalar_tensor_tensor(out=z, in0=num, scalar=tc[:, 4:5], in1=z, op0=ALU.mult, op1=ALU.add))
                        ct(v.tensor_scalar(tb[:, D:2 * D], z, -THRESH, THRESH, ALU.max, ALU.min))
                        ct(v.tensor_tensor(row(feat, it), z, tb[:, D:2 * D], ALU.subtract))
                    elif m == KEYS2:
                        ct(v.reciprocal(tc[:, 4:5], tc[:, 2:3]))
                        ct(v.tensor_scalar(z, num, tc[:, 4:5], None, ALU.mult))
                        ct(v.scalar_tensor_tensor(out=tb[:, D:2 * D], in0=z, scalar=sc[:, 27:28], in1=row(feat, it), op0=ALU.mult, op1=ALU.add))
                        ct(v.scalar_tensor_tensor(out=z, in0=z, scalar=coe[:, 1:2], in1=row(xs, it), op0=ALU.mult, op1=ALU.add))
                        ct(v.scalar_tensor_tensor(out=z, in0=tb[:, D:2 * D], scalar=one(k2), in1=z, op0=ALU.mult, op1=ALU.add))
                        ct(v.scalar_tensor_tensor(out=z, in0=h0t[:, 0, :], scalar=sc[:, 26:27], in1=z, op0=ALU.mult, op1=ALU.add))
                    elif m == CONV:
                        ct(v.tensor_tensor(z, num, row(feat, it), ALU.add))
                        ct(v.scalar_tensor_tensor(out=z, in0=z, scalar=one(dinv), in1=row(xs, it), op0=ALU.mult, op1=ALU.add))
                        ct(v.tensor_tensor(z, z, b1row[:], ALU.add))
                    elif m == GCN:
                        ct(v.tensor_tensor(z, num, bgrow[:], ALU.add))
                        ct(v.tensor_scalar(z, z, 0.0, None, ALU.max))
                    else:
                        ct(v.tensor_tensor(z, num, row(xs, it), ALU.add))
                    if m != KEYS1:
                        ct(v.bn_stats(bn6[:], z))
                        passed(v)
                        ask(v.bn_aggr(mv[:], bn6[:]))
                        ct(v.reciprocal(rstd[:, 0:1], rstd[:, 0:1]))
                        dst = xn[:, 0, :] if m in (GCN, DIST) else row(xs, it)
                        ct(v.tensor_scalar(dst, z, mv[:, 0:1], rstd[:, 0:1], ALU.subtract, ALU.mult))
                    if m == GCN:
                        v.sem_inc(S["g_hx"], 1)
                        v.wait_ge(S["g_hE"], it + 1)
                    if m == DIST:
                        v.sem_inc(S["g_fin"], 1)
                        v.wait_ge(S["g_out"], it * 16 + 16)
                    passed(v)
                    v.sem_inc(S["g_end"], 1)
                    ct.end()
                ct.close(NT)

            def project(k, scale, bias):
                with v.Fori(0, NT) as t:
                    ct.begin(t, 2)
                    passed(v)
                    ct(v.tensor_copy(xn[:, 0, :], row(xs, t)))
                    v.sem_inc(S["g_px"], 1)
                    v.wait_ge(S["g_py"], t + (1 + k * NT))
                    if scale is not None:
                        ct(v.tensor_scalar(row(feat, t), PS[:, 5, 0:D], scale[:, bass.ds(t, 1)], None, ALU.mult))
                    elif bias is not None:
                        ct(v.tensor_tensor(row(feat, t), PS[:, 5, 0:D], bias, ALU.add))
                    else:
                        passed(v)
                        ct(v.tensor_copy(row(feat, t), PS[:, 5, 0:D]))
                    ct.end()
                ct.close(NT)
            v.wait_ge(S["g_in"], 64)
            v.sem_inc(S["g_end"], 1)
            product(KEYS1)
            ct.begin()
            ct(v.tensor_scalar(k2[:], rsum[:], coe[:, 1:2], sc[:, 25:26], ALU.mult, ALU.add))
            ct.end(); ct.close()
            product(KEYS2)
            ct.begin()
            v.tensor_scalar(dinv[:], deg[:], 1.0, None, ALU.add).then_inc(S["g_fin"], 1)
            v.wait_ge(S["g_std"], 1)
            ct(v.reciprocal(dinv[:], dsc[:]))
            ct.end(); ct.close()
            project(0, dinv, None)
            product(CONV)
            project(1, None, None)
            v.memset(h2T[:, 0:3], 0.0).then_inc(S["m_s0"], 1)
            v.memset(state[:], 0.0).then_inc(S["m_s0"], 1)
            product(GCN)
            mamba_vector(v, ct, NCH)
            project(2, None, b3row[:])
            product(DIST)

        block = ctx.enter_context(nc.Block())

        def tiles(eng, step, n=NT, lag=0):
            head = 4 if lag else 2
            for it in range(head):
                step(it, it % 2, it)
            with eng.Fori(head // 2, n // 2) as i:
                step(i * 2, 0, None)
                step(i * 2 + 1, 1, None)
            for it in range(n, n + lag):
                step(it, it % 2, it)

        @block.sync
        def _(q):
            q.dma_start(xs[:, :, :], A["x"].rearrange("(t p) d -> p t d", p=P)).then_inc(S["s_x"], 16)
            q.dma_start(acol[:], A["L0_gnn_a"].rearrange("(k d) o -> d (k o)", k=2)).then_inc(S["s_x"], 16)
            q.dma_start(adjt[:, 0, :], adj_rows[0]).then_inc(S["adj0"], 16)
            q.dma_start(adjt[:, 1, :], adj_rows[1]).then_inc(S["adj1"], 16)
            n_w = 0
            for dst, src in (
                (coe[:], A["L0_gnn_temp"].partition_broadcast(P)),
                (W1[:], A["L1_gnn_weight"]), (Wg[:], A["L2_gnn_gcn_w"]),
                (b1row[:], A["L1_gnn_bias"].partition_broadcast(P)),
                (bgrow[:], A["L2_gnn_gcn_b"].partition_broadcast(P)),
                (lng[:], A["L2_gnn_ln_g"].rearrange("(p o) -> p o", o=1)),
                (lnb[:], A["L2_gnn_ln_b"].rearrange("(p o) -> p o", o=1)),
                (win[:], A["L2_gnn_w_in"]),
                (cwrow, A["L2_gnn_conv_w"].rearrange("e k -> (e k)").partition_broadcast(P)),
                (convb[:], A["L2_gnn_conv_b"].rearrange("(h p) -> p h", p=P)),
                (wxp[:], A["L2_gnn_w_xp"].rearrange("(h p) n -> p h n", p=P)),
                (wdt[:], A["L2_gnn_w_dt"]),
                (bdt[:], A["L2_gnn_b_dt"].rearrange("(h p) -> p h", p=P)),
                (Aneg[:], A["L2_gnn_A_log"].rearrange("(h p) n -> p h n", p=P)),
                (dskip[:], A["L2_gnn_D_skip"].rearrange("(h p) -> p h", p=P)),
                (wout[:], A["L2_gnn_w_out"].rearrange("(h p) n -> p h n", p=P)),
            ):
                q.dma_start(dst, src).then_inc(S["s_w"], 16)
                n_w += 1

            q.wait_ge(S["s_fc"], 8)
            q.dma_start(f2d, f2row[0:1, 0:N]).then_inc(S["s_f2d"], 16)
            def step(it, par, static):
                q.wait_ge(S["a_s1E"], 4 * (it + 1))
                passed(q)
                q.dma_start(stS[bass.ds(it, 1)].rearrange("o p n -> (o p) n"), s1T[:, par, :].bitcast(U8)).then_inc(S[f"a_stS{par}"], 16)
                q.dma_start(stM[bass.ds(it, 1)].rearrange("o p n -> (o p) n"), mT[:, par, :].bitcast(U8)).then_inc(S[f"a_stM{par}"], 16)
                if static is None or static < NT - 2:
                    q.wait_ge(S["a_s1"], it + 1)
                    passed(q)
                    q.dma_start(adjt[:, par, :], adj_rows[bass.ds(it + 2, 1)].rearrange("o p n -> (o p) n")).then_inc(S[f"adj{par}"], 16)
            step(0, 0, 0)
            step(1, 1, 1)
            with q.Fori(1, NT // 2 - 1) as i:
                step(i * 2, 0, None)
                step(i * 2 + 1, 1, None)
            step(NT - 2, 0, NT - 2)
            step(NT - 1, 1, NT - 1)
            for par in range(2):
                q.wait_ge(S[f"a_stS{par}"], 16 * NT // 2)
                q.wait_ge(S[f"a_stM{par}"], 16 * NT // 2)

            def step(it, par, static):
                if static == 0:
                    q.wait_ge(S["a_prod"], NT)
                    q.wait_ge(S["a_s2"], NT)
                elif static == 1:
                    pass
                else:
                    q.wait_ge(S["b_prod"], it - 1)
                passed(q)
                q.dma_start(s1T[:, par, :].bitcast(U8), stS[bass.ds(it, 1)].rearrange("o p n -> (o p) n")).then_inc(S[f"b_ldS{par}"], 16)
                q.dma_start(mT[:, par, :].bitcast(U8), stM[bass.ds(it, 1)].rearrange("o p n -> (o p) n")).then_inc(S[f"b_ldM{par}"], 16)
                if static is None or static >= 2:
                    q.wait_ge(S["b_x1"], it - 1)
                passed(q)
                q.dma_start(h0t[:, par, :], h0_rows[bass.ds(it, 1)].rearrange("o p d -> (o p) d")).then_inc(S[f"b_h{par}"], 16)
            tiles(q, step)

            for st, prev in (("c", "b"), ("d", "c")):
                def step(it, par, static):
                    if static == 0:
                        q.wait_ge(S[prev + "_prod"], NT)
                    elif static != 1:
                        q.wait_ge(S[st + "_prod"], it - 1)
                    passed(q)
                    q.dma_start(mT[:, par, :].bitcast(U8), stM[bass.ds(it, 1)].rearrange("o p n -> (o p) n")).then_inc(S[f"{st}_ldM{par}"], 16)
                tiles(q, step)

            mamba_sync(q, 0)
            q.wait_ge(S["m_out"], CR["m_out"] + 16 * NCH)
            q.wait_ge(S["s_f2d"], 16)
            if_general(q, general_sync)

        @block.tensor
        def _(p):
            p.wait_ge(S["s_id"], 4)
            p.wait_ge(S["s_x"], 32)
            for t in range(NT):
                g = t // 4
                if t % 4 == 0 and g >= 2:
                    p.wait_ge(S["s_xT"], g - 1)
                ins = p.transpose(PS[:, g % 2, (t % 4) * P:(t % 4 + 1) * P], xs[:, t, :], idf[:])
                if t % 4 == 3:
                    ins.then_inc(S["s_tr0"], 1)
            p.wait_ge(S["s_xT"], NT // 4)
            p.wait_ge(S["s_col"], 1)
            for b in range(8):
                ins = p.matmul(PS[:, b, :], a2rep[:], xT[:, b * BANK:(b + 1) * BANK], start=True, stop=True)
                ins.then_inc(S["s_f"], 1)
            p.wait_ge(S["s_fc"], 8)
            for t in range(NT):
                ins = p.matmul(PS[:, 0, 2 * t:2 * t + 2], xT[:, t * P:(t + 1) * P], acol[:], start=True, stop=True)
            ins.then_inc(S["s_f"], 1)
            p.wait_ge(S["p_w"], 1)
            p.matmul(PS[:, 1, 0:2 * D], ones[:], tb[:, 0:2 * D], start=True, stop=True).then_inc(S["s_f"], 1)

            p.wait_ge(S["s_y0"], 1)
            def step(it, par, static):
                if static is None or static < NT:
                    p.wait_ge(S[f"adj{par}"], 16 * (it // 2 + 1) if static is not None else 16 * (it - par) // 2 + 16)
                    for g in range(8):
                        if static != 0 or g >= 2:
                            p.wait_ge(S["a_adjE"], 8 * it + g - 1)
                        for k in range(4):
                            j = 4 * g + k
                            ins = p.transpose(PS[:, 4 + g % 2, k * P:(k + 1) * P], adjt[:, par, j * P:(j + 1) * P], idf[:])
                        ins.then_inc(S["a_adjT"], 1)
                    p.wait_ge(S["a_s1"], it + 1)
                    for g in range(4):
                        if static != 0 or g >= 2:
                            p.wait_ge(S["a_s1E"], 4 * it + g - 1)
                        bank = PS[:, 6 + g % 2, :].bitcast(BF16)
                        for k in range(8):
                            j = 8 * g + k
                            ins = p.transpose(bank[:, k * P:(k + 1) * P], s1r[:, par, j * P:(j + 1) * P], idb[:])
                        ins.then_inc(S["a_s1Tp"], 1)
                if static is None or static >= 1:
                    op = 1 - par
                    p.wait_ge(S["a_s1E"], 4 * it)
                    if static is None or static >= 3:
                        p.wait_ge(S["a_tail"], it - 2)
                    passed(p)
                    for j in range(NT):
                        p.matmul(PS[:, 2 * op, 0:2 * COLS], s1T[:, op, j * P:(j + 1) * P], y1[:, j, :], start=(j == 0), stop=(j == NT - 1))
                    p.wait_ge(S["a_s2"], it)
                    passed(p)
                    for j in range(NT):
                        ins = p.matmul(PS[:, 2 * op + 1, 0:2 * COLS], s2T[:, op, j * P:(j + 1) * P], y2[:, j, :], start=(j == 0), stop=(j == NT - 1))
                    ins.then_inc(S["a_prod"], 1)
            tiles(p, step, lag=1)

            def step(it, par, static):
                if static == 0:
                    p.wait_ge(S["a_spl"], NT)
                    p.wait_ge(S["a_low"], NT)
                if static is None or static < NT:
                    p.wait_ge(S[f"b_ldS{par}"], (it - par) * 8 + 16)
                    if static is None or static >= 2:
                        p.wait_ge(S["b_tail"], it - 1)
                    passed(p)
                    for j in range(NT):
                        p.matmul(PS[:, 2 * par, 0:2 * D], s1T[:, par, j * P:(j + 1) * P], y1b[:, j, :], start=(j == 0), stop=(j == NT - 1))
                    p.wait_ge(S["b_s2"], it + 1)
                    passed(p)
                    for j in range(NT):
                        ins = p.matmul(PS[:, 2 * par + 1, 0:2 * D], s2T[:, par, j * P:(j + 1) * P], y2b[:, j, :], start=(j == 0), stop=(j == NT - 1))
                    ins.then_inc(S["b_prod"], 1)
                if static is None or static >= 2:
                    project("b", W1, it - 2, par)
            def project(st, W, t, par):
                p.wait_ge(S[st + "_x1" if st == "b" else st + "_x"], t + 1)
                if st == "d" and t is not None:
                    p.wait_ge(S["d_xTe"], t)
                p.transpose(PS[:, 4, 0:P], xn[:, par, :], idf[:]).then_inc(S[st + "_xTp"], 1)
                if W is not None:
                    p.wait_ge(S[st + "_xTe"], t + 1)
                    p.wait_ge(S[st + "_low"], t)
                    p.matmul(PS[:, 5, 0:D], xTt[:, par, :], W[:], start=True, stop=True).then_inc(S[st + "_y"], 1)
            tiles(p, step, lag=2)

            for st, W, y, prev in (("c", Wg, y1, "b"), ("d", None, y2, "c")):
                def step(it, par, static):
                    if static == 0:
                        p.wait_ge(S[prev + "_hi"], NT)
                        p.wait_ge(S[prev + "_low"], NT)
                    if static is None or static < NT:
                        p.wait_ge(S[f"{st}_ldM{par}"], (it - par) * 8 + 16)
                        if static is None or static >= 2:
                            p.wait_ge(S[st + "_x"], it - 1)
                        passed(p)
                        for j in range(NT):
                            ins = p.matmul(PS[:, par, 0:2 * D], mT[:, par, j * P:(j + 1) * P], y[:, j, 0:2 * D], start=(j == 0), stop=(j == NT - 1))
                        ins.then_inc(S[st + "_prod"], 1)
                    if static is None or static >= 2:
                        project(st, W, it - 2, par)
                tiles(p, step, lag=2)
            p.wait_ge(S["d_xTe"], NT)
            mamba_pe(p, 0)
            if_general(p, general_pe)

        @block.gpsimd
        def _(g):
            g.memset(idf[:], 0.0).then_inc(S["s_id"], 1)
            g.memset(idb[:], 0.0).then_inc(S["s_id"], 1)
            g.wait_ge(S["s_id"], 2)
            for m in (idf, idb):
                g.affine_select(out=m[:], in_=m[:], compare_op=ALU.not_equal, fill=1.0, base=0, pattern=[[-1, P]], channel_multiplier=1).then_inc(S["s_id"], 1)
            g.wait_ge(S["s_red"], 1)
            g.partition_all_reduce(stat[:], red[:], P, RMAX).then_inc(S["s_red"], 1)
            def step(it, par, static):
                g.wait_ge(S["a_s1E"], 4 * it + 4)
                if static is None or static >= 2:
                    g.wait_ge(S["a_prod"], it - 1)
                passed(g)
                g.tensor_tensor(s2T[:, par, :], mT[:, par, :], s1T[:, par, :], ALU.subtract, saturate=False).then_inc(S["a_s2"], 1)
            tiles(g, step)
            g.wait_ge(S["s_red"], 3)
            g.partition_all_reduce(stat[:], red[:], P, RMAX).then_inc(S["s_red"], 1)
            for st, x in (("b", "b_x1"), ("c", "c_x")):
                def step(it, par, static):
                    g.wait_ge(S[x], it + 1)
                    g.tensor_copy(xs[:, bass.ds(it, 1), :].rearrange("p o d -> p (o d)"), xn[:, par, :]).then_inc(S[st + "_cp"], 1)
                tiles(g, step)
            mamba_gpsimd(g, 0)
            if_general(g, general_gpsimd)

        @block.scalar
        def _(s):
            ch = Chain(s, S["a_chain"])
            for g in range(8):
                s.wait_ge(S["s_tr0"], g + 1)
                s.activation(xT[:, g * BANK:(g + 1) * BANK], PS[:, g % 2, :], ACT.Copy).then_inc(S["s_xT"], 1)
            for b in range(8):
                s.wait_ge(S["s_f"], b + 1)
                s.activation(f2row[:, b * BANK:(b + 1) * BANK], PS[:, b, :], ACT.Copy).then_inc(S["s_fc"], 1)
            s.wait_ge(S["s_w"], 16 * 16)
            ch.begin()
            ch(s.activation(coe[:], coe[:], ACT.Sigmoid))
            ch(s.activation(Aneg[:], Aneg[:], ACT.Exp))
            ch(s.activation(Aneg[:], Aneg[:], ACT.Copy, scale=-1.0))
            s.wait_ge(S["s_ex"], 1)
            s.activation(EE[:, 0, :], f12[:, :, 1], ACT.Exp, bias=sc[:, 0:1])
            s.activation(EE[:, 1, :], f12[:, :, 1], ACT.Exp, bias=sc[:, 1:2], scale=ALPHA)
            s.activation(Ea[:], Ea2[:], ACT.Exp)
            s.activation(Eb[:], Eb2[:], ACT.Exp)
            ch(s.activation(sc[:, 8:10], sc[:, 6:8], ACT.Sqrt))
            s.sem_inc(S["s_exd"], 1)
            s.wait_ge(S["s_y0a"], 1)
            for t in range(NT):
                s.activation(y1[:, t, 0:D], xs[:, t, :], ACT.Copy, scale=Es[:, 0, t:t + 1])
                ins = s.activation(y2[:, t, 0:D], xs[:, t, :], ACT.Copy, scale=Es[:, 1, t:t + 1])
                ins.then_inc(S["s_init"], 1)
            ch.end(); ch.close()

            def step(it, par, static):
                if static is None or static < NT:
                    for g in range(8):
                        s.wait_ge(S["a_adjT"], 8 * it + g + 1)
                        if g == 0 and (static is None or static >= 2):
                            s.wait_ge(S[f"a_stM{par}"], (it - par) * 8)
                            s.wait_ge(S["a_s2"], it - 1)
                        passed(s)
                        s.activation(mT[:, par, g * BANK:(g + 1) * BANK], PS[:, 4 + g % 2, :], ACT.Copy, saturate=False).then_inc(S["a_adjE"], 1)
                    for g in range(4):
                        s.wait_ge(S["a_s1Tp"], 4 * it + g + 1)
                        if g == 0 and (static is None or static >= 2):
                            s.wait_ge(S[f"a_stS{par}"], (it - par) * 8)
                            s.wait_ge(S["a_prod"], it - 1)
                        passed(s)
                        s.activation(s1T[:, par, g * 1024:(g + 1) * 1024], PS[:, 6 + g % 2, :].bitcast(BF16), ACT.Copy, saturate=False).then_inc(S["a_s1E"], 1)
                if static is None or static >= 2:
                    t = it - 2
                    s.wait_ge(S["a_prod"], it - 1)
                    if static is None or static >= 4:
                        s.wait_ge(S["a_tail"], it - 3)
                    s.activation(ta[:, par, :], PS[:, 2 * par, 0:2 * COLS], ACT.Copy, scale=Ea[:, bass.ds(t, 1)]).then_inc(S["a_ta"], 1)
                    s.wait_ge(S["a_feat"], it - 1)
                    f = feat[:, bass.ds(t, 1), :].rearrange("p o d -> p (o d)")
                    s.activation(y1b[:, bass.ds(t, 1), 0:D].rearrange("p o d -> p (o d)"), f, ACT.Copy, scale=Es2[:, 0, bass.ds(t, 1)])
                    s.activation(y2b[:, bass.ds(t, 1), 0:D].rearrange("p o d -> p (o d)"), f, ACT.Copy, scale=Es2[:, 1, bass.ds(t, 1)]).then_inc(S["a_spl"], 1)
            tiles(s, step, lag=2)

            s.wait_ge(S["s_ex"], 2)
            s.activation(dsc[:], dinv[:], ACT.Sqrt).then_inc(S["s_exd"], 1)

            def rstd_step(st, t, par):
                s.wait_ge(S[st + "_var"], t + 1)
                s.activation(rstd[:, par:par + 1], mv[:, 1:2], ACT.Sqrt, bias=sc[:, 12:13]).then_inc(S[st + "_std"], 1)

            def evac_xT(st, t, par, scale):
                s.wait_ge(S[st + "_xTp"], t + 1)
                s.activation(xTt[:, par, :], PS[:, 4, 0:P], ACT.Copy).then_inc(S[st + "_xTe"], 1)
                s.wait_ge(S[st + "_y"], t + 1)

            def step(it, par, static):
                if static is None or static < NT:
                    s.wait_ge(S["b_prod"], it + 1)
                    if static is None or static >= 2:
                        s.wait_ge(S["b_tail"], it - 1)
                    s.activation(ta[:, par, 0:2 * D], PS[:, 2 * par, 0:2 * D], ACT.Copy, scale=g1[:, bass.ds(it, 1)]).then_inc(S["b_ta"], 1)
                    rstd_step("b", it, par)
                if static is None or static >= 2:
                    t, op = it - 2, par
                    evac_xT("b", t, op, None)
                    s.activation(y1[:, bass.ds(t, 1), 0:D].rearrange("p o d -> p (o d)"), PS[:, 5, 0:D], ACT.Copy, scale=dsc[:, bass.ds(t, 1)]).then_inc(S["b_hi"], 1)
            tiles(s, step, lag=2)

            def step(it, par, static):
                if static is None or static < NT:
                    s.wait_ge(S["c_prod"], it + 1)
                    if static is None or static >= 2:
                        s.wait_ge(S["c_x"], it - 1)
                    s.activation(ta[:, par, 0:D], PS[:, par, D:2 * D], ACT.Copy).then_inc(S["c_ta"], 1)
                    rstd_step("c", it, par)
                if static is None or static >= 2:
                    t, op = it - 2, par
                    evac_xT("c", t, op, None)
                    s.activation(y2[:, bass.ds(t, 1), 0:D].rearrange("p o d -> p (o d)"), PS[:, 5, 0:D], ACT.Copy, scale=sc[:, 11:12]).then_inc(S["c_hi"], 1)
            tiles(s, step, lag=2)

            def step(it, par, static):
                if static is None or static < NT:
                    s.wait_ge(S["d_prod"], it + 1)
                    if static is None or static >= 2:
                        s.wait_ge(S["d_x"], it - 1)
                    s.activation(ta[:, par, 0:D], PS[:, par, D:2 * D], ACT.Copy, scale=sc[:, 13:14]).then_inc(S["d_ta"], 1)
                    rstd_step("d", it, par)
                if static is None or static >= 2:
                    t = it - 2
                    s.wait_ge(S["d_xTp"], t + 1)
                    s.activation(h2T[:, bass.ds(t * P + 3, P)], PS[:, 4, 0:P], ACT.Identity, scale=lng[:, 0:1], bias=lnb[:, 0:1]).then_inc(S["d_xTe"], 1)
            tiles(s, step, lag=2)
            mamba_scalar(s, ch, 0)
            if_general(s, lambda q: general_scalar(q, ch))

        @block.vector
        def _(v):
            ch = Chain(v, S["v_chain"])
            ch.begin()
            ch(v.memset(ones[:], 1.0))
            v.wait_ge(S["s_x"], 32)
            v.tensor_scalar(a2rep[:], ones[:], acol[:, 1:2], None, ALU.mult).then_inc(S["s_col"], 1)
            ch(v.tensor_reduce(red[:, 2:3], xs[:, :, :].rearrange("p t d -> p (t d)"), AX_X, ALU.max))
            ch(v.tensor_reduce(red[:, 3:4], xs[:, :, :].rearrange("p t d -> p (t d)"), AX_X, ALU.min))
            ch(v.tensor_scalar(red[:, 3:4], red[:, 3:4], -1.0, None, ALU.mult))
            ch(v.tensor_tensor(red[:, 2:3], red[:, 2:3], red[:, 3:4], ALU.max))
            v.wait_ge(S["s_w"], 16 * 16)
            ch(v.tensor_tensor(wtap[:, :, :], cwrow.rearrange("p (e k) -> p k e", k=KC),
                               win[:, 0:DI].unsqueeze(1).broadcast_to([P, KC, DI]), ALU.mult))
            ch(v.tensor_tensor(tb[:, 0:D], W1[:], W1[:], ALU.mult))
            v.tensor_tensor(tb[:, D:2 * D], Wg[:], Wg[:], ALU.mult).then_inc(S["p_w"], 1)
            v.wait_ge(S["s_f"], 9)
            ch(v.tensor_copy(f12[:, :, :].rearrange("p t k -> p (t k)"), PS[:, 0, 0:2 * NT]))
            v.wait_ge(S["s_f"], 10)
            ch(v.tensor_reduce(sc[:, 6:8], PS[:, 1, 0:2 * D].rearrange("p (k d) -> p k d", k=2), AX_X, ALU.max))
            ch(v.tensor_scalar(nf1[:], f12[:, :, 0], -1.0, None, ALU.mult))
            ch(v.tensor_reduce(red[:, 0:1], f12[:, :, 1], AX_X, ALU.max))
            ch(v.tensor_reduce(red[:, 1:2], f12[:, :, 1], AX_X, ALU.min))
            v.tensor_scalar(red[:, 1:2], red[:, 1:2], -1.0, None, ALU.mult).then_inc(S["s_red"], 1)
            v.wait_ge(S["s_red"], 2)
            ch(v.tensor_scalar(sc[:, 0:1], stat[:, 0:1], -1.0, None, ALU.mult))
            ch(v.tensor_scalar(sc[:, 1:2], stat[:, 0:1], -ALPHA, None, ALU.mult))
            ch(v.tensor_tensor(sc[:, 14:15], stat[:, 0:1], stat[:, 1:2], ALU.add))
            ch(v.tensor_scalar(sc[:, 2:3], stat[:, 2:3], 1e-30, 1.0 / HALFMAX, ALU.max, ALU.mult))
            ch(v.reciprocal(sc[:, 3:4], sc[:, 2:3]))
            ch(v.tensor_scalar(sc[:, 4:5], sc[:, 2:3], SUMSCALE, None, ALU.mult))
            ch(v.tensor_scalar(sc[:, 5:6], sc[:, 2:3], SUMSCALE * 2.0, None, ALU.mult))
            ch(v.tensor_scalar(Ea[:], f12[:, :, 0], stat[:, 0:1], None, ALU.add))
            ch(v.tensor_scalar(Ea2[:], Ea[:], 1.0 - ALPHA, 0.0, ALU.mult, ALU.min))
            ch(v.tensor_scalar(Eb2[:], Ea[:], ALPHA - 1.0, 0.0, ALU.mult, ALU.min))
            v.memset(sc[:, 12:13], EPS).then_inc(S["s_ex"], 1)
            v.wait_ge(S["s_exd"], 1)
            ch(v.tensor_scalar(Es[:], EE[:], sc[:, 3:4], None, ALU.mult))
            v.tensor_scalar(Es2[:], EE[:], sc[:, 3:4], 0.5, ALU.mult, ALU.mult).then_inc(S["s_y0a"], 1)
            ch(v.tensor_tensor(Ea2[:], Ea[:], Ea[:], ALU.mult))
            ch(v.tensor_tensor(Eb2[:], Eb[:], Eb[:], ALU.mult))
            ch(v.tensor_tensor(EE2[:], EE[:], EE[:], ALU.mult))
            ch(v.tensor_scalar(sc[:, 8:10], sc[:, 8:10], 1e-30, ROWNORM / HALFMAX, ALU.max, ALU.mult))
            ch(v.reciprocal(sc[:, 10:12], sc[:, 8:10]))
            ch(v.tensor_copy(sc[:, 13:14], sc[:, 9:10]))
            ch(v.tensor_scalar(sc[:, 20:25], coe[:, 0:5], -1.0, 1.0, ALU.mult, ALU.add))
            ch(v.tensor_tensor(sc[:, 25:26], sc[:, 21:22], coe[:, 0:1], ALU.mult))
            ch(v.tensor_tensor(sc[:, 26:27], sc[:, 21:22], sc[:, 20:21], ALU.mult))
            ch(v.tensor_scalar(sc[:, 27:28], coe[:, 3:4], -1.0, None, ALU.mult))
            for y, k in ((y1, 0), (y2, 1)):
                for c, E in ((D, EE), (D + 1, EE2)):
                    ch(v.tensor_scalar(y[:, :, c], E[:, k, :], SUMSCALE, None, ALU.mult))
                    ch(v.scalar_tensor_tensor(out=y[:, :, COLS + c], in0=E[:, k, :], scalar=SUMSCALE, in1=y[:, :, c], op0=ALU.mult, op1=ALU.subtract))
                ch(v.memset(y[:, :, D + 2], 1.0))
                ch(v.memset(y[:, :, COLS + D + 2], 0.0))
            for t in range(NT):
                v.wait_ge(S["s_init"], t + 1)
                v.scalar_tensor_tensor(out=y1[:, t, COLS:COLS + D], in0=xs[:, t, :], scalar=Es[:, 0, t:t + 1], in1=y1[:, t, 0:D], op0=ALU.mult, op1=ALU.subtract)
                ins = v.scalar_tensor_tensor(out=y2[:, t, COLS:COLS + D], in0=xs[:, t, :], scalar=Es[:, 1, t:t + 1], in1=y2[:, t, 0:D], op0=ALU.mult, op1=ALU.subtract)
            ins.then_inc(S["s_y0"], 1)
            ch.end(); ch.close()

            ct = Chain(v, S["g_chain"])
            def row(ap, t):
                return ap[:, bass.ds(t, 1), :].rearrange("p o d -> p (o d)")
            def step(it, par, static):
                if static is None or static < NT:
                    ch.begin(it)
                    v.wait_ge(S[f"adj{par}"], (it - par) * 8 + 16)
                    if static is None or static >= 2:
                        v.wait_ge(S["a_s1Tp"], 4 * (it - 1))
                    ch(v.scalar_tensor_tensor(out=s1r[:, par, :], in0=adjt[:, par, :], scalar=0.0, in1=adjt[:, par, :],
                                              op0=ALU.is_gt, op1=ALU.not_equal, accum_out=cnt[:, bass.ds(it, 1)]))
                    v.scalar_tensor_tensor(out=s1r[:, par, :], in0=f2row[:, 0:N], scalar=nf1[:, bass.ds(it, 1)], in1=adjt[:, par, :],
                                           op0=ALU.is_gt, op1=ALU.mult).then_inc(S["a_s1"], 1)
                    ch.end()
                if static is None or static >= 2:
                    t = it - 2
                    one = lambda ap: ap[:, bass.ds(t, 1)]
                    ct.begin(t)
                    Bq = PS[:, 2 * par + 1, 0:2 * COLS]
                    v.wait_ge(S["a_ta"], it - 1)
                    taq = ta[:, par, :]
                    sq = slice(D + 1, D + 2 + COLS, COLS)
                    ct(v.scalar_tensor_tensor(out=tb[:], in0=Bq, scalar=one(Eb), in1=taq, op0=ALU.mult, op1=ALU.add))
                    ct(v.tensor_scalar(tc[:, 0:2], taq[:, sq], one(Ea), None, ALU.mult))
                    ct(v.scalar_tensor_tensor(out=tc[:, 2:4], in0=Bq[:, sq], scalar=one(Eb2), in1=tc[:, 0:2], op0=ALU.mult, op1=ALU.add))
                    ct(v.tensor_copy(tc[:, 6:7], Bq[:, D + 2:D + 3]))
                    ct(v.tensor_tensor(one(deg), PS[:, 2 * par, D + 2:D + 3], tc[:, 6:7], ALU.add))
                    ct(v.tensor_tensor(tc[:, 4:5], tc[:, 2:3], tc[:, 3:4], ALU.add))
                    v.sem_inc(S["a_tail"], 1)
                    ct(v.tensor_tensor(tc[:, 8:8 + D + 1], tb[:, 0:D + 1], tb[:, COLS:COLS + D + 1], ALU.add))
                    ct(v.reciprocal(one(rden), tc[:, 8 + D:9 + D]))
                    ct(v.tensor_scalar(tc[:, 5:6], tc[:, 4:5], one(rden), 0.5 * SUMSCALE, ALU.mult, ALU.mult))
                    ct(v.tensor_scalar(one(rsum), tc[:, 5:6], one(rden), None, ALU.mult))
                    ct(v.tensor_tensor(tc[:, 4:5], sc[:, 22:23], one(rsum), ALU.subtract))
                    ct(v.tensor_tensor(tc[:, 5:6], sc[:, 4:5], one(rden), ALU.mult))
                    ct(v.tensor_scalar(tb[:, 0:D], row(xs, t), tc[:, 4:5], None, ALU.mult))
                    ct(v.scalar_tensor_tensor(out=tb[:, 0:D], in0=tc[:, 8:8 + D], scalar=tc[:, 5:6], in1=tb[:, 0:D], op0=ALU.mult, op1=ALU.add))
                    ct(v.tensor_scalar(tb[:, D:2 * D], tb[:, 0:D], -THRESH, THRESH, ALU.max, ALU.min))
                    v.tensor_tensor(row(feat, t), tb[:, 0:D], tb[:, D:2 * D], ALU.subtract).then_inc(S["a_feat"], 1)
                    v.wait_ge(S["a_spl"], it - 1)
                    for k, y in ((0, y1b), (1, y2b)):
                        ct(v.scalar_tensor_tensor(out=y[:, bass.ds(t, 1), D:2 * D].rearrange("p o d -> p (o d)"), in0=row(feat, t), scalar=Es2[:, k, bass.ds(t, 1)],
                                                  in1=y[:, bass.ds(t, 1), 0:D].rearrange("p o d -> p (o d)"), op0=ALU.mult, op1=ALU.subtract))
                    v.sem_inc(S["a_low"], 1)
                    ct.end()
            tiles(v, step, lag=2)
            ch.close(NT); ct.close(NT)

            ct.begin()
            ct(v.tensor_reduce(red[:, 0:1], cnt[:], AX_X, ALU.add))
            ct(v.tensor_reduce(red[:, 1:2], deg[:], AX_X, ALU.min))
            ct(v.tensor_scalar(red[:, 1:2], red[:, 1:2], 0.5, None, ALU.is_lt))
            ct(v.tensor_scalar(red[:, 2:3], sc[:, 14:15], SPREAD, None, ALU.is_gt))
            v.tensor_tensor(red[:, 3:4], red[:, 1:2], red[:, 2:3], ALU.max).then_inc(S["s_red"], 1)
            v.wait_ge(S["s_red"], 4)
            ct(v.tensor_tensor(stat[:, 0:1], stat[:, 0:1], stat[:, 3:4], ALU.max))
            v.tensor_scalar(flag[:], stat[:, 0:1], 0.5, None, ALU.is_gt).then_inc(S["s_flag"], 1)
            ct(v.tensor_scalar(g1[:], rden[:], sc[:, 5:6], None, ALU.mult))
            ct(v.tensor_tensor(g2[:], g1[:], Eb[:], ALU.mult))
            ct(v.tensor_tensor(g1[:], g1[:], Ea[:], ALU.mult))
            ct(v.tensor_scalar(k2[:], rsum[:], coe[:, 1:2], sc[:, 25:26], ALU.mult, ALU.add))
            ct(v.tensor_scalar(dinv[:], deg[:], 1.0, None, ALU.add))
            v.sem_inc(S["s_ex"], 1)
            v.wait_ge(S["s_exd"], 2)
            ct(v.reciprocal(dinv[:], dsc[:]))
            ct(v.tensor_scalar(dsc[:], dinv[:], sc[:, 10:11], None, ALU.mult))
            ct(v.tensor_scalar(deg[:], dinv[:], sc[:, 8:9], None, ALU.mult))
            v.sem_inc(S["s_ex"], 1)
            ct.end(); ct.close()

            def norm(st, z, dst, par, inc):
                ct(v.bn_stats(bn6[:], z))
                passed(v)
                v.bn_aggr(mv[:], bn6[:]).then_inc(S[st + "_var"], 1)
                v.wait_ge(S[st + "_std"], inc)
                ct(v.reciprocal(rstd[:, par:par + 1], rstd[:, par:par + 1]))
                return v.tensor_scalar(dst, z, mv[:, 0:1], rstd[:, par:par + 1], ALU.subtract, ALU.mult)

            def stepB(it, par, static):
                one = lambda ap: ap[:, bass.ds(it, 1)]
                if static is None or static < NT:
                    masks(it, par, static)
                    ct.begin(it)
                    v.wait_ge(S["b_ta"], it + 1)
                    ct(v.scalar_tensor_tensor(out=tb[:, 0:2 * D], in0=PS[:, 2 * par + 1, 0:2 * D], scalar=one(g2), in1=ta[:, par, 0:2 * D], op0=ALU.mult, op1=ALU.add))
                    v.sem_inc(S["b_tail"], 1)
                    ct(v.tensor_tensor(tb[:, 0:D], tb[:, 0:D], tb[:, D:2 * D], ALU.add))
                    ct(v.scalar_tensor_tensor(out=tb[:, D:2 * D], in0=tb[:, 0:D], scalar=sc[:, 27:28], in1=row(feat, it), op0=ALU.mult, op1=ALU.add))
                    ct(v.scalar_tensor_tensor(out=tb[:, 0:D], in0=tb[:, 0:D], scalar=coe[:, 1:2], in1=row(xs, it), op0=ALU.mult, op1=ALU.add))
                    ct(v.scalar_tensor_tensor(out=tb[:, 0:D], in0=tb[:, D:2 * D], scalar=one(k2), in1=tb[:, 0:D], op0=ALU.mult, op1=ALU.add))
                    v.wait_ge(S[f"b_h{par}"], (it - par) * 8 + 16)
                    ct(v.scalar_tensor_tensor(out=tb[:, 0:D], in0=h0t[:, par, :], scalar=sc[:, 26:27], in1=tb[:, 0:D], op0=ALU.mult, op1=ALU.add))
                    if static is None or static >= 2:
                        v.wait_ge(S["b_xTp"], it - 1)
                        v.wait_ge(S["b_cp"], it - 1)
                    norm("b", tb[:, 0:D], xn[:, par, :], par, it + 1).then_inc(S["b_x1"], 1)
                    v.wait_ge(S["b_x1"], it + 1)
                    ct.end()
                if static is None or static >= 2:
                    lowpart("b", y1, feat, dsc, it - 2)
            def masks(it, par, static):
                v.wait_ge(S[f"b_ldS{par}"], (it - par) * 8 + 16)
                v.wait_ge(S[f"b_ldM{par}"], (it - par) * 8 + 16)
                if static is None or static >= 2:
                    v.wait_ge(S["b_prod"], it - 1)
                passed(v)
                v.tensor_tensor(s2T[:, par, :], mT[:, par, :], s1T[:, par, :], ALU.subtract, saturate=False).then_inc(S["b_s2"], 1)

            def lowpart(st, y, keep, scale, t):
                v.wait_ge(S[st + "_hi"], t + 1)
                sca = scale[:, bass.ds(t, 1)] if keep is not None else scale
                hi = y[:, bass.ds(t, 1), 0:D].rearrange("p o d -> p (o d)")
                low = y[:, bass.ds(t, 1), D:2 * D].rearrange("p o d -> p (o d)")
                if keep is not None:
                    v.tensor_scalar(row(keep, t), PS[:, 5, 0:D], sca, None, ALU.mult)
                v.scalar_tensor_tensor(out=low, in0=PS[:, 5, 0:D], scalar=sca, in1=hi, op0=ALU.mult, op1=ALU.subtract).then_inc(S[st + "_low"], 1)
            tiles(v, stepB, lag=2)
            ct.close(NT)

            def stepC(it, par, static):
                if static is None or static < NT:
                    ct.begin(it)
                    if static == 0:
                        v.wait_ge(S["b_cp"], NT)
                    v.wait_ge(S["c_ta"], it + 1)
                    ct(v.tensor_tensor(tb[:, 0:D], ta[:, par, 0:D], row(feat, it), ALU.add))
                    ct(v.tensor_tensor(tb[:, 0:D], PS[:, par, 0:D], tb[:, 0:D], ALU.add))
                    ct(v.scalar_tensor_tensor(out=tb[:, 0:D], in0=tb[:, 0:D], scalar=deg[:, bass.ds(it, 1)], in1=row(xs, it), op0=ALU.mult, op1=ALU.add))
                    ct(v.tensor_tensor(tb[:, 0:D], tb[:, 0:D], b1row[:], ALU.add))
                    if static is None or static >= 2:
                        v.wait_ge(S["c_xTp"], it - 1)
                        v.wait_ge(S["c_cp"], it - 1)
                    norm("c", tb[:, 0:D], xn[:, par, :], par, it + 1).then_inc(S["c_x"], 1)
                    v.wait_ge(S["c_x"], it + 1)
                    ct.end()
                if static is None or static >= 2:
                    lowpart("c", y2, None, sc[:, 11:12], it - 2)
            tiles(v, stepC, lag=2)
            ct.close(NT)

            def stepD(it, par, static):
                ct.begin(it)
                v.wait_ge(S["d_ta"], it + 1)
                ct(v.scalar_tensor_tensor(out=tb[:, 0:D], in0=PS[:, par, 0:D], scalar=sc[:, 13:14], in1=ta[:, par, 0:D], op0=ALU.mult, op1=ALU.add))
                ct(v.tensor_tensor(tb[:, 0:D], tb[:, 0:D], bgrow[:], ALU.add))
                ct(v.tensor_scalar(tb[:, 0:D], tb[:, 0:D], 0.0, None, ALU.max))
                if static is None or static >= 2:
                    v.wait_ge(S["d_xTp"], it - 1)
                norm("d", tb[:, 0:D], xn[:, par, :], par, it + 1).then_inc(S["d_x"], 1)
                v.wait_ge(S["d_x"], it + 1)
                ct.end()
            v.wait_ge(S["c_cp"], NT)
            v.memset(h2T[:, 0:3], 0.0).then_inc(S["m_s0"], 1)
            v.memset(state[:], 0.0).then_inc(S["m_s0"], 1)
            for name, credit in CR.items():
                v.sem_inc(S[name], credit)
            tiles(v, stepD)
            ct.close(NT)
            mamba_vector(v, ct, 0)
            if_general(v, lambda q: general_vector(q, ct, norm))

    return nc


_INS = ['x', 'adj', 'L0_gnn_h0', 'L0_gnn_a', 'L0_gnn_temp', 'L1_gnn_weight', 'L1_gnn_bias', 'L2_gnn_gcn_w', 'L2_gnn_gcn_b', 'L2_gnn_ln_g', 'L2_gnn_ln_b', 'L2_gnn_w_in', 'L2_gnn_conv_w', 'L2_gnn_conv_b', 'L2_gnn_w_xp', 'L2_gnn_w_dt', 'L2_gnn_b_dt', 'L2_gnn_A_log', 'L2_gnn_D_skip', 'L2_gnn_w_out', 'L3_gnn_W', 'L3_gnn_B']
_OUTS = [((4096, 128), 'float32')]


def kernel(**inputs):
    import numpy as _np
    import concourse.bacc as _bacc
    from concourse import mybir as _mybir
    from concourse.bass_utils import run_bass_kernel_spmd as _run

    nc = _bacc.Bacc("TRN2", target_bir_lowering=False, num_devices=1)
    arrays, args = {}, {}
    for name in _INS:
        a = _np.ascontiguousarray(inputs[name])
        arrays[f"in_{name}_dram"] = a
        args[name] = nc.dram_tensor(f"in_{name}_dram", a.shape, _mybir.dt.from_np(a.dtype), kind="ExternalInput").ap()
    shape, dtype = _OUTS[0]
    out = nc.dram_tensor("out_0_dram", shape, _mybir.dt.from_np(_np.dtype(dtype)), kind="ExternalOutput").ap()
    build(nc, args, out)
    r = _run(nc, [arrays], core_ids=[0])
    return r.results[0]["out_0_dram"]
```

```python
from contextlib import ExitStack

import concourse.bass as bass
from concourse import mybir

ALU = mybir.AluOpType
ACT = mybir.ActivationFunctionType
AX_X = mybir.AxisListType.X
F32, BF16, F16 = mybir.dt.float32, mybir.dt.bfloat16, mybir.dt.float16
F8, U8, I32 = mybir.dt.float8e4, mybir.dt.uint8, mybir.dt.int32
RMAX = bass.bass_isa.ReduceOp.max

P = 128
N = 4096
D = 128
NT = N // P
BANK = 512
COLS = D + 3
ALPHA = 0.2
THRESH = 1e-6
EPS = 1e-5
SUMSCALE = 16384.0
HALFMAX = 30000.0
ROWNORM = 11.32
SPREAD = 14.0
DI = 256
NH = DI // P
DS = 16
DTR = 8
KC = 4
T = 1024
NCH = N // T
TB = T // BANK
TPC = T // P


class Chain:

    def __init__(self, eng, sem):
        self.eng, self.sem, self.start, self.per = eng, sem, 0, None

    def begin(self, idx=0, per=None):
        self.idx, self.k = idx, 0
        self.per = self.per if per is None else per

    def mark(self, ins):
        self.k += 1
        ins.then_inc(self.sem, 1)
        return self.k

    def need(self, k):
        at = self.start + k
        if self.per is not None:
            at = at + self.idx * self.per
        self.eng.wait_ge(self.sem, at)

    def __call__(self, ins):
        self.need(self.mark(ins))
        return ins

    def end(self, tiles=1):
        if self.per is None:
            self.per = self.k
        assert self.per * tiles == self.k

    def close(self, n=1):
        self.start += n * self.per
        self.per = None


def build(nc, A, out):
    ctx = ExitStack()
    with ctx:
        ctx.enter_context(nc.allow_non_contiguous_dma(reason="a few small vectors go to one element a partition"))
        sb = lambda n, s, d: ctx.enter_context(nc.sbuf_tensor(n, s, d))
        sem = lambda n: ctx.enter_context(nc.semaphore(n))

        xs = sb("xs", [P, NT, D], F32)
        feat = sb("feat", [P, NT, D], F32)
        y1 = sb("y1", [P, NT, 2 * COLS], F16)
        y2 = sb("y2", [P, NT, 2 * COLS], F16)
        y1b = sb("y1b", [P, NT, 2 * D], F16)
        y2b = sb("y2b", [P, NT, 2 * D], F16)
        f2row = sb("f2row", [P, N + 4], F32)
        adjt = sb("adjt", [P, 2, N], F32)
        s1r = sb("s1r", [P, 2, N], BF16)
        s1T = sb("s1T", [P, 2, N], F8)
        s2T = sb("s2T", [P, 2, N], F8)
        mT = sb("mT", [P, 2, N], F8)
        idf = sb("idf", [P, P], F32)
        idb = sb("idb", [P, P], BF16)
        ones = sb("ones", [P, P], F32)
        acol = sb("acol", [P, 2], F32)
        a2rep = sb("a2rep", [P, P], F32)
        coe = sb("coe", [P, 5], F32)
        W1 = sb("W1", [P, D], F32)
        Wg = sb("Wg", [P, D], F32)
        b1row = sb("b1row", [P, D], F32)
        bgrow = sb("bgrow", [P, D], F32)
        lng = sb("lng", [P, 1], F32)
        lnb = sb("lnb", [P, 1], F32)
        win = sb("win", [P, 2 * DI], F32)
        wtap = sb("wtap", [P, KC, DI], F32)
        convb = sb("convb", [P, NH], F32)
        wxp = sb("wxp", [P, NH, DTR + 2 * DS], F32)
        wdt = sb("wdt", [DTR, DI], F32)
        bdt = sb("bdt", [P, NH], F32)
        Aneg = sb("Aneg", [P, NH, DS], F32)
        dskip = sb("dskip", [P, NH], F32)
        wout = sb("wout", [P, NH, D], F32)
        f12 = sb("f12", [P, NT, 2], F32)
        nf1 = sb("nf1", [P, NT], F32)
        Ea = sb("Ea", [P, NT], F32)
        Eb = sb("Eb", [P, NT], F32)
        Ea2 = sb("Ea2", [P, NT], F32)
        Eb2 = sb("Eb2", [P, NT], F32)
        EE = sb("EE", [P, 2, NT], F32)
        EE2 = sb("EE2", [P, 2, NT], F32)
        Es = sb("Es", [P, 2, NT], F32)
        Es2 = sb("Es2", [P, 2, NT], F32)
        cnt = sb("cnt", [P, NT], F32)
        deg = sb("deg", [P, NT], F32)
        dinv = sb("dinv", [P, NT], F32)
        dsc = sb("dsc", [P, NT], F32)
        rden = sb("rden", [P, NT], F32)
        rsum = sb("rsum", [P, NT], F32)
        k2 = sb("k2", [P, NT], F32)
        g1 = sb("g1", [P, NT], F32)
        g2 = sb("g2", [P, NT], F32)
        sc = sb("sc", [P, 48], F32)
        stat = sb("stat", [P, 4], F32)
        red = sb("red", [P, 4], F32)
        ta = sb("ta", [P, 2, 2 * COLS], F32)
        tails = sb("tails", [P, 4 * COLS], F32)
        tb2 = tails[:, :].rearrange("p (k n) -> p k n", k=2)
        tb = tails[:, 0:2 * COLS]
        h0t = tails[:, 2 * COLS:2 * COLS + 2 * D].rearrange("p (k d) -> p k d", k=2)
        tc = sb("tc", [P, 8], F32)
        tp = sb("tp", [P, 2, 8], F32)
        bn6 = sb("bn6", [P, 6], F32)
        mv = sb("mv", [P, 2], F32)
        bn8 = sb("bn8", [P, TPC, 6], F32)
        mv8 = sb("mv8", [P, TPC, 2], F32)
        rstd8 = sb("rstd8", [P, TPC], F32)
        rstd = sb("rstd", [P, 2], F32)
        xTt = sb("xTt", [P, 2, P], F32)
        state = sb("state", [P, NH * DS], F32)
        xn = sb("xn", [P, 2, D], F32)
        flag = sb("flag", [P, 1], I32)
        W3, b3row = ones, a2rep
        outt = xn

        cwrow = s1r[:, 0, 0:2 * DI * KC].bitcast(F32)

        PS = ctx.enter_context(nc.psum_tensor("PS", [P, 8, BANK], F32))

        stS = nc.dram_tensor("scratch_s1T", [NT, P, N], U8).ap()
        stM = nc.dram_tensor("scratch_mT", [NT, P, N], U8).ap()
        f2d = nc.dram_tensor("scratch_f2", [1, N], F32).ap()
        bcd = nc.dram_tensor("scratch_bc", [2 * DS, N], F32).ap()

        h2T = f2row
        xT = feat[:, :, :].rearrange("p t d -> p (t d)")
        adj_rows = A["adj"].rearrange("(t p) n -> t p n", p=P)
        h0_rows = A["L0_gnn_h0"].rearrange("(t p) d -> t p d", p=P)
        out_rows = out.rearrange("(t p) d -> t p d", p=P)

        S = {n: sem(n) for n in (
            "pad", "s_f2d", "s_flag", "s_x", "s_w", "s_id", "s_tr0", "s_xT", "s_f", "s_fc", "s_col", "s_red", "s_ex", "s_exd", "s_y0", "s_y0a", "s_init",
            "v_chain", "t_chain", "a_chain", "g_chain", "p_w",
            "adj0", "adj1", "a_s1", "a_adjT", "a_adjE", "a_s1Tp", "a_s1E", "a_s2", "a_prod", "a_ta", "a_tail", "a_feat", "a_low", "a_spl", "a_stS0", "a_stS1", "a_stM0", "a_stM1",
            "b_ldS0", "b_ldS1", "b_ldM0", "b_ldM1", "b_h0", "b_h1", "b_s2", "b_s2g", "b_prod", "b_ta", "b_var", "b_std", "b_x1", "b_xTp", "b_xTe", "b_y", "b_hi", "b_tail", "b_low", "b_cp",
            "c_ldM0", "c_ldM1", "c_prod", "c_ta", "c_var", "c_std", "c_x", "c_xTp", "c_xTe", "c_y", "c_hi", "c_low", "c_cp", 
            "d_ldM0", "d_ldM1", "d_prod", "d_ta", "d_var", "d_std", "d_x", "d_xTp", "d_xTe", 
            "m_x", "m_u", "m_z", "m_sz", "m_dbc", "m_dbcE", "m_dt", "m_sp", "m_dtu", "m_lp", "m_bcS", "m_BC0", "m_BC1", "m_BC2", "m_BC3",
            "m_dA", "m_dBu", "m_h", "m_st", "m_hC", "m_y", "m_yg", "m_yo", "m_o", "m_var", "m_std", "m_x3", "m_out", "m_s0")}

        S.update({"g_" + n: sem("g_" + n) for n in ("bar", "in", "adj", "ask", "did", "rows", "tr", "trE", "prod", "end",
                                                    "hx", "hT", "hE", "px", "pT", "pE", "py", "fin", "std", "out")})

        def passed(eng):
            eng.sem_inc(S["pad"], 1)


        def rows(ap):
            return ap.rearrange("p a n -> p (a n)").bitcast(F32)[:, 0:4 * T].rearrange("p (k t) -> p k t", t=T)
        u4, dt4 = rows(y1b[:, :, :]), rows(y2b[:, :, :])
        dtu4 = feat[:, :, :].rearrange("p t d -> p (t d)").rearrange("p (k t) -> p k t", t=T)
        sz4 = y1[:, :, :].rearrange("p t d -> p (t d)")[:, 0:8 * T].bitcast(F32).rearrange("p (k t) -> p k t", t=T)
        tmp = rows(s1r[:, :, :])
        lnw, ex = tmp[:, 0:2, :], tmp[:, 2:4, :]
        yg = lnw
        dbcs = tmp[0:DTR + 2 * DS, 0, :]
        zt = ex[:, 0, :].rearrange("p (t d) -> p t d", d=D)
        zo = ex[:, 1, :].rearrange("p (t d) -> p t d", d=D)
        BC = adjt[:, :, :].rearrange("p a n -> p (a n)").rearrange("p (s k t) -> p s k t", k=2, t=T)
        NB = 4
        hh = y2[:, :, :].rearrange("p t d -> p (t d)")[:, 0:8 * T].bitcast(F32).rearrange("p (k t) -> p k t", t=T)
        dA = s1T[:, :, :].rearrange("p a n -> p (a n)").bitcast(F32).rearrange("p (k t) -> p k t", t=T)
        dBu = s2T[:, :, :].rearrange("p a n -> p (a n)").bitcast(F32).rearrange("p (k t) -> p k t", t=T)
        hC = mT[:, :, :].rearrange("p a n -> p (a n)").bitcast(F32).rearrange("p (k t) -> p k t", t=T)
        PER = NH * DS
        CR = {"m_h": 2, "m_dBu": NH * NB, "m_hC": NH * NB, "m_st": 4, "m_y": 2, "m_yg": 2 * NH, "m_o": 2, "m_yo": 2, "m_x3": 2,
              "m_bcS": 16, "m_out": 32}
        PE_AHEAD = {4: range(16), 7: [16], 8: [17], 9: [18], 10: [19], 13: [20], 14: [21], 17: [22], 18: [23]}
        ACT_AHEAD = {6: [0, 1], 13: [2, 3], 17: [4], **{20 + k: [5 + k] for k in range(6)}, 26: [11, 12], 27: [13, 14]}
        DVE_AHEAD = {28 + k: [k] for k in range(4)}
        SYNC_AHEAD = 12

        PE_D = {10: range(16), 12: range(16, 20), 14: range(20, 22), 16: range(22, 24)}
        ACT_D = {10: range(2), 12: range(2, 4), 14: [4], 16: [5, 6], 18: [7, 8], 20: [9, 10], 22: [11, 12], 24: [13, 14]}
        DVE_D = {26: [0], 28: [1], 30: [2, 3]}
        SYNC_D = {18: [0]}
        EARLY = 4
        assert min(*PE_AHEAD, *ACT_AHEAD, *DVE_AHEAD) >= EARLY

        def halves(ap, a):
            if isinstance(a, int):
                return ap[:, NH * (a % 2):NH * (a % 2) + NH, :]
            return ap[:, bass.ds((a & 1) * NH, NH), :]

        def half(ap, a, h):
            if isinstance(a, int):
                return ap[:, NH * (a % 2) + h, :]
            return ap[:, bass.ds((a & 1) * NH + h, 1), :].rearrange("p o t -> p (o t)")

        def chunks(eng, ahead, parts, steps, tail, c0):
            for k in range(parts if c0 else 0):
                ahead(k, c0, 0)
            steps(c0, 0, 0, EARLY, True)
            def chunk(c, a, more):
                steps(c, a, EARLY, PER, more)
                tail(c, a, more, lambda: steps(c + 1, a + 1, 0, EARLY, True) if more else None)
            with eng.Fori(0, NCH - 1) as a:
                chunk(a + c0 if c0 else a, a, True)
            chunk(c0 + NCH - 1, NCH - 1, False)

        def between(parts, f):
            def part(ks):
                return lambda: [f(k) for k in ks]
            return {it: part(ks) for it, ks in parts.items()}

        def bank2(b):
            return PS[:, b:b + TB, :].rearrange("p b n -> p (b n)")

        skip = h0t
        def skips(v):
            for h in range(NH):
                v.tensor_scalar(skip[:, h, :], idf[:], dskip[:, h:h + 1], None, ALU.mult).then_inc(S["m_s0"], 1)

        def mamba_sync(q, c0, part=None):
            def ahead(k, c, a):
                q.wait_ge(S["m_dbcE"], c + 1)
                passed(q)
                q.dma_start(bcd[:, bass.ds(a * T, T)], dbcs[DTR:DTR + 2 * DS, :]).then_inc(S["m_bcS"], 16)
            def steps(c, a, lo, hi, more):
                if lo == 0:
                    q.wait_ge(S["m_bcS"], c * 16 + (CR["m_bcS"] + 16))
                for n in range(NB if lo else 0, DS if lo else NB):
                    q.wait_ge(S["m_dBu"], c * PER + NH * (n + 1))
                    q.wait_ge(S["m_hC"], c * PER + NH * (n + 1))
                    passed(q)
                    q.dma_start(BC[:, n % NB, :, :], bcd.rearrange("(k n) t -> n k t", k=2)[n, :, bass.ds(a * T, T)].partition_broadcast(P)).then_inc(S[f"m_BC{n % NB}"], 16)
                    if more and n == SYNC_AHEAD:
                        ahead(0, c + 1, a + 1)
            def tail(c, a, more, early):
                early()
                if not c0:
                    q.wait_ge(S["m_x3"], c + (CR["m_x3"] + 1))
                    passed(q)
                    q.dma_start(out.rearrange("(t p) d -> p t d", p=P)[:, bass.ds(a * TPC, TPC), :], zo).then_inc(S["m_out"], 16)
            if part is not None:
                return ahead(part, 0, 0)
            chunks(q, ahead, 1, steps, tail, c0)

        def mamba_pe(p, c0, part=None):
            if c0 or part == 0:
                p.wait_ge(S["m_s0"], 8 if c0 else 4)
                p.wait_ge(S["d_xTe"], TPC)
            def ahead(k, c, a):
                u_, b = halves(u4, a), k % TB
                if k < 16:
                    h, b, tap = k // 8, k // KC % TB, k % KC
                    if k == 0:
                        p.wait_ge(S["m_o"], c + (CR["m_o"] - 1))
                        p.wait_ge(S["m_sp"], c * NH)
                    ins = p.matmul(PS[:, 4 + TB * h + b, :], wtap[:, tap, h * P:(h + 1) * P], h2T[:, bass.ds(a * T + (b * BANK + tap), BANK)], start=(tap == 0), stop=(tap == KC - 1))
                    if k % 8 == 7:
                        ins.then_inc(S["m_x"], 1)
                elif k < 20:
                    h = k // TB % NH
                    if b == 0:
                        p.wait_ge(S["m_u"], c * NH + h + 1)
                    ins = p.matmul(PS[:, 4 + TB * h + b, :], win[:, DI + h * P:DI + (h + 1) * P], h2T[:, bass.ds(a * T + (b * BANK + KC - 1), BANK)], start=True, stop=True)
                    if b == TB - 1:
                        ins.then_inc(S["m_z"], 1)
                elif k < 22:
                    p.wait_ge(S["m_sz"], c * NH + 1)
                    for h in range(NH):
                        ins = p.matmul(PS[0:DTR + 2 * DS, 4 + b, :], wxp[:, h, :], half(u4, a, h)[:, b * BANK:(b + 1) * BANK], start=(h == 0), stop=(h == NH - 1))
                    if b == TB - 1:
                        ins.then_inc(S["m_dbc"], 1)
                else:
                    h = k - 22
                    p.wait_ge(S["m_dbcE"], c + 1)
                    p.wait_ge(S["m_sz"], c * NH + NH)
                    for b in range(TB):
                        ins = p.matmul(PS[:, 4 + TB * h + b, :], wdt[:, h * P:(h + 1) * P], dbcs[0:DTR, b * BANK:(b + 1) * BANK], start=True, stop=True)
                    ins.then_inc(S["m_dt"], 1)
            def steps(c, a, lo, hi, more):
                for i in range(lo, hi):
                    if more:
                        for k in PE_AHEAD.get(i, ()):
                            ahead(k, c + 1, a + 1)
                    h = i % NH
                    if i == 0:
                        p.wait_ge(S["m_yg"], c * NH + CR["m_yg"])
                    if NH <= i < 2 * NH:
                        for b in range(TB):
                            p.matmul(PS[:, TB * h + b, :], skip[:, h, :], half(u4, a, h)[:, b * BANK:(b + 1) * BANK], start=False, stop=False)
                    p.wait_ge(S["m_hC"], c * PER + (CR["m_hC"] + i + 1))
                    for b in range(TB):
                        ins = p.matmul(PS[:, TB * h + b, :], idf[:], hC[:, i % 2, b * BANK:(b + 1) * BANK], start=(i < NH), stop=(i >= PER - NH))
                    ins.then_inc(S["m_y"], 1)
            def tail(c, a, more, early):
                p.wait_ge(S["m_sp"], c * NH + (2 * NH if more else NH))
                p.wait_ge(S["m_yg"], c * NH + (CR["m_yg"] + NH))
                for t in range(TPC):
                    for h in range(NH):
                        ins = p.matmul(PS[:, 6 + t // 4, t % 4 * D:t % 4 * D + D], yg[:, h, t * P:(t + 1) * P], wout[:, h, :], start=(h == 0), stop=(h == NH - 1))
                ins.then_inc(S["m_yo"], 1)
                early()
            if part is not None:
                return ahead(part, 0, 0)
            chunks(p, ahead, 24, steps, tail, c0)

        def mamba_scalar(s, ch, c0, part=None):
            def ahead(k, c, a):
                if k < 2:
                    if k == 0:
                        s.wait_ge(S["m_yg"], c * NH + (CR["m_yg"] - NH))
                    s.wait_ge(S["m_x"], c * NH + k + 1)
                    passed(s)
                    s.activation(half(u4, a, k), bank2(4 + TB * k), ACT.Silu, bias=convb[:, k:k + 1]).then_inc(S["m_u"], 1)
                elif k < 4:
                    h = k - 2
                    s.wait_ge(S["m_z"], c * NH + h + 1)
                    passed(s)
                    s.activation(half(sz4, a, h), bank2(4 + TB * h), ACT.Silu).then_inc(S["m_sz"], 1)
                elif k == 4:
                    s.wait_ge(S["m_dbc"], c + 1)
                    s.wait_ge(S["m_yo"], c + (CR["m_yo"] - 1))
                    s.wait_ge(S["m_bcS"], c * 16 + CR["m_bcS"])
                    s.activation(dbcs, PS[0:DTR + 2 * DS, 4:4 + TB, :].rearrange("p b n -> p (b n)"), ACT.Copy).then_inc(S["m_dbcE"], 1)
                else:
                    j, h = (k - 5) // NH, (k - 5) % NH
                    v_, w = bank2(4 + TB * h), half(dtu4, a, h)
                    if j == 0:
                        if h == 0:
                            ch.begin(a, 4 * NH)
                            s.wait_ge(S["m_x3"], c + (CR["m_x3"] - 1))
                            if not c0:
                                s.wait_ge(S["m_out"], c * 16 + (CR["m_out"] - 16))
                        s.wait_ge(S["m_dt"], c * NH + h + 1)
                        ch(s.activation(ex[:, h, :], v_, ACT.Abs, bias=bdt[:, h:h + 1]))
                    elif j == 1:
                        ch(s.activation(ex[:, h, :], ex[:, h, :], ACT.Exp, scale=-1.0))
                    elif j == 2:
                        passed(s)
                        ch(s.activation(half(dt4, a, h), v_, ACT.Relu, bias=bdt[:, h:h + 1]))
                    elif j == 3:
                        passed(s)
                        ch(s.activation(w, ex[:, h, :], ACT.Identity, bias=1.0))
                    else:
                        if h == 0:
                            s.wait_ge(S["m_dt"], c * NH + NH)
                            s.wait_ge(S["m_bcS"], c * 16 + (CR["m_bcS"] + 16))
                        passed(s)
                        s.activation(lnw[:, h, :], w, ACT.Ln).then_inc(S["m_sp"], 1)
                        if h == NH - 1:
                            ch.end()
            def steps(c, a, lo, hi, more):
                for i in range(lo, hi):
                    n, h = i // NH, i % NH
                    if i == 0:
                        s.wait_ge(S["m_dtu"], c + 1)
                    s.wait_ge(S["m_h"], c * PER + (i + 1))
                    passed(s)
                    s.activation(dA[:, i % 2, :], half(dt4, a, h), ACT.Exp, scale=Aneg[:, h, n:n + 1]).then_inc(S["m_dA"], 1)
                    if more:
                        for k in ACT_AHEAD.get(i, ()):
                            ahead(k, c + 1, a + 1)
            def tail(c, a, more, early):
                early()
                for r in range(1 if c0 else 2):
                    s.wait_ge(S["m_var"], (c - c0 if c0 else c) * (1 if c0 else 2) + (2 * NCH if c0 else 0) + r + 1)
                    s.activation(rstd8[:], mv8[:, :, 1], ACT.Sqrt, bias=sc[:, 12:13]).then_inc(S["m_std"], 1)
            if part is not None:
                return ahead(part, 0, 0)
            chunks(s, ahead, 15, steps, tail, c0)
            ch.close(NCH)

        def mamba_gpsimd(g, c0):
            def steps(c, a, lo, hi, more):
                g.wait_ge(S["m_dtu"], c + 1)
                for i in range(lo, hi):
                    n, h = i // NH, i % NH
                    if h == 0:
                        g.wait_ge(S[f"m_BC{n % NB}"], c * (16 * DS // NB) + 16 * (n // NB + 1))
                    g.wait_ge(S["m_h"], c * PER + (i + 1))
                    passed(g)
                    g.tensor_tensor(dBu[:, i % 2, :], half(dtu4, a, h), BC[:, n % NB, 0, :], ALU.mult).then_inc(S["m_dBu"], 1)
            chunks(g, None, 0, steps, lambda c, a, more, early: early(), c0)

        def mamba_vector(v, ct, c0, part=None):
            def ahead(k, c, a):
                if k == 0:
                    v.wait_ge(S["m_sp"], c * NH + NH)
                    ins = v.scalar_tensor_tensor(out=ex, in0=halves(dtu4, a), scalar=1.0, in1=ex, op0=ALU.subtract, op1=ALU.subtract)
                else:
                    v.wait_ge(S["m_lp"], c * 3 + k)
                    if k == 1:
                        ins = v.tensor_tensor(ex, lnw, ex, ALU.subtract)
                    elif k == 2:
                        ins = v.tensor_tensor(halves(dt4, a), halves(dt4, a), ex, ALU.add)
                    else:
                        v.tensor_tensor(halves(dtu4, a), halves(dt4, a), halves(u4, a), ALU.mult).then_inc(S["m_dtu"], 1)
                        return
                ins.then_inc(S["m_lp"], 1)
            def steps(c, a, lo, hi, more):
                def readout(i):
                    n, h = i // NH, i % NH
                    v.wait_ge(S["m_h"], c * PER + (CR["m_h"] + i + 1))
                    v.tensor_copy(state[:, i:i + 1], hh[:, i % 4, T - 1:T]).then_inc(S["m_st"], 1)
                    if h == 0:
                        v.wait_ge(S[f"m_BC{n % NB}"], c * (16 * DS // NB) + 16 * (n // NB + 1))
                    v.wait_ge(S["m_y"], c * PER + (i + 1))
                    v.tensor_tensor(hC[:, i % 2, :], hh[:, i % 4, :], BC[:, n % NB, 1, :], ALU.mult).then_inc(S["m_hC"], 1)
                for i in range(lo, hi):
                    v.wait_ge(S["m_dA"], c * PER + i + 1)
                    v.wait_ge(S["m_dBu"], c * PER + (CR["m_dBu"] + i + 1))
                    v.wait_ge(S["m_st"], c * PER + (i + 1))
                    v.wait_ge(S["m_hC"], c * PER + (CR["m_hC"] + i - 3))
                    v.tensor_tensor_scan(hh[:, i % 4, :], dA[:, i % 2, :], dBu[:, i % 2, :], state[:, i:i + 1], ALU.mult, ALU.add).then_inc(S["m_h"], 1)
                    if more:
                        for k in DVE_AHEAD.get(i, ()):
                            ahead(k, c + 1, a + 1)
                    if i > lo:
                        readout(i - 1)
                readout(hi - 1)
            def tail(c, a, more, early):
                ct.begin(a, 1 + 3 * (1 if c0 else 2))
                v.wait_ge(S["m_y"], c * PER + (CR["m_y"] + PER))
                v.tensor_tensor(yg, PS[:, 0:NH * TB, :].rearrange("p (h b) n -> p h (b n)", h=NH), halves(sz4, a), ALU.mult).then_inc(S["m_yg"], NH)
                early()
                r = xs[:, bass.ds(a * TPC, TPC), :]
                v.wait_ge(S["m_yo"], c + (CR["m_yo"] + 1))
                ct(v.tensor_tensor(zt, PS[:, 6:8, :].rearrange("p b (t d) -> p (b t) d", d=D), r, ALU.add))
                v.sem_inc(S["m_o"], 1)
                for k in range(1 if c0 else 2):
                    for t in range(TPC):
                        ins = v.bn_stats(bn8[:, t, :], zt[:, t, :])
                    ct(ins)
                    passed(v)
                    for t in range(TPC):
                        ins = v.bn_aggr(mv8[:, t, :], bn8[:, t, :])
                    ins.then_inc(S["m_var"], 1)
                    v.wait_ge(S["m_std"], (c - c0 if c0 else c) * (1 if c0 else 2) + (2 * NCH if c0 else 0) + k + 1)
                    ct(v.reciprocal(rstd8[:], rstd8[:]))
                    for t in range(TPC):
                        if c0:
                            dst = xs[:, bass.ds(a * TPC + t, 1), :].rearrange("p o d -> p (o d)")
                        else:
                            dst = zo[:, t, :] if k else zt[:, t, :]
                        ins = v.tensor_scalar(dst, zt[:, t, :], mv8[:, t, 0:1], rstd8[:, t:t + 1], ALU.subtract, ALU.mult)
                    ct(ins)
                v.sem_inc(S["m_x3"], 1)
                ct.end()
            if part is not None:
                return ahead(part, 0, 0)
            chunks(v, ahead, 4, steps, tail, c0)
            ct.close(NCH)


        A0, A1 = adjt[:, 0, :], adjt[:, 1, :]
        GT = s1r[:, :, :].rearrange("p a n -> p (a n)").bitcast(F32)
        KEYS1, KEYS2, CONV, GCN, DIST = range(5)
        ASKS = [2, 2, 1, 1, 3]
        RHS = [xs, feat, feat, feat, feat]
        STEPS = [17, 14, 7, 6, 9]
        NEG = -9000000000000000.0

        def if_general(eng, body):
            eng.wait_ge(S["s_flag"], 1)
            r = eng.value_load(flag[0:1, 0:1])
            with eng.If(r > 0):
                eng.drain().then_inc(S["g_bar"], 1)
                eng.wait_ge(S["g_bar"], 5)
                body(eng)

        def general_sync(q):
            q.dma_start(xs[:, :, :], A["x"].rearrange("(t p) d -> p t d", p=P)).then_inc(S["g_in"], 16)
            q.dma_start(f2row[:, 0:N], f2d[0].partition_broadcast(P)).then_inc(S["g_in"], 16)
            q.dma_start(W3[:], A["L3_gnn_W"]).then_inc(S["g_in"], 16)
            q.dma_start(b3row[:], A["L3_gnn_B"].partition_broadcast(P)).then_inc(S["g_in"], 16)
            for m in range(5):
                if m == DIST:
                    mamba_sync(q, NCH)
                    q.wait_ge(S["m_dBu"], CR["m_dBu"] + 2 * NCH * PER)
                    q.wait_ge(S["m_hC"], CR["m_hC"] + 2 * NCH * PER)
                with q.Fori(0, NT) as it:
                    q.wait_ge(S["g_end"], it + (1 + m * NT))
                    passed(q)
                    if m == KEYS2:
                        q.dma_start(h0t[:, 0, :], h0_rows[bass.ds(it, 1)].rearrange("o p d -> (o p) d")).then_inc(S["g_adj"], 16)
                    q.dma_start(A0, adj_rows[bass.ds(it, 1)].rearrange("o p n -> (o p) n")).then_inc(S["g_adj"], 16)
                    if m == DIST:
                        q.wait_ge(S["g_fin"], it + 2)
                        passed(q)
                        q.dma_start(out_rows[bass.ds(it, 1)].rearrange("o p d -> (o p) d"), outt[:, 0, :]).then_inc(S["g_out"], 16)
            q.wait_ge(S["g_out"], 16 * NT)

        def general_pe(p):
            def product(m):
                with p.Fori(0, NT) as it:
                    p.wait_ge(S["g_rows"], it + (1 + m * NT))
                    for g in range(8):
                        if g >= 2:
                            p.wait_ge(S["g_trE"], it * 8 + (8 * m * NT + g - 1))
                        for k in range(4):
                            j = 4 * g + k
                            src = A0 if m in (CONV, GCN) else A1
                            ins = p.transpose(PS[:, 4 + g % 2, k * P:(k + 1) * P], src[:, j * P:(j + 1) * P], idf[:])
                        ins.then_inc(S["g_tr"], 1)
                    p.wait_ge(S["g_trE"], it * 8 + (8 * m * NT + 8))
                    for j in range(NT):
                        ins = p.matmul(PS[:, 0, 0:D], GT[:, j * P:(j + 1) * P], RHS[m][:, j, :], start=(j == 0), stop=(j == NT - 1))
                    ins.then_inc(S["g_prod"], 1)
                    if m == GCN:
                        p.wait_ge(S["g_hx"], it + 1)
                        p.transpose(PS[:, 6, 0:P], xn[:, 0, :], idf[:]).then_inc(S["g_hT"], 1)

            def project(k, W):
                with p.Fori(0, NT) as t:
                    p.wait_ge(S["g_px"], t + (1 + k * NT))
                    p.transpose(PS[:, 4, 0:P], xn[:, 0, :], idf[:]).then_inc(S["g_pT"], 1)
                    p.wait_ge(S["g_pE"], t + (1 + k * NT))
                    p.matmul(PS[:, 5, 0:D], xTt[:, 0, :], W[:], start=True, stop=True).then_inc(S["g_py"], 1)
            product(KEYS1)
            product(KEYS2)
            project(0, W1)
            product(CONV)
            project(1, Wg)
            product(GCN)
            p.wait_ge(S["g_hE"], NT)
            mamba_pe(p, NCH)
            project(2, W3)
            product(DIST)

        def general_scalar(s, ch):
            def product(m):
                with s.Fori(0, NT) as it:
                    asks = [sum(ASKS[:m]) * NT]
                    def asked():
                        asks[0] += 1
                        s.wait_ge(S["g_ask"], it * ASKS[m] + asks[0])
                    if m in (KEYS1, KEYS2):
                        asked()
                        s.activation(A1, A1, ACT.Exp, bias=tc[:, 1:2], accum_out=tc[:, 2:3]).then_inc(S["g_did"], 1)
                    if m == KEYS1:
                        asked()
                        s.activation(A0, A1, ACT.Square, accum_out=tc[:, 3:4]).then_inc(S["g_did"], 1)
                    if m == DIST:
                        asked()
                        s.activation(A1, A1, ACT.Square, bias=tc[:, 1:2]).then_inc(S["g_did"], 1)
                        asked()
                        s.activation(A1, A1, ACT.Exp, scale=-2.0).then_inc(S["g_did"], 1)
                    for g in range(8):
                        s.wait_ge(S["g_tr"], it * 8 + (8 * m * NT + g + 1))
                        s.activation(GT[:, g * BANK:(g + 1) * BANK], PS[:, 4 + g % 2, :], ACT.Copy).then_inc(S["g_trE"], 1)
                    if m != KEYS1:
                        asked()
                        s.activation(rstd[:, 0:1], mv[:, 1:2], ACT.Sqrt, bias=sc[:, 12:13]).then_inc(S["g_did"], 1)
                    if m == GCN:
                        s.wait_ge(S["g_hT"], it + 1)
                        s.activation(h2T[:, bass.ds(it * P + 3, P)], PS[:, 6, 0:P], ACT.Identity, scale=lng[:, 0:1], bias=lnb[:, 0:1]).then_inc(S["g_hE"], 1)

            def project(k):
                with s.Fori(0, NT) as t:
                    s.wait_ge(S["g_pT"], t + (1 + k * NT))
                    s.activation(xTt[:, 0, :], PS[:, 4, 0:P], ACT.Copy).then_inc(S["g_pE"], 1)
            product(KEYS1)
            product(KEYS2)
            s.wait_ge(S["g_fin"], 1)
            s.activation(dsc[:], dinv[:], ACT.Sqrt).then_inc(S["g_std"], 1)
            project(0)
            product(CONV)
            project(1)
            product(GCN)
            mamba_scalar(s, ch, NCH)
            project(2)
            product(DIST)

        def general_gpsimd(g):
            mamba_gpsimd(g, NCH)

        def general_vector(v, ct, norm):
            row = lambda ap, t: ap[:, bass.ds(t, 1), :].rearrange("p o d -> p (o d)")
            z = tb[:, 0:D]

            def product(m):
                asks = [0]
                with v.Fori(0, NT) as it:
                    one = lambda ap: ap[:, bass.ds(it, 1)]
                    base = sum(ASKS[:m]) * NT
                    ct.begin(it, STEPS[m])

                    def ask(ins):
                        asks[0] += 1
                        ins.then_inc(S["g_ask"], 1)
                        v.wait_ge(S["g_did"], it * ASKS[m] + (base + asks[0]))
                    loads = 2 if m == KEYS2 else 1
                    v.wait_ge(S["g_adj"], it * (16 * loads) + 16 * (loads + (m + (m > KEYS2)) * NT))
                    if m in (KEYS1, KEYS2):
                        if m == KEYS1:
                            ct(v.tensor_reduce(tc[:, 4:5], A0, AX_X, ALU.add))
                            passed(v)
                            ct(v.tensor_copy(one(deg), tc[:, 4:5]))
                        ct(v.tensor_scalar(A1, f2row[:, 0:N], f12[:, bass.ds(it, 1), 0], None, ALU.add))
                        ct(v.scalar_tensor_tensor(out=A1, in0=A1, scalar=ALPHA, in1=A1, op0=ALU.mult, op1=ALU.max))
                        ct(v.tensor_scalar(A0, A0, 0.0, NEG, ALU.is_le, ALU.mult))
                        ct(v.tensor_tensor(A1, A1, A0, ALU.add))
                        ct(v.tensor_reduce(tc[:, 0:1], A1, AX_X, ALU.max))
                        ask(v.tensor_scalar(tc[:, 1:2], tc[:, 0:1], -1.0, None, ALU.mult))
                        if m == KEYS1:
                            ask(v.tensor_copy(tc[:, 0:1], tc[:, 2:3]))
                        v.sem_inc(S["g_rows"], 1)
                    elif m == DIST:
                        ct(v.memset(tc[:, 1:2], -1.0))
                        ct(v.tensor_scalar(A1, A0, 0.0, 0.001, ALU.is_equal, ALU.mult))
                        ct(v.tensor_tensor(A1, A1, A0, ALU.add))
                        ct(v.reciprocal(A1, A1))
                        ask(v.tensor_scalar(A1, A1, -10000.0, 10000.0, ALU.max, ALU.min))
                        ask(v.tensor_copy(tc[:, 0:1], tc[:, 1:2]))
                        ct(v.scalar_tensor_tensor(out=A1, in0=A0, scalar=1.0, in1=A1, op0=ALU.is_lt, op1=ALU.mult))
                        v.sem_inc(S["g_rows"], 1)
                    else:
                        ct(v.memset(tc[:, 1:2], -1.0))
                        v.sem_inc(S["g_rows"], 1)
                    v.wait_ge(S["g_prod"], it + (1 + m * NT))
                    num = PS[:, 0, 0:D]
                    if m == KEYS1:
                        ct(v.reciprocal(tc[:, 4:5], tc[:, 2:3]))
                        passed(v)
                        ct(v.tensor_copy(one(rden), tc[:, 4:5]))
                        ct(v.tensor_scalar(tc[:, 5:6], tc[:, 3:4], tc[:, 4:5], 0.5, ALU.mult, ALU.mult))
                        ct(v.tensor_scalar(tc[:, 5:6], tc[:, 5:6], tc[:, 4:5], None, ALU.mult))
                        passed(v)
                        ct(v.tensor_copy(one(rsum), tc[:, 5:6]))
                        ct(v.tensor_tensor(tc[:, 6:7], sc[:, 22:23], tc[:, 5:6], ALU.subtract))
                        ct(v.tensor_scalar(z, row(xs, it), tc[:, 6:7], None, ALU.mult))
                        ct(v.scalar_tensor_tensor(out=z, in0=num, scalar=tc[:, 4:5], in1=z, op0=ALU.mult, op1=ALU.add))
                        ct(v.tensor_scalar(tb[:, D:2 * D], z, -THRESH, THRESH, ALU.max, ALU.min))
                        ct(v.tensor_tensor(row(feat, it), z, tb[:, D:2 * D], ALU.subtract))
                    elif m == KEYS2:
                        ct(v.reciprocal(tc[:, 4:5], tc[:, 2:3]))
                        ct(v.tensor_scalar(z, num, tc[:, 4:5], None, ALU.mult))
                        ct(v.scalar_tensor_tensor(out=tb[:, D:2 * D], in0=z, scalar=sc[:, 27:28], in1=row(feat, it), op0=ALU.mult, op1=ALU.add))
                        ct(v.scalar_tensor_tensor(out=z, in0=z, scalar=coe[:, 1:2], in1=row(xs, it), op0=ALU.mult, op1=ALU.add))
                        ct(v.scalar_tensor_tensor(out=z, in0=tb[:, D:2 * D], scalar=one(k2), in1=z, op0=ALU.mult, op1=ALU.add))
                        ct(v.scalar_tensor_tensor(out=z, in0=h0t[:, 0, :], scalar=sc[:, 26:27], in1=z, op0=ALU.mult, op1=ALU.add))
                    elif m == CONV:
                        ct(v.tensor_tensor(z, num, row(feat, it), ALU.add))
                        ct(v.scalar_tensor_tensor(out=z, in0=z, scalar=one(dinv), in1=row(xs, it), op0=ALU.mult, op1=ALU.add))
                        ct(v.tensor_tensor(z, z, b1row[:], ALU.add))
                    elif m == GCN:
                        ct(v.tensor_tensor(z, num, bgrow[:], ALU.add))
                        ct(v.tensor_scalar(z, z, 0.0, None, ALU.max))
                    else:
                        ct(v.tensor_tensor(z, num, row(xs, it), ALU.add))
                    if m != KEYS1:
                        ct(v.bn_stats(bn6[:], z))
                        passed(v)
                        ask(v.bn_aggr(mv[:], bn6[:]))
                        ct(v.reciprocal(rstd[:, 0:1], rstd[:, 0:1]))
                        dst = xn[:, 0, :] if m in (GCN, DIST) else row(xs, it)
                        ct(v.tensor_scalar(dst, z, mv[:, 0:1], rstd[:, 0:1], ALU.subtract, ALU.mult))
                    if m == GCN:
                        v.sem_inc(S["g_hx"], 1)
                        v.wait_ge(S["g_hE"], it + 1)
                    if m == DIST:
                        v.sem_inc(S["g_fin"], 1)
                        v.wait_ge(S["g_out"], it * 16 + 16)
                    passed(v)
                    v.sem_inc(S["g_end"], 1)
                    ct.end()
                ct.close(NT)

            def project(k, scale, bias):
                with v.Fori(0, NT) as t:
                    ct.begin(t, 2)
                    passed(v)
                    ct(v.tensor_copy(xn[:, 0, :], row(xs, t)))
                    v.sem_inc(S["g_px"], 1)
                    v.wait_ge(S["g_py"], t + (1 + k * NT))
                    if scale is not None:
                        ct(v.tensor_scalar(row(feat, t), PS[:, 5, 0:D], scale[:, bass.ds(t, 1)], None, ALU.mult))
                    elif bias is not None:
                        ct(v.tensor_tensor(row(feat, t), PS[:, 5, 0:D], bias, ALU.add))
                    else:
                        passed(v)
                        ct(v.tensor_copy(row(feat, t), PS[:, 5, 0:D]))
                    ct.end()
                ct.close(NT)
            v.wait_ge(S["g_in"], 64)
            v.sem_inc(S["g_end"], 1)
            product(KEYS1)
            ct.begin()
            ct(v.tensor_scalar(k2[:], rsum[:], coe[:, 1:2], sc[:, 25:26], ALU.mult, ALU.add))
            ct.end(); ct.close()
            product(KEYS2)
            ct.begin()
            v.tensor_scalar(dinv[:], deg[:], 1.0, None, ALU.add).then_inc(S["g_fin"], 1)
            v.wait_ge(S["g_std"], 1)
            ct(v.reciprocal(dinv[:], dsc[:]))
            ct.end(); ct.close()
            project(0, dinv, None)
            product(CONV)
            project(1, None, None)
            v.memset(h2T[:, 0:3], 0.0).then_inc(S["m_s0"], 1)
            v.memset(state[:], 0.0).then_inc(S["m_s0"], 1)
            skips(v)
            product(GCN)
            mamba_vector(v, ct, NCH)
            project(2, None, b3row[:])
            product(DIST)

        block = ctx.enter_context(nc.Block())

        def tiles(eng, step, n=NT, lag=0, at={}):
            start = 4 if lag else 2
            for it in range(start):
                step(it, it % 2, it)
            for stop in [*sorted(at), n]:
                with eng.Fori(start // 2, stop // 2) as i:
                    step(i * 2, 0, None)
                    step(i * 2 + 1, 1, None)
                if stop in at:
                    at[stop]()
                start = stop
            for it in range(n, n + lag):
                step(it, it % 2, it)

        @block.sync
        def _(q):
            q.dma_start(xs[:, :, :], A["x"].rearrange("(t p) d -> p t d", p=P)).then_inc(S["s_x"], 16)
            q.dma_start(acol[:], A["L0_gnn_a"].rearrange("(k d) o -> d (k o)", k=2)).then_inc(S["s_x"], 16)
            q.dma_start(adjt[:, 0, :], adj_rows[0]).then_inc(S["adj0"], 16)
            q.dma_start(adjt[:, 1, :], adj_rows[1]).then_inc(S["adj1"], 16)
            n_w = 0
            for dst, src in (
                (coe[:], A["L0_gnn_temp"].partition_broadcast(P)),
                (W1[:], A["L1_gnn_weight"]), (Wg[:], A["L2_gnn_gcn_w"]),
                (b1row[:], A["L1_gnn_bias"].partition_broadcast(P)),
                (bgrow[:], A["L2_gnn_gcn_b"].partition_broadcast(P)),
                (lng[:], A["L2_gnn_ln_g"].rearrange("(p o) -> p o", o=1)),
                (lnb[:], A["L2_gnn_ln_b"].rearrange("(p o) -> p o", o=1)),
                (win[:], A["L2_gnn_w_in"]),
                (cwrow, A["L2_gnn_conv_w"].rearrange("e k -> (e k)").partition_broadcast(P)),
                (convb[:], A["L2_gnn_conv_b"].rearrange("(h p) -> p h", p=P)),
                (wxp[:], A["L2_gnn_w_xp"].rearrange("(h p) n -> p h n", p=P)),
                (wdt[:], A["L2_gnn_w_dt"]),
                (bdt[:], A["L2_gnn_b_dt"].rearrange("(h p) -> p h", p=P)),
                (Aneg[:], A["L2_gnn_A_log"].rearrange("(h p) n -> p h n", p=P)),
                (dskip[:], A["L2_gnn_D_skip"].rearrange("(h p) -> p h", p=P)),
                (wout[:], A["L2_gnn_w_out"].rearrange("(h p) n -> p h n", p=P)),
            ):
                q.dma_start(dst, src).then_inc(S["s_w"], 16)
                n_w += 1

            q.wait_ge(S["s_fc"], 8)
            q.dma_start(f2d, f2row[0:1, 0:N]).then_inc(S["s_f2d"], 16)
            def step(it, par, static):
                if static is None or static < NT - 2:
                    q.wait_ge(S["a_adjE"], 8 * (it + 1))
                    q.wait_ge(S["a_s1"], it + 1)
                    passed(q)
                    q.dma_start(adjt[:, par, :], adj_rows[bass.ds(it + 2, 1)].rearrange("o p n -> (o p) n")).then_inc(S[f"adj{par}"], 16)
                q.wait_ge(S["a_s1E"], 4 * (it + 1))
                passed(q)
                q.dma_start(stS[bass.ds(it, 1)].rearrange("o p n -> (o p) n"), s1T[:, par, :].bitcast(U8)).then_inc(S[f"a_stS{par}"], 16)
                q.dma_start(stM[bass.ds(it, 1)].rearrange("o p n -> (o p) n"), mT[:, par, :].bitcast(U8)).then_inc(S[f"a_stM{par}"], 16)
            step(0, 0, 0)
            step(1, 1, 1)
            with q.Fori(1, NT // 2 - 1) as i:
                step(i * 2, 0, None)
                step(i * 2 + 1, 1, None)
            step(NT - 2, 0, NT - 2)
            step(NT - 1, 1, NT - 1)
            for par in range(2):
                q.wait_ge(S[f"a_stS{par}"], 16 * NT // 2)
                q.wait_ge(S[f"a_stM{par}"], 16 * NT // 2)

            def step(it, par, static):
                if static == 0:
                    q.wait_ge(S["a_prod"], NT)
                    q.wait_ge(S["a_s2"], NT)
                elif static == 1:
                    pass
                else:
                    q.wait_ge(S["b_prod"], it - 1)
                passed(q)
                q.dma_start(s1T[:, par, :].bitcast(U8), stS[bass.ds(it, 1)].rearrange("o p n -> (o p) n")).then_inc(S[f"b_ldS{par}"], 16)
                q.dma_start(mT[:, par, :].bitcast(U8), stM[bass.ds(it, 1)].rearrange("o p n -> (o p) n")).then_inc(S[f"b_ldM{par}"], 16)
                if static == 0:
                    q.wait_ge(S["a_feat"], NT)
                if static is None or static >= 2:
                    q.wait_ge(S["b_x1"], it - 1)
                passed(q)
                q.dma_start(h0t[:, par, :], h0_rows[bass.ds(it, 1)].rearrange("o p d -> (o p) d")).then_inc(S[f"b_h{par}"], 16)
            tiles(q, step)

            for st, prev in (("c", "b"), ("d", "c")):
                def step(it, par, static):
                    if static == 0:
                        q.wait_ge(S[prev + "_prod"], NT)
                    elif static != 1:
                        q.wait_ge(S[st + "_prod"], it - 1)
                    passed(q)
                    q.dma_start(mT[:, par, :].bitcast(U8), stM[bass.ds(it, 1)].rearrange("o p n -> (o p) n")).then_inc(S[f"{st}_ldM{par}"], 16)
                tiles(q, step, at=between(SYNC_D, lambda k: mamba_sync(q, 0, k)) if st == "d" else {})

            mamba_sync(q, 0)
            q.wait_ge(S["m_out"], CR["m_out"] + 16 * NCH)
            q.wait_ge(S["s_f2d"], 16)
            if_general(q, general_sync)

        @block.tensor
        def _(p):
            p.wait_ge(S["s_id"], 4)
            p.wait_ge(S["s_x"], 32)
            for t in range(NT):
                g = t // 4
                if t % 4 == 0 and g >= 2:
                    p.wait_ge(S["s_xT"], g - 1)
                ins = p.transpose(PS[:, g % 2, (t % 4) * P:(t % 4 + 1) * P], xs[:, t, :], idf[:])
                if t % 4 == 3:
                    ins.then_inc(S["s_tr0"], 1)
            p.wait_ge(S["s_xT"], NT // 4)
            p.wait_ge(S["s_col"], 1)
            for b in range(8):
                ins = p.matmul(PS[:, b, :], a2rep[:], xT[:, b * BANK:(b + 1) * BANK], start=True, stop=True)
                ins.then_inc(S["s_f"], 1)
            p.wait_ge(S["s_fc"], 8)
            for t in range(NT):
                ins = p.matmul(PS[:, 0, 2 * t:2 * t + 2], xT[:, t * P:(t + 1) * P], acol[:], start=True, stop=True)
            ins.then_inc(S["s_f"], 1)
            p.wait_ge(S["p_w"], 1)
            p.matmul(PS[:, 1, 0:2 * D], ones[:], tb[:, 0:2 * D], start=True, stop=True).then_inc(S["s_f"], 1)

            def step(it, par, static):
                new, old = static is None or static < NT, static is None or static >= 1
                op = 1 - par
                if new:
                    p.wait_ge(S[f"adj{par}"], 16 * (it // 2 + 1) if static is not None else 16 * (it - par) // 2 + 16)
                for g in range(8):
                    if new:
                        if static != 0 or g >= 2:
                            p.wait_ge(S["a_adjE"], 8 * it + g - 1)
                        for k in range(4):
                            j = 4 * g + k
                            ins = p.transpose(PS[:, 4 + g % 2, k * P:(k + 1) * P], adjt[:, par, j * P:(j + 1) * P], idf[:])
                        ins.then_inc(S["a_adjT"], 1)
                    if old:
                        if static == 1:
                            p.wait_ge(S["s_y0"], 4 * g + 4)
                        if g == 0:
                            p.wait_ge(S["a_s1E"], 4 * it)
                            if static is None or static >= 3:
                                p.wait_ge(S["a_tail"], it - 2)
                            passed(p)
                        for j in range(4 * g, 4 * g + 4):
                            p.matmul(PS[:, 2 * op, 0:2 * COLS], s1T[:, op, j * P:(j + 1) * P], y1[:, j, :], start=(j == 0), stop=(j == NT - 1))
                if new:
                    p.wait_ge(S["a_s1"], it + 1)
                for g in range(4):
                    if new:
                        if static != 0 or g >= 2:
                            p.wait_ge(S["a_s1E"], 4 * it + g - 1)
                        bank = PS[:, 6 + g % 2, :].bitcast(BF16)
                        for k in range(8):
                            j = 8 * g + k
                            ins = p.transpose(bank[:, k * P:(k + 1) * P], s1r[:, par, j * P:(j + 1) * P], idb[:])
                        ins.then_inc(S["a_s1Tp"], 1)
                    if old:
                        if g == 0:
                            p.wait_ge(S["a_s2"], it)
                            passed(p)
                        for j in range(8 * g, 8 * g + 8):
                            ins = p.matmul(PS[:, 2 * op + 1, 0:2 * COLS], s2T[:, op, j * P:(j + 1) * P], y2[:, j, :], start=(j == 0), stop=(j == NT - 1))
                if old:
                    ins.then_inc(S["a_prod"], 1)
            tiles(p, step, lag=1)

            def step(it, par, static):
                if static == 0:
                    p.wait_ge(S["a_spl"], NT)
                    p.wait_ge(S["a_low"], NT)
                if static is None or static >= 2:
                    turn("b", it - 2, par)
                if static is None or static < NT:
                    p.wait_ge(S[f"b_ldS{par}"], (it - par) * 8 + 16)
                    if static is None or static >= 2:
                        p.wait_ge(S["b_tail"], it - 1)
                    passed(p)
                    for j in range(NT):
                        p.matmul(PS[:, 2 * par, 0:2 * D], s1T[:, par, j * P:(j + 1) * P], y1b[:, j, :], start=(j == 0), stop=(j == NT - 1))
                    p.wait_ge(S["b_s2"], it + 1)
                    p.wait_ge(S["b_s2g"], it + 1)
                    passed(p)
                    for j in range(NT):
                        ins = p.matmul(PS[:, 2 * par + 1, 0:2 * D], s2T[:, par, j * P:(j + 1) * P], y2b[:, j, :], start=(j == 0), stop=(j == NT - 1))
                    ins.then_inc(S["b_prod"], 1)
                if static is None or static >= 2:
                    project("b", W1, it - 2, par)
            def turn(st, t, par):
                p.wait_ge(S[st + "_x1" if st == "b" else st + "_x"], t + 1)
                if st == "d" and t is not None:
                    p.wait_ge(S["d_xTe"], t)
                bank = 2 if st == "d" else 4
                p.transpose(PS[:, bank, 0:P], xn[:, par, :], idf[:]).then_inc(S[st + "_xTp"], 1)
            def project(st, W, t, par):
                if W is not None:
                    p.wait_ge(S[st + "_xTe"], t + 1)
                    p.wait_ge(S[st + "_low"], t)
                    p.matmul(PS[:, 5, 0:D], xTt[:, par, :], W[:], start=True, stop=True).then_inc(S[st + "_y"], 1)
            tiles(p, step, lag=2)

            for st, W, y, prev in (("c", Wg, y1, "b"), ("d", None, y2, "c")):
                def step(it, par, static):
                    if static == 0:
                        p.wait_ge(S[prev + "_hi"], NT)
                        p.wait_ge(S[prev + "_low"], NT)
                    if static is None or static >= 2:
                        turn(st, it - 2, par)
                    if static is None or static < NT:
                        p.wait_ge(S[f"{st}_ldM{par}"], (it - par) * 8 + 16)
                        if static is None or static >= 2:
                            p.wait_ge(S[st + "_x"], it - 1)
                        passed(p)
                        for j in range(NT):
                            ins = p.matmul(PS[:, par, 0:2 * D], mT[:, par, j * P:(j + 1) * P], y[:, j, 0:2 * D], start=(j == 0), stop=(j == NT - 1))
                        ins.then_inc(S[st + "_prod"], 1)
                    if static is None or static >= 2:
                        project(st, W, it - 2, par)
                tiles(p, step, lag=2, at=between(PE_D, lambda k: mamba_pe(p, 0, k)) if st == "d" else {})
            p.wait_ge(S["d_xTe"], NT)
            mamba_pe(p, 0)
            if_general(p, general_pe)

        @block.gpsimd
        def _(g):
            g.memset(idf[:], 0.0).then_inc(S["s_id"], 1)
            g.memset(idb[:], 0.0).then_inc(S["s_id"], 1)
            g.wait_ge(S["s_id"], 2)
            for m in (idf, idb):
                g.affine_select(out=m[:], in_=m[:], compare_op=ALU.not_equal, fill=1.0, base=0, pattern=[[-1, P]], channel_multiplier=1).then_inc(S["s_id"], 1)
            g.wait_ge(S["s_red"], 1)
            g.partition_all_reduce(stat[:], red[:], P, RMAX).then_inc(S["s_red"], 1)
            def step(it, par, static):
                g.wait_ge(S["a_s1E"], 4 * it + 4)
                if static is None or static >= 2:
                    g.wait_ge(S["a_prod"], it - 1)
                passed(g)
                g.tensor_tensor(s2T[:, par, :], mT[:, par, :], s1T[:, par, :], ALU.subtract, saturate=False).then_inc(S["a_s2"], 1)
            tiles(g, step)
            g.wait_ge(S["s_red"], 3)
            g.partition_all_reduce(stat[:], red[:], P, RMAX).then_inc(S["s_red"], 1)
            def masks(it, par, static):
                g.wait_ge(S[f"b_ldS{par}"], (it - par) * 8 + 16)
                g.wait_ge(S[f"b_ldM{par}"], (it - par) * 8 + 16)
                if static is None or static >= 2:
                    g.wait_ge(S["b_prod"], it - 1)
                passed(g)
                g.tensor_tensor(s2T[:, par, N // 2:N], mT[:, par, N // 2:N], s1T[:, par, N // 2:N], ALU.subtract, saturate=False).then_inc(S["b_s2g"], 1)
            def step(it, par, static):
                if static is None or static < NT:
                    masks(it, par, static)
                if static is None or static >= 2:
                    g.wait_ge(S["b_x1"], it - 1)
                    passed(g)
                    g.tensor_tensor(xs[:, bass.ds(it - 2, 1), :].rearrange("p o d -> p (o d)"), xn[:, par, :], b1row[:], ALU.add).then_inc(S["b_cp"], 1)
            tiles(g, step, lag=2)
            def step(it, par, static):
                g.wait_ge(S["c_x"], it + 1)
                g.tensor_copy(xs[:, bass.ds(it, 1), :].rearrange("p o d -> p (o d)"), xn[:, par, :]).then_inc(S["c_cp"], 1)
            tiles(g, step)
            mamba_gpsimd(g, 0)
            if_general(g, general_gpsimd)

        @block.scalar
        def _(s):
            ch = Chain(s, S["a_chain"])
            for g in range(8):
                s.wait_ge(S["s_tr0"], g + 1)
                s.activation(xT[:, g * BANK:(g + 1) * BANK], PS[:, g % 2, :], ACT.Copy).then_inc(S["s_xT"], 1)
            for b in range(8):
                s.wait_ge(S["s_f"], b + 1)
                s.activation(f2row[:, b * BANK:(b + 1) * BANK], PS[:, b, :], ACT.Copy).then_inc(S["s_fc"], 1)
            s.wait_ge(S["s_w"], 16 * 16)
            ch.begin()
            ch(s.activation(coe[:], coe[:], ACT.Sigmoid))
            ch(s.activation(Aneg[:], Aneg[:], ACT.Exp))
            ch(s.activation(Aneg[:], Aneg[:], ACT.Copy, scale=-1.0))
            s.wait_ge(S["s_ex"], 1)
            s.activation(EE[:, 0, :], f12[:, :, 1], ACT.Exp, bias=sc[:, 0:1])
            s.activation(EE[:, 1, :], f12[:, :, 1], ACT.Exp, bias=sc[:, 1:2], scale=ALPHA)
            s.activation(Ea[:], Ea2[:], ACT.Exp)
            s.activation(Eb[:], Eb2[:], ACT.Exp)
            ch(s.activation(sc[:, 8:10], sc[:, 6:8], ACT.Sqrt))
            s.sem_inc(S["s_exd"], 1)
            ch.end(); ch.close()

            def high():
                s.wait_ge(S["s_y0a"], 1)
                for t in range(NT):
                    s.activation(y1[:, t, 0:D], xs[:, t, :], ACT.Copy, scale=Es[:, 0, t:t + 1])
                    s.activation(y2[:, t, 0:D], xs[:, t, :], ACT.Copy, scale=Es[:, 1, t:t + 1]).then_inc(S["s_init"], 1)

            def step(it, par, static):
                t = it - 2
                if static == 1:
                    high()
                if static is None or static >= 2:
                    s.wait_ge(S["a_prod"], it - 1)
                    if static is None or static >= 4:
                        s.wait_ge(S["a_tail"], it - 3)
                    s.activation(ta[:, par, :], PS[:, 2 * par, 0:2 * COLS], ACT.Copy, scale=Ea[:, bass.ds(t, 1)]).then_inc(S["a_ta"], 1)
                if static is None or static < NT:
                    for g in range(8):
                        s.wait_ge(S["a_adjT"], 8 * it + g + 1)
                        if g == 0 and (static is None or static >= 2):
                            s.wait_ge(S[f"a_stM{par}"], (it - par) * 8)
                            s.wait_ge(S["a_s2"], it - 1)
                        passed(s)
                        s.activation(mT[:, par, g * BANK:(g + 1) * BANK], PS[:, 4 + g % 2, :], ACT.Copy, saturate=False).then_inc(S["a_adjE"], 1)
                if static is None or static < NT:
                    for g in range(4):
                        s.wait_ge(S["a_s1Tp"], 4 * it + g + 1)
                        if g == 0 and (static is None or static >= 2):
                            s.wait_ge(S[f"a_stS{par}"], (it - par) * 8)
                            s.wait_ge(S["a_prod"], it - 1)
                        passed(s)
                        s.activation(s1T[:, par, g * 1024:(g + 1) * 1024], PS[:, 6 + g % 2, :].bitcast(BF16), ACT.Copy, saturate=False).then_inc(S["a_s1E"], 1)
                if par == 1 and (static is None or static >= 3):
                    s.wait_ge(S["a_feat"], it - 1)
                    for k in (3, 2):
                        f = feat[:, bass.ds(it - k, 1), :].rearrange("p o d -> p (o d)")
                        s.activation(y1b[:, bass.ds(it - k, 1), 0:D].rearrange("p o d -> p (o d)"), f, ACT.Copy, scale=Es2[:, 0, bass.ds(it - k, 1)])
                        s.activation(y2b[:, bass.ds(it - k, 1), 0:D].rearrange("p o d -> p (o d)"), f, ACT.Copy, scale=Es2[:, 1, bass.ds(it - k, 1)]).then_inc(S["a_spl"], 1)
            tiles(s, step, lag=2)

            s.wait_ge(S["s_ex"], 2)
            s.activation(dsc[:], dinv[:], ACT.Sqrt).then_inc(S["s_exd"], 1)

            def rstd_step(st, t, par):
                s.wait_ge(S[st + "_var"], t + 1)
                s.activation(rstd[:, par:par + 1], mv[:, 1:2], ACT.Sqrt, bias=sc[:, 12:13]).then_inc(S[st + "_std"], 1)

            def evac_xT(st, t, par):
                s.wait_ge(S[st + "_xTp"], t + 1)
                s.activation(xTt[:, par, :], PS[:, 4, 0:P], ACT.Copy).then_inc(S[st + "_xTe"], 1)

            def step(it, par, static):
                t = it - 2
                if static is None or static >= 2:
                    evac_xT("b", t, par)
                if static is None or static < NT:
                    s.wait_ge(S["b_prod"], it + 1)
                    if static is None or static >= 2:
                        s.wait_ge(S["b_tail"], it - 1)
                    s.activation(ta[:, par, 0:2 * D], PS[:, 2 * par, 0:2 * D], ACT.Copy, scale=g1[:, bass.ds(it, 1)]).then_inc(S["b_ta"], 1)
                if static is None or static >= 2:
                    s.wait_ge(S["b_y"], t + 1)
                    s.activation(y1[:, bass.ds(t, 1), 0:D].rearrange("p o d -> p (o d)"), PS[:, 5, 0:D], ACT.Copy, scale=dsc[:, bass.ds(t, 1)]).then_inc(S["b_hi"], 1)
                if static is None or static < NT:
                    rstd_step("b", it, par)
            tiles(s, step, lag=2)

            def step(it, par, static):
                t = it - 2
                if static is None or static >= 2:
                    evac_xT("c", t, par)
                if static is None or static < NT:
                    s.wait_ge(S["c_prod"], it + 1)
                    if static is None or static >= 2:
                        s.wait_ge(S["c_x"], it - 1)
                    s.activation(ta[:, par, 0:D], PS[:, par, D:2 * D], ACT.Copy).then_inc(S["c_ta"], 1)
                if static is None or static >= 2:
                    s.wait_ge(S["c_y"], t + 1)
                    s.activation(y2[:, bass.ds(t, 1), 0:D].rearrange("p o d -> p (o d)"), PS[:, 5, 0:D], ACT.Copy, scale=sc[:, 11:12]).then_inc(S["c_hi"], 1)
                if static is None or static < NT:
                    rstd_step("c", it, par)
            tiles(s, step, lag=2)

            def step(it, par, static):
                if static is None or static >= 2:
                    t = it - 2
                    s.wait_ge(S["d_xTp"], t + 1)
                    s.activation(h2T[:, bass.ds(t * P + 3, P)], PS[:, 2, 0:P], ACT.Identity, scale=lng[:, 0:1], bias=lnb[:, 0:1]).then_inc(S["d_xTe"], 1)
                if static is None or static < NT:
                    s.wait_ge(S["d_prod"], it + 1)
                    if static is None or static >= 2:
                        s.wait_ge(S["d_x"], it - 1)
                    s.activation(ta[:, par, 0:D], PS[:, par, D:2 * D], ACT.Copy, scale=sc[:, 13:14]).then_inc(S["d_ta"], 1)
                    rstd_step("d", it, par)
            tiles(s, step, lag=2, at=between(ACT_D, lambda k: mamba_scalar(s, ch, 0, k)))
            mamba_scalar(s, ch, 0)
            if_general(s, lambda q: general_scalar(q, ch))

        @block.vector
        def _(v):
            ch = Chain(v, S["v_chain"])
            ch.begin()
            ch(v.memset(ones[:], 1.0))
            v.wait_ge(S["s_x"], 32)
            v.tensor_scalar(a2rep[:], ones[:], acol[:, 1:2], None, ALU.mult).then_inc(S["s_col"], 1)
            ch(v.tensor_reduce(red[:, 2:3], xs[:, :, :].rearrange("p t d -> p (t d)"), AX_X, ALU.max))
            ch(v.tensor_reduce(red[:, 3:4], xs[:, :, :].rearrange("p t d -> p (t d)"), AX_X, ALU.min))
            ch(v.tensor_scalar(red[:, 3:4], red[:, 3:4], -1.0, None, ALU.mult))
            ch(v.tensor_tensor(red[:, 2:3], red[:, 2:3], red[:, 3:4], ALU.max))
            v.wait_ge(S["s_w"], 16 * 16)
            ch(v.tensor_tensor(wtap[:, :, :], cwrow.rearrange("p (e k) -> p k e", k=KC),
                               win[:, 0:DI].unsqueeze(1).broadcast_to([P, KC, DI]), ALU.mult))
            ch(v.tensor_tensor(tb[:, 0:D], W1[:], W1[:], ALU.mult))
            v.tensor_tensor(tb[:, D:2 * D], Wg[:], Wg[:], ALU.mult).then_inc(S["p_w"], 1)
            v.wait_ge(S["s_f"], 9)
            ch(v.tensor_copy(f12[:, :, :].rearrange("p t k -> p (t k)"), PS[:, 0, 0:2 * NT]))
            v.wait_ge(S["s_f"], 10)
            ch(v.tensor_reduce(sc[:, 6:8], PS[:, 1, 0:2 * D].rearrange("p (k d) -> p k d", k=2), AX_X, ALU.max))
            ch(v.tensor_scalar(nf1[:], f12[:, :, 0], -1.0, None, ALU.mult))
            ch(v.tensor_reduce(red[:, 0:1], f12[:, :, 1], AX_X, ALU.max))
            ch(v.tensor_reduce(red[:, 1:2], f12[:, :, 1], AX_X, ALU.min))
            v.tensor_scalar(red[:, 1:2], red[:, 1:2], -1.0, None, ALU.mult).then_inc(S["s_red"], 1)
            v.wait_ge(S["s_red"], 2)
            ch(v.tensor_scalar(sc[:, 0:1], stat[:, 0:1], -1.0, None, ALU.mult))
            ch(v.tensor_scalar(sc[:, 1:2], stat[:, 0:1], -ALPHA, None, ALU.mult))
            ch(v.tensor_tensor(sc[:, 14:15], stat[:, 0:1], stat[:, 1:2], ALU.add))
            ch(v.tensor_scalar(sc[:, 2:3], stat[:, 2:3], 1e-30, 1.0 / HALFMAX, ALU.max, ALU.mult))
            ch(v.reciprocal(sc[:, 3:4], sc[:, 2:3]))
            ch(v.tensor_scalar(sc[:, 4:5], sc[:, 2:3], SUMSCALE, None, ALU.mult))
            ch(v.tensor_scalar(sc[:, 5:6], sc[:, 2:3], SUMSCALE * 2.0, None, ALU.mult))
            ch(v.tensor_scalar(Ea[:], f12[:, :, 0], stat[:, 0:1], None, ALU.add))
            ch(v.tensor_scalar(Ea2[:], Ea[:], 1.0 - ALPHA, 0.0, ALU.mult, ALU.min))
            ch(v.tensor_scalar(Eb2[:], Ea[:], ALPHA - 1.0, 0.0, ALU.mult, ALU.min))
            v.memset(sc[:, 12:13], EPS).then_inc(S["s_ex"], 1)
            v.wait_ge(S["s_exd"], 1)
            ch(v.tensor_scalar(Es[:], EE[:], sc[:, 3:4], None, ALU.mult))
            v.tensor_scalar(Es2[:], EE[:], sc[:, 3:4], 0.5, ALU.mult, ALU.mult).then_inc(S["s_y0a"], 1)
            ch(v.tensor_tensor(Ea2[:], Ea[:], Ea[:], ALU.mult))
            ch(v.tensor_tensor(Eb2[:], Eb[:], Eb[:], ALU.mult))
            ch(v.tensor_tensor(EE2[:], EE[:], EE[:], ALU.mult))
            ch(v.tensor_scalar(sc[:, 8:10], sc[:, 8:10], 1e-30, ROWNORM / HALFMAX, ALU.max, ALU.mult))
            ch(v.reciprocal(sc[:, 10:12], sc[:, 8:10]))
            ch(v.tensor_copy(sc[:, 13:14], sc[:, 9:10]))
            ch(v.tensor_scalar(sc[:, 20:25], coe[:, 0:5], -1.0, 1.0, ALU.mult, ALU.add))
            ch(v.tensor_tensor(sc[:, 25:26], sc[:, 21:22], coe[:, 0:1], ALU.mult))
            ch(v.tensor_tensor(sc[:, 26:27], sc[:, 21:22], sc[:, 20:21], ALU.mult))
            ch(v.tensor_scalar(sc[:, 27:28], coe[:, 3:4], -1.0, None, ALU.mult))
            for y, k in ((y1, 0), (y2, 1)):
                for c, E in ((D, EE), (D + 1, EE2)):
                    ch(v.tensor_scalar(y[:, :, c], E[:, k, :], SUMSCALE, None, ALU.mult))
                    ch(v.scalar_tensor_tensor(out=y[:, :, COLS + c], in0=E[:, k, :], scalar=SUMSCALE, in1=y[:, :, c], op0=ALU.mult, op1=ALU.subtract))
                ch(v.memset(y[:, :, D + 2], 1.0))
                ch(v.memset(y[:, :, COLS + D + 2], 0.0))
            ch.end(); ch.close()

            def firstlow():
                for t in range(NT):
                    v.wait_ge(S["s_init"], t + 1)
                    v.scalar_tensor_tensor(out=y1[:, t, COLS:COLS + D], in0=xs[:, t, :], scalar=Es[:, 0, t:t + 1], in1=y1[:, t, 0:D], op0=ALU.mult, op1=ALU.subtract)
                    ins = v.scalar_tensor_tensor(out=y2[:, t, COLS:COLS + D], in0=xs[:, t, :], scalar=Es[:, 1, t:t + 1], in1=y2[:, t, 0:D], op0=ALU.mult, op1=ALU.subtract)
                    ins.then_inc(S["s_y0"], 1)

            ct = Chain(v, S["g_chain"])
            tt = Chain(v, S["t_chain"])
            def row(ap, t):
                return ap[:, bass.ds(t, 1), :].rearrange("p o d -> p (o d)")
            def step(it, par, static):
                if static == 1:
                    firstlow()
                if static is None or static < NT:
                    ch.begin(it)
                    v.wait_ge(S[f"adj{par}"], (it - par) * 8 + 16)
                    if static is None or static >= 2:
                        v.wait_ge(S["a_s1Tp"], 4 * (it - 1))
                    ch(v.scalar_tensor_tensor(out=s1r[:, par, :], in0=adjt[:, par, :], scalar=0.0, in1=adjt[:, par, :],
                                              op0=ALU.is_gt, op1=ALU.not_equal, accum_out=cnt[:, bass.ds(it, 1)]))
                    v.scalar_tensor_tensor(out=s1r[:, par, :], in0=f2row[:, 0:N], scalar=nf1[:, bass.ds(it, 1)], in1=adjt[:, par, :],
                                           op0=ALU.is_gt, op1=ALU.mult).then_inc(S["a_s1"], 1)
                    ch.end()
                if par == 0 and (static is None or static >= 4):
                    v.wait_ge(S["a_feat"], it - 2)
                    for k in (4, 3):
                        low(it - k)
                if static is None or 2 <= static < NT + 2:
                    sums(it, par, static, it - 2)
                if par == 1 and (static is None or 3 <= static < NT + 2):
                    pair(it - 3)
            def sums(it, par, static, t):
                one = lambda ap: ap[:, bass.ds(t, 1)]
                tt.begin(t, 4)
                Bq = PS[:, 2 * par + 1, 0:2 * COLS]
                sq = slice(D + 1, D + 2 + COLS, COLS)
                v.wait_ge(S["a_ta"], it - 1)
                if par == 0 and (static is None or static >= 4):
                    v.wait_ge(S["a_feat"], t)
                taq = ta[:, par, :]
                squares = tt.mark(v.tensor_scalar(tp[:, par, 0:2], taq[:, sq], one(Ea), None, ALU.mult))
                count = tt.mark(v.tensor_copy(tp[:, par, 4:5], Bq[:, D + 2:D + 3]))
                v.scalar_tensor_tensor(out=tb2[:, par, :], in0=Bq, scalar=one(Eb), in1=taq, op0=ALU.mult, op1=ALU.add)
                tt.need(squares)
                tt.mark(v.scalar_tensor_tensor(out=tp[:, par, 2:4], in0=Bq[:, sq], scalar=one(Eb2), in1=tp[:, par, 0:2], op0=ALU.mult, op1=ALU.add))
                tt.need(count)
                tt(v.tensor_tensor(one(deg), PS[:, 2 * par, D + 2:D + 3], tp[:, par, 4:5], ALU.add))
                v.sem_inc(S["a_tail"], 1)
                tt.end()
            def pair(t):
                two = lambda ap: ap[:, bass.ds(t, 2)]
                wide = lambda ap: ap.unsqueeze(2).broadcast_to([P, 2, D])
                ct.begin(t, 5)
                lo, hi = tb2[:, :, 0:D], tb2[:, :, COLS:COLS + D]
                s4 = tp[:, :, 5]
                ct.mark(v.tensor_tensor(s4, tp[:, :, 2], tp[:, :, 3], ALU.add))
                ct(v.tensor_tensor(tb2[:, :, 0:D + 1], tb2[:, :, 0:D + 1], tb2[:, :, COLS:COLS + D + 1], ALU.add))
                ct(v.reciprocal(two(rden), tb2[:, :, D]))
                ct(v.tensor_tensor(s4, s4, two(rden), ALU.mult))
                scaled = ct.mark(v.tensor_scalar(tp[:, :, 6], two(rden), sc[:, 4:5], None, ALU.mult))
                rs = ct.mark(v.scalar_tensor_tensor(out=two(rsum), in0=s4, scalar=0.5 * SUMSCALE, in1=two(rden), op0=ALU.mult, op1=ALU.mult))
                ct.need(scaled)
                v.tensor_tensor(lo, lo, wide(tp[:, :, 6]), ALU.mult)
                ct.need(rs)
                ct(v.tensor_scalar(tp[:, :, 7], two(rsum), -1.0, sc[:, 22:23], ALU.mult, ALU.add))
                ct(v.tensor_tensor(hi, xs[:, bass.ds(t, 2), :], wide(tp[:, :, 7]), ALU.mult))
                ct(v.tensor_tensor(lo, lo, hi, ALU.add))
                ct(v.tensor_scalar(hi, lo, -THRESH, THRESH, ALU.max, ALU.min))
                v.tensor_tensor(feat[:, bass.ds(t, 2), :], lo, hi, ALU.subtract).then_inc(S["a_feat"], 2)
                ct.end(2)
            def low(t):
                v.wait_ge(S["a_spl"], t + 1)
                for k, y in ((0, y1b), (1, y2b)):
                    ins = v.scalar_tensor_tensor(out=y[:, bass.ds(t, 1), D:2 * D].rearrange("p o d -> p (o d)"), in0=row(feat, t), scalar=Es2[:, k, bass.ds(t, 1)],
                                                 in1=y[:, bass.ds(t, 1), 0:D].rearrange("p o d -> p (o d)"), op0=ALU.mult, op1=ALU.subtract)
                ins.then_inc(S["a_low"], 1)
            tiles(v, step, lag=3)
            ch.close(NT); ct.close(NT)

            ct.begin()
            ct(v.tensor_reduce(red[:, 0:1], cnt[:], AX_X, ALU.add))
            ct(v.tensor_reduce(red[:, 1:2], deg[:], AX_X, ALU.min))
            ct(v.tensor_scalar(red[:, 1:2], red[:, 1:2], 0.5, None, ALU.is_lt))
            ct(v.tensor_scalar(red[:, 2:3], sc[:, 14:15], SPREAD, None, ALU.is_gt))
            v.tensor_tensor(red[:, 3:4], red[:, 1:2], red[:, 2:3], ALU.max).then_inc(S["s_red"], 1)
            v.wait_ge(S["s_red"], 4)
            ct(v.tensor_tensor(stat[:, 0:1], stat[:, 0:1], stat[:, 3:4], ALU.max))
            v.tensor_scalar(flag[:], stat[:, 0:1], 0.5, None, ALU.is_gt).then_inc(S["s_flag"], 1)
            ct(v.tensor_scalar(g1[:], rden[:], sc[:, 5:6], None, ALU.mult))
            ct(v.tensor_tensor(g2[:], g1[:], Eb[:], ALU.mult))
            ct(v.tensor_tensor(g1[:], g1[:], Ea[:], ALU.mult))
            ct(v.tensor_scalar(k2[:], rsum[:], coe[:, 1:2], sc[:, 25:26], ALU.mult, ALU.add))
            ct(v.tensor_scalar(dinv[:], deg[:], 1.0, None, ALU.add))
            v.sem_inc(S["s_ex"], 1)
            v.wait_ge(S["s_exd"], 2)
            ct(v.reciprocal(dinv[:], dsc[:]))
            ct(v.tensor_scalar(dsc[:], dinv[:], sc[:, 10:11], None, ALU.mult))
            ct(v.tensor_scalar(deg[:], dinv[:], sc[:, 8:9], None, ALU.mult))
            v.sem_inc(S["s_ex"], 1)
            ct.end(); ct.close()

            def norm(st, z, dst, par, inc):
                ct(v.bn_stats(bn6[:], z))
                passed(v)
                v.bn_aggr(mv[:], bn6[:]).then_inc(S[st + "_var"], 1)
                v.wait_ge(S[st + "_std"], inc)
                ct(v.reciprocal(rstd[:, par:par + 1], rstd[:, par:par + 1]))
                return v.tensor_scalar(dst, z, mv[:, 0:1], rstd[:, par:par + 1], ALU.subtract, ALU.mult)

            def stepB(it, par, static):
                if static is None or static < NT:
                    masks(it, par, static)
                if static is None or 1 <= static <= NT:
                    tailB(it - 1, 1 - par, static is None or static >= 3)
                if static is None or static >= 3:
                    lowpart("b", y1, feat, dsc, it - 3)
            def tailB(t, par, ringed):
                one = lambda ap: ap[:, bass.ds(t, 1)]
                ct.begin(t)
                v.wait_ge(S["b_ta"], t + 1)
                ct(v.scalar_tensor_tensor(out=tb[:, 0:2 * D], in0=PS[:, 2 * par + 1, 0:2 * D], scalar=one(g2), in1=ta[:, par, 0:2 * D], op0=ALU.mult, op1=ALU.add))
                v.sem_inc(S["b_tail"], 1)
                ct(v.tensor_tensor(tb[:, 0:D], tb[:, 0:D], tb[:, D:2 * D], ALU.add))
                ct(v.scalar_tensor_tensor(out=tb[:, D:2 * D], in0=tb[:, 0:D], scalar=sc[:, 27:28], in1=row(feat, t), op0=ALU.mult, op1=ALU.add))
                ct(v.scalar_tensor_tensor(out=tb[:, 0:D], in0=tb[:, 0:D], scalar=coe[:, 1:2], in1=row(xs, t), op0=ALU.mult, op1=ALU.add))
                ct(v.scalar_tensor_tensor(out=tb[:, 0:D], in0=tb[:, D:2 * D], scalar=one(k2), in1=tb[:, 0:D], op0=ALU.mult, op1=ALU.add))
                v.wait_ge(S[f"b_h{par}"], (t - par) * 8 + 16)
                ct(v.scalar_tensor_tensor(out=tb[:, 0:D], in0=h0t[:, par, :], scalar=sc[:, 26:27], in1=tb[:, 0:D], op0=ALU.mult, op1=ALU.add))
                if ringed:
                    v.wait_ge(S["b_xTp"], t - 1)
                    v.wait_ge(S["b_cp"], t - 1)
                norm("b", tb[:, 0:D], xn[:, par, :], par, t + 1).then_inc(S["b_x1"], 1)
                v.wait_ge(S["b_x1"], t + 1)
                ct.end()
            def masks(it, par, static):
                v.wait_ge(S[f"b_ldS{par}"], (it - par) * 8 + 16)
                v.wait_ge(S[f"b_ldM{par}"], (it - par) * 8 + 16)
                if static is None or static >= 2:
                    v.wait_ge(S["b_prod"], it - 1)
                passed(v)
                v.tensor_tensor(s2T[:, par, 0:N // 2], mT[:, par, 0:N // 2], s1T[:, par, 0:N // 2], ALU.subtract, saturate=False).then_inc(S["b_s2"], 1)

            def lowpart(st, y, keep, scale, t):
                v.wait_ge(S[st + "_hi"], t + 1)
                sca = scale[:, bass.ds(t, 1)] if keep is not None else scale
                hi = y[:, bass.ds(t, 1), 0:D].rearrange("p o d -> p (o d)")
                low = y[:, bass.ds(t, 1), D:2 * D].rearrange("p o d -> p (o d)")
                if keep is not None:
                    v.tensor_scalar(row(keep, t), PS[:, 5, 0:D], sca, None, ALU.mult)
                v.scalar_tensor_tensor(out=low, in0=PS[:, 5, 0:D], scalar=sca, in1=hi, op0=ALU.mult, op1=ALU.subtract).then_inc(S[st + "_low"], 1)
            tiles(v, stepB, lag=3)
            ct.close(NT)

            def stepC(it, par, static):
                if static is None or static < NT:
                    ct.begin(it)
                    if static == 0:
                        v.wait_ge(S["b_cp"], NT)
                    v.wait_ge(S["c_ta"], it + 1)
                    ct(v.tensor_tensor(tb[:, 0:D], ta[:, par, 0:D], row(feat, it), ALU.add))
                    ct(v.tensor_tensor(tb[:, 0:D], PS[:, par, 0:D], tb[:, 0:D], ALU.add))
                    ct(v.scalar_tensor_tensor(out=tb[:, 0:D], in0=tb[:, 0:D], scalar=deg[:, bass.ds(it, 1)], in1=row(xs, it), op0=ALU.mult, op1=ALU.add))
                    if static is None or static >= 2:
                        v.wait_ge(S["c_xTp"], it - 1)
                        v.wait_ge(S["c_cp"], it - 1)
                    norm("c", tb[:, 0:D], xn[:, par, :], par, it + 1).then_inc(S["c_x"], 1)
                    v.wait_ge(S["c_x"], it + 1)
                    ct.end()
                if static is None or static >= 2:
                    lowpart("c", y2, None, sc[:, 11:12], it - 2)
            tiles(v, stepC, lag=2)
            ct.close(NT)

            def stepD(it, par, static):
                ct.begin(it)
                v.wait_ge(S["d_ta"], it + 1)
                ct(v.scalar_tensor_tensor(out=tb[:, 0:D], in0=PS[:, par, 0:D], scalar=sc[:, 13:14], in1=ta[:, par, 0:D], op0=ALU.mult, op1=ALU.add))
                ct(v.tensor_tensor(tb[:, 0:D], tb[:, 0:D], bgrow[:], ALU.add))
                ct(v.tensor_scalar(tb[:, 0:D], tb[:, 0:D], 0.0, None, ALU.max))
                if static is None or static >= 2:
                    v.wait_ge(S["d_xTp"], it - 1)
                norm("d", tb[:, 0:D], xn[:, par, :], par, it + 1).then_inc(S["d_x"], 1)
                v.wait_ge(S["d_x"], it + 1)
                ct.end()
            v.wait_ge(S["c_cp"], NT)
            v.memset(h2T[:, 0:3], 0.0).then_inc(S["m_s0"], 1)
            v.memset(state[:], 0.0).then_inc(S["m_s0"], 1)
            skips(v)
            for name, credit in CR.items():
                v.sem_inc(S[name], credit)
            tiles(v, stepD, at=between(DVE_D, lambda k: mamba_vector(v, ct, 0, k)))
            ct.close(NT)
            mamba_vector(v, ct, 0)
            if_general(v, lambda q: general_vector(q, ct, norm))

    return nc


_INS = ['x', 'adj', 'L0_gnn_h0', 'L0_gnn_a', 'L0_gnn_temp', 'L1_gnn_weight', 'L1_gnn_bias', 'L2_gnn_gcn_w', 'L2_gnn_gcn_b', 'L2_gnn_ln_g', 'L2_gnn_ln_b', 'L2_gnn_w_in', 'L2_gnn_conv_w', 'L2_gnn_conv_b', 'L2_gnn_w_xp', 'L2_gnn_w_dt', 'L2_gnn_b_dt', 'L2_gnn_A_log', 'L2_gnn_D_skip', 'L2_gnn_w_out', 'L3_gnn_W', 'L3_gnn_B']
_OUTS = [((4096, 128), 'float32')]


def kernel(**inputs):
    import numpy as _np
    import concourse.bacc as _bacc
    from concourse import mybir as _mybir
    from concourse.bass_utils import run_bass_kernel_spmd as _run

    nc = _bacc.Bacc("TRN2", target_bir_lowering=False, num_devices=1)
    arrays, args = {}, {}
    for name in _INS:
        a = _np.ascontiguousarray(inputs[name])
        arrays[f"in_{name}_dram"] = a
        args[name] = nc.dram_tensor(f"in_{name}_dram", a.shape, _mybir.dt.from_np(a.dtype), kind="ExternalInput").ap()
    shape, dtype = _OUTS[0]
    out = nc.dram_tensor("out_0_dram", shape, _mybir.dt.from_np(_np.dtype(dtype)), kind="ExternalOutput").ap()
    build(nc, args, out)
    r = _run(nc, [arrays], core_ids=[0])
    return r.results[0]["out_0_dram"]
```
